# Optimizing a Trainium2 kernel written in Bass

```python
import numpy as np
import jax
import jax.numpy as jnp

def _softmax(x, axis=-1):
    return jax.nn.softmax(x, axis=axis)

def _gelu(x):
    return jax.nn.gelu(x, approximate=True)

def _silu(x):
    return jax.nn.silu(x)

def _sigmoid(x):
    return jax.nn.sigmoid(x)

def _layernorm(x, axis=-1, eps=1e-05):
    m = jnp.mean(x, axis=axis, keepdims=True)
    v = jnp.var(x, axis=axis, keepdims=True)
    return (x - m) / jnp.sqrt(v + eps)

def _scatter_add(tgt, idx, src, axis=0):
    return tgt.at[idx].add(src)

def _segment_sum(src, seg, n):
    return jax.ops.segment_sum(src, seg, n)
kernel_name = 'mk_flamingo_gated_d2_seqx_r8_045f1e'

def setup_inputs(seed: int=0):
    np.random.seed(seed)
    _w = jnp.asarray

    def _rec_inputs():
        import jax
        import jax.numpy as jnp
        _rk = jax.random.key(seed)
        x = 7.22e-05 + 1 * jax.random.normal(jax.random.fold_in(_rk, 1), (4, 256, 256), jnp.float32)
        _lenS = 256 - jax.random.randint(jax.random.fold_in(_rk, 7), (4,), 0, max(1, 256 // 4) + 1, jnp.int32)
        _lenS2 = 1601 - jax.random.randint(jax.random.fold_in(_rk, 8), (4,), 0, max(1, 1601 // 4) + 1, jnp.int32)
        _ctx_1024P = jax.random.normal(jax.random.fold_in(_rk, 11), (4, 16, 128), jnp.float32)
        _ctx_1024c = jax.random.dirichlet(jax.random.fold_in(_rk, 511), 0.3 * jnp.ones((16,), jnp.float32), (4, 1601))
        _ctx_1024t = jnp.einsum('bsk,bkd->bsd', _ctx_1024c, _ctx_1024P)
        _ctx_1024t = _ctx_1024t * jax.lax.rsqrt(jnp.mean(jnp.square(_ctx_1024t)) + 1e-12) * 0.953939
        ctx_1024 = -0.000673644 + 1.00013 * (_ctx_1024t + 0.3 * jax.random.normal(jax.random.fold_in(_rk, 611), (4, 1601, 128), jnp.float32))
        _g = jax.random.normal(jax.random.fold_in(_rk, 9001), (2, 2), jnp.float32)
        _g = jnp.sign(_g) * jnp.maximum(jnp.abs(_g), 1.0) + (_g == 0) * 1.0
        g_xattn = _g[0]
        g_ffn = _g[1]
        return (x, ctx_1024, g_xattn, g_ffn)
    x, ctx_1024, g_xattn, g_ffn = _rec_inputs()

    def _L0_xattn_setup():
        import jax, jax.numpy as jnp
        import numpy as np
        B, S1, S2, DCA = (2, 256, 128, 16)
        QDIM, KDIM, H = (256, 128, 16)
        HD = QDIM // H
        SCALE = HD ** (-0.5)
        EPS = 1e-06
        DCA_WEIGHT = 1.0

        def _ln(t, w, b):
            m = jnp.mean(t, axis=-1, keepdims=True)
            v = jnp.var(t, axis=-1, keepdims=True)
            return (t - m) * jax.lax.rsqrt(v + EPS) * w + b

        def _attn(q, k, v):
            s = jnp.einsum('bhqd,bhkd->bhqk', q, k) * SCALE
            p = jax.nn.softmax(s, axis=-1)
            return jnp.einsum('bhqk,bhkd->bhqd', p, v)
        key = jax.random.key(seed)
        ks = jax.random.split(key, 8)
        w = lambda k, shape: jax.random.normal(k, shape, jnp.float32) * 0.02
        return {'x': jax.random.normal(ks[0], (B, S1, QDIM), jnp.float32), 'y': jax.random.normal(ks[1], (B, S2 + DCA, KDIM), jnp.float32), 'Wq': w(ks[2], (QDIM, QDIM)), 'bq': jnp.zeros((QDIM,), jnp.float32), 'Wk': w(ks[3], (KDIM, QDIM)), 'bk': jnp.zeros((QDIM,), jnp.float32), 'Wv': w(ks[4], (KDIM, QDIM)), 'bv': jnp.zeros((QDIM,), jnp.float32), 'Wkv_dca': w(ks[5], (KDIM, 2 * QDIM)), 'bkv_dca': jnp.zeros((2 * QDIM,), jnp.float32), 'qn_w': jnp.ones((HD,), jnp.float32), 'qn_b': jnp.zeros((HD,), jnp.float32), 'kn_w': jnp.ones((HD,), jnp.float32), 'kn_b': jnp.zeros((HD,), jnp.float32), 'kn_dca_w': jnp.ones((HD,), jnp.float32), 'kn_dca_b': jnp.zeros((HD,), jnp.float32), 'Wo': w(ks[6], (QDIM, QDIM)), 'bo': jnp.zeros((QDIM,), jnp.float32)}
    _L0_xattn_all = _L0_xattn_setup()
    _L0_xattn_in = {k: v for k, v in _L0_xattn_all.items() if k in ('Wq', 'bq', 'Wk', 'bk', 'Wv', 'bv', 'Wkv_dca', 'bkv_dca', 'qn_w', 'qn_b', 'kn_w', 'kn_b', 'kn_dca_w', 'kn_dca_b', 'Wo', 'bo')}
    del _L0_xattn_all

    def _L0_ffn_setup():
        import jax, jax.numpy as jnp
        import numpy as np
        HIDDEN = 256
        INTER = 96
        N_EXPERTS = 32
        TOP_K = 8
        key = jax.random.key(seed)
        k = jax.random.split(key, 5)
        s = 1.0 / np.sqrt(HIDDEN)
        return {'hidden_states': jax.random.normal(k[0], (1, 128, HIDDEN), jnp.float32), 'gate_w': jax.random.normal(k[1], (HIDDEN, N_EXPERTS), jnp.float32) * s, 'w_gate': jax.random.normal(k[2], (N_EXPERTS, HIDDEN, INTER), jnp.float32) * s, 'w_up': jax.random.normal(k[3], (N_EXPERTS, HIDDEN, INTER), jnp.float32) * s, 'w_down': jax.random.normal(k[4], (N_EXPERTS, INTER, HIDDEN), jnp.float32) * (1.0 / np.sqrt(INTER))}
    _L0_ffn_all = _L0_ffn_setup()
    _L0_ffn_in = {k: v for k, v in _L0_ffn_all.items() if k in ('gate_w', 'w_gate', 'w_up', 'w_down')}
    del _L0_ffn_all

    def _L1_xattn_setup():
        import jax, jax.numpy as jnp
        import numpy as np
        EPS = 1e-05

        def rmsnorm(x, g, eps=EPS):
            var = jnp.mean(jnp.square(x), axis=-1, keepdims=True)
            return x * jax.lax.rsqrt(var + eps) * g
        key = jax.random.key(seed)
        ks = jax.random.split(key, 8)
        B, Sq, Skv = (2, 512, 64)
        dim, cdim, H, D = (256, 128, 16, 128)
        inner = H * D
        s = lambda f: 1.0 / np.sqrt(f)
        return {'hidden_states': jax.random.normal(ks[0], (B, Sq, dim), jnp.float32), 'encoder_hidden_states': jax.random.normal(ks[1], (B, Skv, cdim), jnp.float32), 'Wq': jax.random.normal(ks[2], (dim, inner), jnp.float32) * s(dim), 'Wk': jax.random.normal(ks[3], (cdim, inner), jnp.float32) * s(cdim), 'Wv': jax.random.normal(ks[4], (cdim, inner), jnp.float32) * s(cdim), 'Wo': jax.random.normal(ks[5], (inner, dim), jnp.float32) * s(inner), 'gq': jnp.ones((D,), jnp.float32), 'gk': jnp.ones((D,), jnp.float32)}
    _L1_xattn_all = _L1_xattn_setup()
    _L1_xattn_in = {k: v for k, v in _L1_xattn_all.items() if k in ('Wq', 'Wk', 'Wv', 'Wo', 'gq', 'gk')}
    del _L1_xattn_all

    def _L1_ffn_setup():
        import jax, jax.numpy as jnp
        import numpy as np
        B, T, D, E, F, K, ND = (2, 32, 256, 64, 64, 4, 4)
        H = F * K
        N_SHARED = 2
        key = jax.random.key(seed)
        ks = jax.random.split(key, 12)
        s = lambda k, shape: jax.random.normal(k, shape, jnp.float32) * 0.02
        x = jax.random.normal(ks[0], (B, T, D), jnp.float32)
        Wr = s(ks[1], (E, D))
        router_bias = jnp.zeros((E,), jnp.float32)
        affinity = s(ks[2], (E, ND))
        te_W1 = s(ks[3], (D // 2, D))
        te_b1 = jnp.zeros((D // 2,), jnp.float32)
        te_W2 = s(ks[4], (ND, D // 2))
        te_b2 = jnp.zeros((ND,), jnp.float32)
        Wg = s(ks[5], (E, D, F))
        Wu = s(ks[6], (E, D, F))
        Wd = s(ks[7], (E, F, D))
        Sg = s(ks[8], (N_SHARED, D, H))
        Su = s(ks[9], (N_SHARED, D, H))
        Sd = s(ks[10], (N_SHARED, H, D))
        return dict(x=x, Wr=Wr, router_bias=router_bias, affinity=affinity, te_W1=te_W1, te_b1=te_b1, te_W2=te_W2, te_b2=te_b2, Wg=Wg, Wu=Wu, Wd=Wd, Sg=Sg, Su=Su, Sd=Sd)
    _L1_ffn_all = _L1_ffn_setup()
    _L1_ffn_in = {k: v for k, v in _L1_ffn_all.items() if k in ('Wr', 'router_bias', 'affinity', 'te_W1', 'te_b1', 'te_W2', 'te_b2', 'Wg', 'Wu', 'Wd', 'Sg', 'Su', 'Sd')}
    del _L1_ffn_all
    return {'x': x, 'ctx_1024': ctx_1024, 'g_xattn': g_xattn, 'g_ffn': g_ffn, 'L0_xattn_Wq': _L0_xattn_in['Wq'], 'L0_xattn_bq': _L0_xattn_in['bq'], 'L0_xattn_Wk': _L0_xattn_in['Wk'], 'L0_xattn_bk': _L0_xattn_in['bk'], 'L0_xattn_Wv': _L0_xattn_in['Wv'], 'L0_xattn_bv': _L0_xattn_in['bv'], 'L0_xattn_Wkv_dca': _L0_xattn_in['Wkv_dca'], 'L0_xattn_bkv_dca': _L0_xattn_in['bkv_dca'], 'L0_xattn_qn_w': _L0_xattn_in['qn_w'], 'L0_xattn_qn_b': _L0_xattn_in['qn_b'], 'L0_xattn_kn_w': _L0_xattn_in['kn_w'], 'L0_xattn_kn_b': _L0_xattn_in['kn_b'], 'L0_xattn_kn_dca_w': _L0_xattn_in['kn_dca_w'], 'L0_xattn_kn_dca_b': _L0_xattn_in['kn_dca_b'], 'L0_xattn_Wo': _L0_xattn_in['Wo'], 'L0_xattn_bo': _L0_xattn_in['bo'], 'L0_ffn_gate_w': _L0_ffn_in['gate_w'], 'L0_ffn_w_gate': _L0_ffn_in['w_gate'], 'L0_ffn_w_up': _L0_ffn_in['w_up'], 'L0_ffn_w_down': _L0_ffn_in['w_down'], 'L1_xattn_Wq': _L1_xattn_in['Wq'], 'L1_xattn_Wk': _L1_xattn_in['Wk'], 'L1_xattn_Wv': _L1_xattn_in['Wv'], 'L1_xattn_Wo': _L1_xattn_in['Wo'], 'L1_xattn_gq': _L1_xattn_in['gq'], 'L1_xattn_gk': _L1_xattn_in['gk'], 'L1_ffn_Wr': _L1_ffn_in['Wr'], 'L1_ffn_router_bias': _L1_ffn_in['router_bias'], 'L1_ffn_affinity': _L1_ffn_in['affinity'], 'L1_ffn_te_W1': _L1_ffn_in['te_W1'], 'L1_ffn_te_b1': _L1_ffn_in['te_b1'], 'L1_ffn_te_W2': _L1_ffn_in['te_W2'], 'L1_ffn_te_b2': _L1_ffn_in['te_b2'], 'L1_ffn_Wg': _L1_ffn_in['Wg'], 'L1_ffn_Wu': _L1_ffn_in['Wu'], 'L1_ffn_Wd': _L1_ffn_in['Wd'], 'L1_ffn_Sg': _L1_ffn_in['Sg'], 'L1_ffn_Su': _L1_ffn_in['Su'], 'L1_ffn_Sd': _L1_ffn_in['Sd']}

def reference(x, ctx_1024, g_xattn, g_ffn, L0_xattn_Wq, L0_xattn_bq, L0_xattn_Wk, L0_xattn_bk, L0_xattn_Wv, L0_xattn_bv, L0_xattn_Wkv_dca, L0_xattn_bkv_dca, L0_xattn_qn_w, L0_xattn_qn_b, L0_xattn_kn_w, L0_xattn_kn_b, L0_xattn_kn_dca_w, L0_xattn_kn_dca_b, L0_xattn_Wo, L0_xattn_bo, L0_ffn_gate_w, L0_ffn_w_gate, L0_ffn_w_up, L0_ffn_w_down, L1_xattn_Wq, L1_xattn_Wk, L1_xattn_Wv, L1_xattn_Wo, L1_xattn_gq, L1_xattn_gk, L1_ffn_Wr, L1_ffn_router_bias, L1_ffn_affinity, L1_ffn_te_W1, L1_ffn_te_b1, L1_ffn_te_W2, L1_ffn_te_b2, L1_ffn_Wg, L1_ffn_Wu, L1_ffn_Wd, L1_ffn_Sg, L1_ffn_Su, L1_ffn_Sd):
    import jax
    import jax.numpy as jnp

    def _L0_xattn_ref(x, y, Wq, bq, Wk, bk, Wv, bv, Wkv_dca, bkv_dca, qn_w, qn_b, kn_w, kn_b, kn_dca_w, kn_dca_b, Wo, bo):
        import jax, jax.numpy as jnp
        import numpy as np
        B, S1, S2, DCA = (2, 256, 128, 16)
        QDIM, KDIM, H = (256, 128, 16)
        HD = QDIM // H
        SCALE = HD ** (-0.5)
        EPS = 1e-06
        DCA_WEIGHT = 1.0

        def _ln(t, w, b):
            m = jnp.mean(t, axis=-1, keepdims=True)
            v = jnp.var(t, axis=-1, keepdims=True)
            return (t - m) * jax.lax.rsqrt(v + EPS) * w + b

        def _attn(q, k, v):
            s = jnp.einsum('bhqd,bhkd->bhqk', q, k) * SCALE
            p = jax.nn.softmax(s, axis=-1)
            return jnp.einsum('bhqk,bhkd->bhqd', p, v)
        b, s1, _ = x.shape
        y_dca = y[:, -DCA:, :]
        y_main = y[:, :-DCA, :]
        kv_dca = (y_dca @ Wkv_dca + bkv_dca).reshape(b, DCA, 2, H, HD)
        k_dca = _ln(kv_dca[:, :, 0], kn_dca_w, kn_dca_b)
        v_dca = kv_dca[:, :, 1]
        s2 = y_main.shape[1]
        q = _ln((x @ Wq + bq).reshape(b, s1, H, HD), qn_w, qn_b)
        kv = jnp.concatenate([y_main @ Wk + bk, y_main @ Wv + bv], axis=-1)
        kv = kv.reshape(b, s2, H, 2 * HD)
        k = _ln(kv[..., :HD], kn_w, kn_b)
        v = kv[..., HD:]
        qT = q.transpose(0, 2, 1, 3)
        ctx = _attn(qT, k.transpose(0, 2, 1, 3), v.transpose(0, 2, 1, 3))
        ctx = ctx.transpose(0, 2, 1, 3).reshape(b, s1, QDIM)
        ctx_dca = _attn(qT, k_dca.transpose(0, 2, 1, 3), v_dca.transpose(0, 2, 1, 3))
        ctx_dca = ctx_dca.transpose(0, 2, 1, 3).reshape(b, s1, QDIM)
        ctx = ctx + DCA_WEIGHT * ctx_dca
        return ctx @ Wo + bo

    def _L0_ffn_ref(hidden_states, gate_w, w_gate, w_up, w_down):
        import jax, jax.numpy as jnp
        import numpy as np
        HIDDEN = 256
        INTER = 96
        N_EXPERTS = 32
        TOP_K = 8
        B, S, H = hidden_states.shape
        E = gate_w.shape[1]
        x = hidden_states.reshape(-1, H)
        T = x.shape[0]
        K = TOP_K
        P = T * K
        C = 2 * (P // E)
        probs = jax.nn.softmax(x @ gate_w, axis=-1)
        w, sel = jax.lax.top_k(probs, K)
        w = w / jnp.sum(w, axis=-1, keepdims=True)
        flat_e = sel.reshape(-1)
        flat_t = jnp.repeat(jnp.arange(T), K)
        flat_w = w.reshape(-1)
        order = jnp.argsort(flat_e)
        se = flat_e[order]
        start = jnp.searchsorted(se, jnp.arange(E))
        pos = jnp.arange(P) - start[se]
        slot = jnp.where(pos < C, se * C + pos, E * C)
        slot_pair = jnp.full((E * C,), P, dtype=jnp.int32).at[slot].set(order.astype(jnp.int32), mode='drop')
        t_slot = jnp.concatenate([flat_t, jnp.array([T])])[slot_pair]
        w_slot = jnp.concatenate([flat_w, jnp.zeros((1,), flat_w.dtype)])[slot_pair]
        x_pad = jnp.concatenate([x, jnp.zeros((1, H), x.dtype)], axis=0)
        xg = x_pad[t_slot].reshape(E, C, H)
        g = jnp.einsum('ech,ehi->eci', xg, w_gate)
        u = jnp.einsum('ech,ehi->eci', xg, w_up)
        y = jnp.einsum('eci,eih->ech', jax.nn.silu(g) * u, w_down).reshape(E * C, H)
        out = jnp.zeros((T + 1, H), x.dtype).at[t_slot].add(w_slot[:, None] * y)
        return out[:T].reshape(B, S, H)

    def _L1_xattn_ref(hidden_states, encoder_hidden_states, Wq, Wk, Wv, Wo, gq, gk):
        import jax, jax.numpy as jnp
        import numpy as np
        EPS = 1e-05

        def rmsnorm(x, g, eps=EPS):
            var = jnp.mean(jnp.square(x), axis=-1, keepdims=True)
            return x * jax.lax.rsqrt(var + eps) * g
        B, Sq, _ = hidden_states.shape
        Skv = encoder_hidden_states.shape[1]
        D = gq.shape[0]
        H = Wq.shape[1] // D
        scale = 1.0 / np.sqrt(D)
        q = (hidden_states @ Wq).reshape(B, Sq, H, D)
        k = (encoder_hidden_states @ Wk).reshape(B, Skv, H, D)
        v = (encoder_hidden_states @ Wv).reshape(B, Skv, H, D)
        q = rmsnorm(q, gq)
        k = rmsnorm(k, gk)
        scores = jnp.einsum('bqhd,bkhd->bhqk', q, k) * scale
        attn = jax.nn.softmax(scores, axis=-1)
        out = jnp.einsum('bhqk,bkhd->bqhd', attn, v)
        out = out.reshape(B, Sq, H * D)
        return out @ Wo

    def _L1_ffn_ref(x, Wr, router_bias, affinity, te_W1, te_b1, te_W2, te_b2, Wg, Wu, Wd, Sg, Su, Sd):
        import jax, jax.numpy as jnp
        import numpy as np
        B, T, D, E, F, K, ND = (2, 32, 256, 64, 64, 4, 4)
        H = F * K
        N_SHARED = 2
        b, t, d = x.shape
        n = b * t
        flat = x.reshape(n, d)
        xm = x.mean(axis=1)
        h1 = jax.nn.gelu(xm @ te_W1.T + te_b1, approximate=False)
        task_dist = jax.nn.softmax(h1 @ te_W2.T + te_b2, axis=-1)
        dom = task_dist @ affinity.T
        logits = (flat @ Wr.T).reshape(b, t, E) + 0.5 * dom[:, None, :]
        logits = logits.reshape(n, E)
        scores = jax.nn.softmax(logits, axis=-1)
        _, topk_idx = jax.lax.top_k(logits + router_bias, K)
        topk_scores = jnp.take_along_axis(scores, topk_idx, axis=-1)
        topk_scores = topk_scores / (topk_scores.sum(-1, keepdims=True) + 1e-08)
        combine = jnp.zeros((n, E), x.dtype).at[jnp.arange(n)[:, None], topk_idx].add(topk_scores)
        g = jnp.einsum('nd,edf->enf', flat, Wg)
        u = jnp.einsum('nd,edf->enf', flat, Wu)
        h = jax.nn.silu(g) * u
        hw = h * combine.T[:, :, None]
        out = jnp.einsum('enf,efd->nd', hw, Wd)
        for i in range(Sg.shape[0]):
            sh = jax.nn.silu(flat @ Sg[i]) * (flat @ Su[i])
            out = out + sh @ Sd[i]
        return out.reshape(b, t, d)
    x = x + jnp.tanh(g_xattn[0]) * _L0_xattn_ref(_layernorm(x, axis=-1), ctx_1024, L0_xattn_Wq, L0_xattn_bq, L0_xattn_Wk, L0_xattn_bk, L0_xattn_Wv, L0_xattn_bv, L0_xattn_Wkv_dca, L0_xattn_bkv_dca, L0_xattn_qn_w, L0_xattn_qn_b, L0_xattn_kn_w, L0_xattn_kn_b, L0_xattn_kn_dca_w, L0_xattn_kn_dca_b, L0_xattn_Wo, L0_xattn_bo)
    x = x + jnp.tanh(g_ffn[0]) * _L0_ffn_ref(_layernorm(x, axis=-1), L0_ffn_gate_w, L0_ffn_w_gate, L0_ffn_w_up, L0_ffn_w_down)
    x = x + jnp.tanh(g_xattn[1]) * _L1_xattn_ref(_layernorm(x, axis=-1), ctx_1024, L1_xattn_Wq, L1_xattn_Wk, L1_xattn_Wv, L1_xattn_Wo, L1_xattn_gq, L1_xattn_gk)
    x = x + jnp.tanh(g_ffn[1]) * _L1_ffn_ref(_layernorm(x, axis=-1), L1_ffn_Wr, L1_ffn_router_bias, L1_ffn_affinity, L1_ffn_te_W1, L1_ffn_te_b1, L1_ffn_te_W2, L1_ffn_te_b2, L1_ffn_Wg, L1_ffn_Wu, L1_ffn_Wd, L1_ffn_Sg, L1_ffn_Su, L1_ffn_Sd)
    return x

_drawn_inputs = setup_inputs


def setup_inputs(seed=0):
    import zlib

    import numpy as np

    out = dict(_drawn_inputs(seed))
    spreads = {'g_ffn': (-1.0, 0.6),
     'L0_xattn_bq': (0.0, 0.8),
     'L0_xattn_bk': (0.0, 0.447),
     'L0_xattn_bv': (0.0, 0.377),
     'L0_xattn_bkv_dca': (0.0, 0.292),
     'L0_xattn_qn_w': (1.0, 0.6),
     'L0_xattn_qn_b': (0.0, 0.8),
     'L0_xattn_kn_w': (1.0, 0.6),
     'L0_xattn_kn_b': (0.0, 0.8),
     'L0_xattn_kn_dca_w': (1.0, 0.6),
     'L0_xattn_kn_dca_b': (0.0, 0.8),
     'L0_xattn_bo': (0.0, 0.1),
     'L1_xattn_gq': (1.0, 0.2),
     'L1_xattn_gk': (1.0, 0.2),
     'L1_ffn_router_bias': (0.0, 0.8),
     'L1_ffn_te_b1': (0.0, 0.8),
     'L1_ffn_te_b2': (0.0, 0.8)}
    factors = {'L0_xattn_Wq': 2.835,
     'L0_xattn_Wv': 2.72,
     'L1_ffn_Wr': 8.0,
     'L1_ffn_affinity': 8.0,
     'L1_ffn_te_W1': 8.0,
     'L1_ffn_te_W2': 8.0,
     'L1_ffn_Wg': 8.0,
     'L1_ffn_Wu': 8.0,
     'L1_ffn_Wd': 8.0,
     'L1_ffn_Sg': 3.303,
     'L1_ffn_Su': 3.245,
     'L1_ffn_Sd': 3.245}
    for name, (base, spread) in spreads.items():
        noise = np.random.default_rng([zlib.crc32(name.encode()), seed]).standard_normal(out[name].shape)
        drawn = base * np.exp(spread * noise) if base else spread * noise
        out[name] = jnp.asarray(drawn.astype(out[name].dtype))
    for name, factor in factors.items():
        out[name] = (out[name] * factor).astype(out[name].dtype)
    return out
```

```python
from contextlib import ExitStack

import concourse.bass as bass
from concourse import mybir

F32 = mybir.dt.float32
F32R = mybir.dt.float32r
BF16 = mybir.dt.bfloat16
ALU = mybir.AluOpType
ACT = mybir.ActivationFunctionType
AX = mybir.AxisListType.X

P = 128
B, SQ, D = 4, 256, 256
KV, C = 1601, 128
NT = B * SQ // P
KD = D // P
TB = SQ // P
KT = -(-KV // P)
KPAD = KT * P
HALF = 512

H0, D0 = 16, 16
DCA = 16
KMAIN = KV - DCA
KT0 = KT + 1
ROWS0 = [P] * (KT - 1) + [KMAIN - P * (KT - 1), DCA]
COL0 = [P * t for t in range(KT)] + [KMAIN]
HG = 4
NG = H0 // HG
SCALE0 = D0 ** -0.5
E0, I0, TOP0 = 32, 96, 8
CAP = 2 * (B * SQ * TOP0 // E0)
H1, D1 = 16, 128
ROWS1 = [P] * (KT - 1) + [KV - P * (KT - 1)]
E1, F1, TOP1, ND = 64, 64, 4, 4
NSH = 2
TOPS = 8
EXP_ROOM = 70.0
FAR = 3.0e38

NAMES = {}


PRIMED = ("pv0 k_turned scores0 probs0 o0_read ctx_made h1_made h_made down_done "
          "k1_reduced k1_squared probs1 pv1 summed den_made den_read o1_read y1_added").split()


def primed(count):
    return count + 1


class Steps:

    def __init__(self, eng, sem):
        self.eng, self.sem, self.n, self.i, self.per = eng, sem, 0, None, 0

    def did(self, ins):
        ins.then_inc(self.sem, 1)
        self.n += 1

    def wait(self):
        self.eng.wait_ge(self.sem, self.n if self.i is None else self.i * self.per + self.n)

    def do(self, ins):
        self.did(ins)
        self.wait()

    def enter(self, i, per):
        self.i, self.per, self.first = i, per, self.n

    def leave(self, rounds):
        assert self.n - self.first == self.per, (self.n - self.first, self.per)
        self.n = self.first + self.per * rounds
        self.i = None


def at(base, i, per, k):
    return base + k if i is None else i * per + (base + k)


def program(nc, a, out, stages=4):
    ctx = ExitStack()
    with ctx:
        def sem(name):
            return ctx.enter_context(nc.semaphore(name))

        def sb(name, shape, dt=F32, scope=ctx):
            return scope.enter_context(nc.sbuf_tensor("s_" + name, shape, dt))

        ps = ctx.enter_context(nc.psum_tensor("ps", [P, 8, 512], F32))
        x = sb("x", [P, NT, D])
        xn = sb("xn", [P, NT, D])
        xnT = sb("xnT", [P, KD, NT * P])
        ident = sb("ident", [P, P])
        ones = sb("ones", [P, 8])
        tg = sb("tg", [P, 4])
        bn = sb("bn", [P, NT, 6])
        mv = sb("mv", [P, NT, 2])
        lnv = sb("lnv", [P, NT])
        lnr = sb("lnr", [P, NT])
        tri = sb("tri", [P, P], BF16)
        onesb = sb("onesb", [P, P], BF16)
        sel0 = sb("sel0", [3 * E0, E0, I0], BF16)
        sel1 = sb("sel1", [P, E1, F1], BF16)
        wT0 = sb("wT0", [3 * E0, NT * P], BF16)
        wT1a = sb("wT1a", [P, NT * P], BF16)
        wT1b = sb("wT1b", [P, NT * P], BF16)
        zb = sb("zb", [P, HALF], BF16)
        ones512 = sb("ones512", [1, NT * P], BF16)

        sa = ExitStack()
        wq0 = sb("wq0", [P, KD, D], scope=sa)
        wkv0 = sb("wkv0", [P, 2 * D], scope=sa)
        wdca0 = sb("wdca0", [P, 2 * D], scope=sa)
        wo0 = sb("wo0", [P, KD, D], scope=sa)
        bq0 = sb("bq0", [P, D], scope=sa)
        bkv0 = sb("bkv0", [P, 2, 2 * D], scope=sa)
        bo0 = sb("bo0", [P, D], scope=sa)
        qnw = sb("qnw", [P, 2, H0 * D0], scope=sa)
        knwb = sb("knwb", [P, 2, KT0 * HG * D0], scope=sa)
        bnd = sb("bnd", [P, 6, D0], scope=sa)
        bsm = sb("bsm", [P, 32], scope=sa)
        ctxT0 = sb("ctxT0", [P, KV], scope=sa)
        qst = sb("qst", [P, H0, 4, D0], F32R, scope=sa)
        qT0 = sb("qT0", [P, H0 // 2, NT * P], F32R, scope=sa)
        kvp = sb("kvp", [P, KT0, H0, 2, D0], scope=sa)
        kc = sb("kc", [P, NG, KT0, HG, D0], scope=sa)
        kst = sb("kst", [P, KT0 * HG, 4, D0], scope=sa)
        kT0 = sb("kT0", [P, KT0 * 2 * P], F32R, scope=sa)
        vg = sb("vg", [P, KT0, HG, 2 * D0], scope=sa)
        qg = sb("qg", [P, 2, 2, SQ], F32R, scope=sa)
        p0 = sb("p0", [P, 2, 4 * SQ], scope=sa)
        qn = p0[:].rearrange("p a n -> p (a n)").rearrange("p (t h d) -> p t h d", t=NT, h=H0)
        ksq = kst[:].rearrange("p m r d -> p (m r d)")[:, 0:NG * KT0 * HG * D0]
        s1 = sb("s1", [P, KT0 * H0], scope=sa)
        s2 = sb("s2", [P, KT0 * H0], scope=sa)
        oT0 = qnw
        rd0 = sb("rd0", [P, 4 * HG], scope=sa)
        on0 = sb("on0", [P, 4 * HG, D0], scope=sa)
        sa.close()

        sc = ExitStack()
        gatew = sb("gatew", [P, KD, E0], scope=sc)
        wr1 = sb("wr1", [P, KD, E1], scope=sc)
        rb1 = sb("rb1", [P, E1], scope=sc)
        aff1 = sb("aff1", [ND, E1], scope=sc)
        te1 = sb("te1", [P, KD, P], scope=sc)
        teb1 = sb("teb1", [P, 1], scope=sc)
        te2 = sb("te2", [P, ND], scope=sc)
        teb2 = sb("teb2", [B, ND], scope=sc)
        xm = sb("xm", [P, KD * B], scope=sc)
        h1t = sb("h1t", [P, B], scope=sc)
        td = sb("td", [B, 4, ND], scope=sc)
        tdT = sb("tdT", [ND, B, P], scope=sc)
        rl = sb("rl", [P, NT, E1 + TOPS - TOP1], scope=sc)
        rr = sb("rr", [P, NT, E1 + TOPS - TOP1], scope=sc)
        re = sb("re", [P, NT, E1], scope=sc)
        rw = sb("rw", [P, NT, E1], scope=sc)
        m8 = sb("m8", [P, NT, TOPS], scope=sc)
        rsm = sb("rsm", [P, 6, NT], scope=sc)
        selb = sb("selb", [P, NT, E0], BF16, scope=sc)
        pre = sb("pre", [P, NT, E0], BF16, scope=sc)
        hi0 = sb("hi0", [E1, NT * P], BF16, scope=sc)
        mid0 = sb("mid0", [E1, NT * P], BF16, scope=sc)
        rem1 = sb("rem1", [E1, NT * P], scope=sc)
        rem2 = sb("rem2", [E1, NT * P], scope=sc)
        wg = sb("wg", [P, 2, KD, P], scope=sc)
        wu = sb("wu", [P, 2, KD, P], scope=sc)
        wd = sb("wd", [P, 2, D], scope=sc)
        sg = sb("sg", [P, HALF], scope=sc)
        hh = sb("hh", [P, HALF], scope=sc)
        hw = sb("hw", [P, 2, HALF], scope=sc)
        sc.close()

        se = ExitStack()
        wq1 = sb("wq1", [P, KD, H1 * D1], scope=se)
        wk1 = sb("wk1", [P, H1 * D1], scope=se)
        wkT1 = sb("wkT1", [P, H1, C], scope=se)
        wvT1 = sb("wvT1", [P, H1, C], scope=se)
        wo1 = sb("wo1", [P, H1, D], scope=se)
        m1 = sb("m1", [P, H1, D], scope=se)
        ctxT1 = sb("ctxT1", [P, 2, KV], scope=se)
        ctx1 = sb("ctx1", [P, 2, KT, C], scope=se)
        rk1 = sb("rk1", [P, KT, H1], scope=se)
        g1 = sb("g1", [P, 4], scope=se)
        g1r = sb("g1r", [P, 3, D1], scope=se)
        q1 = sb("q1", [P, H1, D1], scope=se)
        q1T = sb("q1T", [P, H1, TB, P], scope=se)
        qq1 = sb("qq1", [P, H1, SQ], scope=se)
        rq1 = sb("rq1", [P, 2, H1], scope=se)
        ksq1 = sb("ksq1", [P, 2, HALF], scope=se)
        p1 = sb("p1", [P, 3, 2, SQ], scope=se)
        dsum = sb("dsum", [P, 2 * SQ], scope=se)
        oT1 = sb("oT1", [P, 2 * SQ], scope=se)
        rd1 = sb("rd1", [P, 4], scope=se)
        se.close()
        acc1 = xn

        S = {n: sem(n) for n in (
            "x_loaded gates_loaded w0_loaded small0_loaded ctxT0_loaded experts0_loaded experts1_loaded "
            "router_loaded w1_loaded ctx1_loaded0 ctx1_loaded1 stored "
            "consts_made ident_made dve_steps act_steps pool_steps tanh_made "
            "ln_var ln_std ln_done ln_turned xnT_act xnT_dve "
            "q0_made q0_read q0_var q0_std qst_ready qT0_turned qT0_act "
            "bound_sq bound_root bound0_ready "
            "kv_made kv_read k_centered k_squared k_var k_std k_normed k_ready "
            "hi_ready kst_ready vg_ready qg_ready k_turned kT_act kT_dve "
            "scores0 probs0 pv0 o0_read o0_turned ctx_made cx_turned cxT_act y0_made x_updated "
            "logits_made logits_read r_shifted r_exp sel_ready pos_made w_ready w_turned wT_ready "
            "xm_ready te_made te_gelu tl_made tl_shifted tl_exp td_ready td_turned tdT_ready "
            "g_made u_made w_made silu_made h1_made h_made down_done wslot0 wslot1 "
            "m1_made m1_read bound1_ready "
            "k1_made k1_squared k1_reduced k1_var k1_std rk1_ready "
            "q1_made q1_read q1_var q1_std q1_normed q1_turned q1T_ready qq_made qq_read "
            "scores1 probs1 pv1 summed o1_read den_made den_read y1_made y1_added").split()}
        s = type("Sems", (), S)

        xf = a["x"].rearrange("b s d -> (b s) d").rearrange("(t p) d -> p t d", p=P)
        of = out.rearrange("b s d -> (b s) d").rearrange("(t p) d -> p t d", p=P)

        def vsrc(t, g):
            return t[:, :, bass.ds(g * HG, HG), 1, :]

        def act_turn(act, k):
            act.wait_ge(s.ln_var, k + 1)
            nc.scalar.activation(lnr[:], lnv[:], ACT.Sqrt).then_inc(s.ln_std, 1)
            act.wait_ge(s.ln_turned, 16 * (k + 1) - 8)
            for j in range(2):
                nc.scalar.copy(xnT[:, 0, j * HALF:(j + 1) * HALF], ps[:, j, :]).then_inc(s.xnT_act, 1)

        def act_ffn(act, u0, i, units):
            for j in range(units):
                u = at(u0, i, 4, j)
                act.wait_ge(s.g_made, at(u0, i, 4, j + 1))
                act.wait_ge(s.h1_made, primed(u))
                nc.scalar.activation(sg[0:act_rows[0], :], ps[0:act_rows[0], 4, :], ACT.Silu).then_inc(s.silu_made, 1)

        act_rows = [I0]

        def kc_group(g):
            return kc[:].rearrange("p g t h d -> p (g t h) d")[:, bass.ds(g * (KT0 * HG), KT0 * HG), :]

        def rk_col(t, hp, j, r):
            return rk1[0:r, t, bass.ds(hp * 2 + j, 1)]

        def pe_turn(pe, k):
            pe.wait_ge(s.ln_done, NT * (k + 1))
            for j in range(4):
                for t in range(4):
                    tt = 4 * (j % 2) + t
                    nc.tensor.transpose(ps[:, j, t * P:(t + 1) * P], xn[:, tt, (j // 2) * P:(j // 2 + 1) * P],
                                        ident[:]).then_inc(s.ln_turned, 1)
            pe.wait_ge(s.xnT_act, 2 * (k + 1))
            pe.wait_ge(s.xnT_dve, 2 * (k + 1))

        def pe_zero(pe):
            for j in range(4):
                ins = nc.tensor.matmul(ps[:, j, :], zb[:, 0:P], zb[:], start=True, stop=False, skip_group_check=True)
            ins.then_inc(s.down_done, 1)

        def pe_up(pe, u0, i, j, rows, weight, loaded):
            slot, half = j // 2 % 2, j % 2
            n = slice(half * HALF, (half + 1) * HALF)
            if half == 0:
                pe.wait_ge(s.wslot1 if slot else s.wslot0, loaded)
            pe.wait_ge(s.silu_made, at(u0, i, 4, j))
            for k in range(KD):
                ins = nc.tensor.matmul(ps[0:rows, 4, :], wg[:, slot, k, 0:rows], xnT[:, k, n], start=k == 0, stop=k == KD - 1)
            ins.then_inc(s.g_made, 1)
            pe.wait_ge(s.h1_made, primed(at(u0, i, 4, j)))
            for k in range(KD):
                ins = nc.tensor.matmul(ps[0:rows, 5, :], wu[:, slot, k, 0:rows], xnT[:, k, n], start=k == 0, stop=k == KD - 1)
            ins.then_inc(s.u_made, 1)
            pe.wait_ge(s.h_made, primed(at(u0, i, 4, j)))
            parts = weight(i, j)
            for k, (sel, wt) in enumerate(parts):
                ins = nc.tensor.matmul(ps[0:rows, 6, :], sel, wt[:, n], start=k == 0, stop=k == len(parts) - 1)
            ins.then_inc(s.w_made, 1)

        def pe_down(pe, u0, i, j, rows):
            slot, half = j // 2 % 2, j % 2
            pe.wait_ge(s.h_made, primed(at(u0, i, 4, j + 1)))
            for t in range(4):
                tt = half * 4 + t
                ins = nc.tensor.matmul(ps[:, tt // 2, (tt % 2) * D:(tt % 2 + 1) * D], hw[0:rows, j % 2, t * P:(t + 1) * P],
                                       wd[0:rows, slot, :], start=False, stop=False, skip_group_check=True)
            ins.then_inc(s.down_done, 1)

        def pe_up4(pe, i, weight):
            i1 = i + 1
            pe_up(pe, 0, i1, 0, I0, weight, i1 * 48 + 48)

        def ksq1v(t, j):
            return t[:].rearrange("p h t n -> p t h n")[:, j]

        def ones_src(t):
            return t[:, 0:1]


        block = ctx.enter_context(nc.Block())
        NW0 = 13

        def store(sp):
            sp.wait_ge(s.x_updated, stages)
            sp.dma_start(of, x[:]).then_inc(s.stored, 16)
            sp.wait_ge(s.stored, 16)

        @block.sync
        def _(sp):
            for name in PRIMED:
                sp.sem_inc(S[name], 1)
            sp.dma_start(x[:], xf).then_inc(s.x_loaded, 16)
            sp.dma_start(tg[:], a["gates"]).then_inc(s.gates_loaded, 16)
            sp.dma_start(wq0[:], a["L0_xattn_Wq"].rearrange("(k p) n -> p k n", p=P)).then_inc(s.w0_loaded, 16)
            sp.dma_start(wkv0[:], a["Wkv0"]).then_inc(s.w0_loaded, 16)
            sp.dma_start(wdca0[:], a["Wdca0"]).then_inc(s.w0_loaded, 16)
            sp.dma_start(ctxT0[:], a["ctxT"][0]).then_inc(s.ctxT0_loaded, 16)
            sp.dma_start(wo0[:], a["L0_xattn_Wo"].rearrange("(k p) n -> p k n", p=P)).then_inc(s.w0_loaded, 16)
            for dst, name in ((bq0[:], "bq0"), (bkv0[:], "bkv0"), (bo0[:], "bo0"), (qnw[:], "qnw"),
                              (knwb[:], "knwb"), (bnd[:], "bnd")):
                sp.dma_start(dst, a[name]).then_inc(s.small0_loaded, 16)
            for b in range(1, B):
                sp.wait_ge(s.kv_made, KT0 * b)
                sp.dma_start(ctxT0[:], a["ctxT"][b]).then_inc(s.ctxT0_loaded, 16)

            def weights(e, slot, wait, g_src, u_src, d_src, width):
                if wait is not None:
                    sp.wait_ge(s.down_done, primed(wait))
                w = s.wslot1 if slot else s.wslot0
                sp.dma_start(g_src[1](wg), g_src[0]).then_inc(w, 16)
                sp.dma_start(u_src[1](wu), u_src[0]).then_inc(w, 16)
                sp.dma_start(d_src[1](wd), d_src[0]).then_inc(w, 16)

            def expert0(e, slot, wait):
                weights(e, slot, wait,
                        (a["L0_ffn_w_gate"][e].rearrange("(k p) i -> p k i", p=P), lambda w: w[:, slot, :, 0:I0]),
                        (a["L0_ffn_w_up"][e].rearrange("(k p) i -> p k i", p=P), lambda w: w[:, slot, :, 0:I0]),
                        (a["L0_ffn_w_down"][e], lambda w: w[0:I0, slot, :]), I0)

            def load_router():
                for dst, src in ((gatew[:], a["L0_ffn_gate_w"].rearrange("(k p) n -> p k n", p=P)),
                                 (wr1[:], a["WrT"].rearrange("(k p) n -> p k n", p=P)),
                                 (rb1[:], a["rb1"]), (aff1[:], a["affT"]),
                                 (te1[:], a["te_W1T"].rearrange("(k p) n -> p k n", p=P)),
                                 (teb1[:], a["teb1"]), (te2[:], a["te_W2T"]), (teb2[:], a["teb2"])):
                    sp.dma_start(dst, src).then_inc(s.router_loaded, 16)

            if stages < 2:
                return store(sp)
            sp.wait_ge(s.x_updated, 1)
            load_router()
            expert0(0, 0, None)
            expert0(1, 1, None)
            with sp.Fori(1, E0 // 2) as i:
                for slot in range(2):
                    expert0(i * 2 + slot, slot, i * 4 + (1 + 2 * slot - 2))

            if stages < 3:
                return store(sp)
            sp.wait_ge(s.x_updated, 2)
            for dst, src in ((wk1[:], a["L1_xattn_Wk"]), (wkT1[:], a["WkT1"]), (wvT1[:], a["WvT1"]),
                             (wo1[:], a["L1_xattn_Wo"].rearrange("(h d) n -> d h n", d=D1)),
                             (wq1[:], a["L1_xattn_Wq"].rearrange("(k p) n -> p k n", p=P)),
                             (g1[:, 0:2], a["g1"]), (g1r[:, 0:2, :], a["g1r"])):
                sp.dma_start(dst, src).then_inc(s.w1_loaded, 16)
            for b in range(B):
                loaded = s.ctx1_loaded1 if b % 2 else s.ctx1_loaded0
                if b >= 2:
                    sp.wait_ge(s.y1_made, H1 // 2 * (b - 1))
                sp.dma_start(ctxT1[:, b % 2, :], a["ctxT"][b]).then_inc(loaded, 16)
                sp.dma_start(ctx1[:, b % 2, 0:KT - 1, :],
                             a["ctx_1024"][b, 0:P * (KT - 1), :].rearrange("(t p) c -> p t c", p=P)).then_inc(loaded, 16)
                sp.dma_start(ctx1[0:ROWS1[-1], b % 2, KT - 1, :], a["ctx_1024"][b, P * (KT - 1):KV, :]).then_inc(loaded, 16)

            if stages < 4:
                return store(sp)
            sp.wait_ge(s.x_updated, 3)
            load_router()
            D0N = 1 + 2 * E0

            def shared(j, slot, wait):
                i, c = j // 2, j % 2
                weights(j, slot, wait,
                        (a["L1_ffn_Sg"][i, :, c * P:(c + 1) * P].rearrange("(k p) n -> p k n", p=P), lambda w: w[:, slot, :, :]),
                        (a["L1_ffn_Su"][i, :, c * P:(c + 1) * P].rearrange("(k p) n -> p k n", p=P), lambda w: w[:, slot, :, :]),
                        (a["L1_ffn_Sd"][i, c * P:(c + 1) * P, :], lambda w: w[:, slot, :]), P)

            def pair1(e, slot, wait):
                if wait is not None:
                    sp.wait_ge(s.down_done, primed(wait))
                w = s.wslot1 if slot else s.wslot0
                for j in range(2):
                    sp.dma_start(wg[:, slot, :, j * F1:(j + 1) * F1],
                                 a["L1_ffn_Wg"][e * 2 + j].rearrange("(k p) n -> p k n", p=P)).then_inc(w, 16)
                    sp.dma_start(wu[:, slot, :, j * F1:(j + 1) * F1],
                                 a["L1_ffn_Wu"][e * 2 + j].rearrange("(k p) n -> p k n", p=P)).then_inc(w, 16)
                    sp.dma_start(wd[j * F1:(j + 1) * F1, slot, :], a["L1_ffn_Wd"][e * 2 + j]).then_inc(w, 16)

            for j in range(2 * NSH):
                shared(j, j % 2, None if j < 2 else D0N + 1 + 2 * (j - 1))
            with sp.Fori(0, E1 // 4) as i:
                for slot in range(2):
                    pair1(i * 2 + slot, slot, i * 4 + (D0N + 1 + 2 * (2 * NSH + slot - 1)))

            store(sp)

        @block.gpsimd
        def _(pool):
            nc.gpsimd.memset(ident[:], 0.0).then_inc(s.pool_steps, 1)
            nc.gpsimd.memset(tri[:], 1.0).then_inc(s.pool_steps, 1)
            nc.gpsimd.memset(sel0[:], 0.0).then_inc(s.pool_steps, 1)
            nc.gpsimd.memset(sel1[:], 0.0).then_inc(s.pool_steps, 1)
            pool.wait_ge(s.pool_steps, 4)
            nc.gpsimd.affine_select(out=ident[:], in_=ident[:], compare_op=ALU.not_equal, fill=1.0, base=0,
                                    pattern=[[-1, P]], channel_multiplier=1).then_inc(s.ident_made, 1)
            nc.gpsimd.affine_select(out=tri[:], in_=tri[:], compare_op=ALU.is_gt, fill=0.0, base=0,
                                    pattern=[[1, P]], channel_multiplier=-1).then_inc(s.consts_made, 1)
            n = 4
            for j in range(3):
                nc.gpsimd.affine_select(out=sel0[:], in_=sel0[:], compare_op=ALU.not_equal, fill=1.0, base=-j * E0,
                                        pattern=[[-1, E0], [0, I0]], channel_multiplier=1).then_inc(s.pool_steps, 1)
                n += 1
                pool.wait_ge(s.pool_steps, n)
            for j in range(2):
                nc.gpsimd.affine_select(out=sel1[:], in_=sel1[:], compare_op=ALU.not_equal, fill=1.0, base=-j * E1,
                                        pattern=[[-1, E1], [0, F1]], channel_multiplier=1).then_inc(s.pool_steps, 1)
                n += 1
                pool.wait_ge(s.pool_steps, n)
            nc.gpsimd.memset(zb[:], 0.0).then_inc(s.consts_made, 1)
            nc.gpsimd.memset(onesb[:], 1.0).then_inc(s.consts_made, 1)
            nc.gpsimd.memset(ones[:], 1.0).then_inc(s.consts_made, 1)
            nc.gpsimd.memset(vg[:], 1.0).then_inc(s.pool_steps, 1)
            n += 1
            pool.wait_ge(s.pool_steps, n)
            for t in (KT0 - 2, KT0 - 1):
                nc.gpsimd.affine_select(out=vg[:, t], in_=vg[:, t], compare_op=ALU.is_gt, fill=0.0, base=ROWS0[t],
                                        pattern=[[0, HG], [0, 2 * D0]], channel_multiplier=-1)\
                    .then_inc(s.consts_made if t == KT0 - 1 else s.pool_steps, 1)
            n += 1
            nc.gpsimd.memset(wT1b[:], 0.0).then_inc(s.consts_made, 1)

            pool.wait_ge(s.small0_loaded, 16 * 6)
            pool.wait_ge(s.consts_made, 5)
            for b in range(B):
                pool.wait_ge(s.k_normed, b + 1)
                flat = kc[:].rearrange("p g t h d -> p g (t h d)")
                nc.gpsimd.tensor_tensor(flat, flat, knwb[:, 0, :].unsqueeze(1).to_broadcast([P, NG, KT0 * HG * D0]),
                                        ALU.mult).then_inc(s.pool_steps, 1)
                n += 1
                pool.wait_ge(s.pool_steps, n)
                nc.gpsimd.tensor_tensor(flat, flat, knwb[:, 1, :].unsqueeze(1).to_broadcast([P, NG, KT0 * HG * D0]),
                                        ALU.add).then_inc(s.k_ready, 1)
                with pool.Fori(0, NG) as g:
                    pool.wait_ge(s.pv0, primed(at(KT0 * NG * b, g, KT0, 0)))
                    nc.gpsimd.tensor_copy(vg[:, :, :, 0:D0],
                                          vsrc(kvp, g)).then_inc(s.vg_ready, 1)

        @block.scalar
        def _(act):
            act.wait_ge(s.gates_loaded, 16)
            nc.scalar.activation(tg[:], tg[:], ACT.Tanh).then_inc(s.tanh_made, 1)
            act.wait_ge(s.bound_sq, 1)
            nc.scalar.activation(bsm[:, 6:12], bsm[:, 0:6], ACT.Sqrt).then_inc(s.bound_root, 1)
            act_turn(act, 0)
            act.wait_ge(s.q0_var, 1)
            nc.scalar.activation(s1[:, 0:NT * H0], s1[:, 0:NT * H0], ACT.Sqrt).then_inc(s.q0_std, 1)
            for t in range(NT):
                act.wait_ge(s.qT0_turned, 2 * t + 2)
                nc.scalar.copy(qT0[:, :, t * P:(t + 1) * P],
                               ps[:, 4:6, :].rearrange("p a (b n) -> p (a b) n", b=4)).then_inc(s.qT0_act, 1)
            act.wait_ge(s.bound0_ready, 1)
            for b in range(B):
                act.wait_ge(s.k_centered, b + 1)
                nc.scalar.activation(ksq, kc[:].rearrange("p g t h d -> p (g t h d)"), ACT.Square).then_inc(s.k_squared, 1)
                act.wait_ge(s.k_var, b + 1)
                nc.scalar.activation(s2[:], s2[:], ACT.Sqrt).then_inc(s.k_std, 1)
                act.wait_ge(s.k_ready, b + 1)
                with act.Fori(0, NG) as g:
                    it = NG * b
                    act.wait_ge(s.k_turned, primed(at(7 * it, g, 7, 0)))
                    nc.scalar.copy(kst[:, :, 0:2, :].bitcast(F32R),
                                   kc_group(g).unsqueeze(2).to_broadcast([P, KT0 * HG, 2, D0])).then_inc(s.hi_ready, 1)
                    for j in range(0, 7, 2):
                        act.wait_ge(s.k_turned, primed(at(7 * it, g, 7, j + 1)))
                        if j == 0:
                            act.wait_ge(s.scores0, primed(at(KT0 * it, g, KT0, 0)))
                        nc.scalar.copy(kT0[:, j * 512:(j + 1) * 512], ps[:, 6, :]).then_inc(s.kT_act, 1)
                    for t in range(KT0):
                        act.wait_ge(s.scores0, primed(at(KT0 * it, g, KT0, t + 1)))
                        act.wait_ge(s.pv0, primed(at(KT0 * it, g, KT0, max(t - 1, 0))))
                        r = ROWS0[t]
                        nc.scalar.activation(p0[0:r, t % 2, :],
                                             ps[0:r, 2 * (t % 2):2 * (t % 2) + 2, :].rearrange("p a n -> p (a n)"),
                                             ACT.Exp, bias=bsm[0:r, (25 if t == KT0 - 1 else 24):(26 if t == KT0 - 1 else 25)],
                                             scale=SCALE0).then_inc(s.probs0, 1)
            act.wait_ge(s.cx_turned, 16)
            for j in range(4):
                nc.scalar.copy(xnT[:, j // 2, (j % 2) * HALF:(j % 2 + 1) * HALF], ps[:, j, :]).then_inc(s.cxT_act, 1)
            if stages < 2:
                return
            act_turn(act, 1)
            act.wait_ge(s.r_shifted, 1)
            nc.scalar.activation(re[:, :, 0:E0], rl[:, :, 0:E0], ACT.Exp).then_inc(s.r_exp, 1)
            act_rows[0] = I0
            with act.Fori(0, E0 // 2) as i:
                act_ffn(act, 0, i, 4)
            if stages < 3:
                return
            act_turn(act, 2)
            for b in range(B):
                with act.Fori(0, 4) as i:
                    for t in range(KT):
                        k = 4 * KT * b
                        act.wait_ge(s.k1_made, at(k, i, KT, t + 1))
                        act.wait_ge(s.k1_reduced, primed(at(k, i, KT, max(t - 1, 0))))
                        r = ROWS1[t]
                        nc.scalar.activation(ksq1[0:r, t % 2, :], ps[0:r, t % 4, :], ACT.Square).then_inc(s.k1_squared, 1)
                act.wait_ge(s.k1_var, b + 1)
                nc.scalar.activation(rk1[:], rk1[:], ACT.Sqrt).then_inc(s.k1_std, 1)
                for t in range(TB):
                    act.wait_ge(s.q1_made, TB * b + t + 1)
                    nc.scalar.copy(q1[:].rearrange("p h d -> p (h d)"),
                                   ps[:, 4:8, :].rearrange("p a n -> p (a n)")).then_inc(s.q1_read, 1)
                    act.wait_ge(s.q1_var, TB * b + t + 1)
                    nc.scalar.activation(rq1[:, 0, :], rq1[:, 0, :], ACT.Sqrt).then_inc(s.q1_std, 1)
                for j in range(H1 // 2):
                    act.wait_ge(s.qq_made, 8 * b + j + 1)
                    nc.scalar.copy(qq1[:, 2 * j:2 * j + 2, :].rearrange("p h n -> p (h n)"),
                                   ps[:, j % 4, :]).then_inc(s.qq_read, 1)
                act.wait_ge(s.rk1_ready, b + 1)
                act.wait_ge(s.bound1_ready, 1)
                with act.Fori(0, H1 // 2) as hp:
                    k = KT * 8 * b
                    for t in range(KT):
                        act.wait_ge(s.scores1, at(k, hp, KT, t + 1))
                        act.wait_ge(s.pv1, primed(at(k, hp, KT, max(t - 2, 0))))
                        act.wait_ge(s.summed, primed(at(k, hp, KT, max(t - 2, 0))))
                        r = ROWS1[t]
                        for j in range(2):
                            ins = nc.scalar.activation(p1[0:r, t % 3, j, :], ps[0:r, t % 3, j * SQ:(j + 1) * SQ], ACT.Exp,
                                                       bias=g1[0:r, 3:4], scale=rk_col(t, hp, j, r))
                        ins.then_inc(s.probs1, 1)
            if stages < 4:
                return
            act_turn(act, 3)
            act.wait_ge(s.te_made, 1)
            nc.scalar.activation(h1t[:], ps[:, 6, 0:B], ACT.Gelu, bias=teb1[:, 0:1]).then_inc(s.te_gelu, 1)
            act.wait_ge(s.tl_shifted, 1)
            nc.scalar.activation(td[:, 1, :], td[:, 0, :], ACT.Exp).then_inc(s.tl_exp, 1)
            act.wait_ge(s.r_shifted, 2)
            nc.scalar.activation(re[:], rl[:, :, 0:E1], ACT.Exp).then_inc(s.r_exp, 1)
            act_rows[0] = P
            u0 = 2 * E0
            act_ffn(act, u0, None, 8)
            with act.Fori(0, E1 // 4) as i:
                act_ffn(act, u0 + 8, i, 4)

        @block.tensor
        def _(pe):
            pe.wait_ge(s.ident_made, 1)
            pe_turn(pe, 0)
            pe.wait_ge(s.w0_loaded, 16 * 4)
            for t in range(NT):
                for k in range(KD):
                    ins = nc.tensor.matmul(ps[:, 4 + t // 2, (t % 2) * D:(t % 2 + 1) * D], xnT[:, k, t * P:(t + 1) * P],
                                           wq0[:, k, :], start=k == 0, stop=k == KD - 1)
                if t % 2:
                    ins.then_inc(s.q0_made, 1)
            pe.wait_ge(s.q0_read, 4)
            for t in range(NT):
                pe.wait_ge(s.qst_ready, t + 1)
                pe.wait_ge(s.qT0_act, t)
                for hp in range(H0 // 2):
                    ins = nc.tensor.transpose(ps[:, 4 + hp // 4, (hp % 4) * P:(hp % 4 + 1) * P],
                                              qst[:, 2 * hp:2 * hp + 2, :, :].rearrange("p h r d -> p (h r d)").bitcast(F32), ident[:])
                    if hp % 4 == 3:
                        ins.then_inc(s.qT0_turned, 1)
            pe.wait_ge(s.qT0_act, NT)
            for b in range(B):
                pe.wait_ge(s.ctxT0_loaded, 16 * (b + 1))
                for t in range(KT0):
                    if KT0 * b + t >= 4:
                        pe.wait_ge(s.kv_read, KT0 * b + t - 3)
                    if t == 0 and b:
                        pe.wait_ge(s.probs0, primed(KT0 * NG * b))
                    nc.tensor.matmul(ps[0:ROWS0[t], t % 4, :], ctxT0[:, COL0[t]:COL0[t] + ROWS0[t]],
                                     (wdca0 if t == KT0 - 1 else wkv0)[:], start=True, stop=True).then_inc(s.kv_made, 1)
                pe.wait_ge(s.kv_read, KT0 * (b + 1))
                with pe.Fori(0, NG) as g:
                    it = NG * b
                    pe.wait_ge(s.kst_ready, at(it, g, 1, 1))
                    pe.wait_ge(s.ctx_made, primed(at(it, g, 1, 0)))
                    for j in range(7):
                        if j >= 2:
                            if j % 2:
                                pe.wait_ge(s.kT_dve, at(3 * it, g, 3, j // 2))
                            else:
                                pe.wait_ge(s.kT_act, at(4 * it, g, 4, j // 2))
                        for m in range(4):
                            t, hp = 2 * j + m // 2, m % 2
                            ins = nc.tensor.transpose(ps[:, 6 + j % 2, m * P:(m + 1) * P],
                                                      kst[:, t * HG + 2 * hp:t * HG + 2 * hp + 2, :, :]
                                                      .rearrange("p h r d -> p (h r d)"), ident[:])
                        ins.then_inc(s.k_turned, 1)
                    pe.wait_ge(s.kT_act, at(4 * it, g, 4, 4))
                    pe.wait_ge(s.kT_dve, at(3 * it, g, 3, 3))
                    pe.wait_ge(s.qg_ready, at(it, g, 1, 1))
                    pe.wait_ge(s.vg_ready, at(it, g, 1, 1))

                    def scores(t):
                        pe.wait_ge(s.probs0, primed(at(KT0 * it, g, KT0, max(t - 1, 0))))
                        for hp in range(2):
                            c = (2 * t + hp) * P
                            ins = nc.tensor.matmul(ps[0:ROWS0[t], 2 * (t % 2) + hp, :], kT0[:, c:c + ROWS0[t]],
                                                   qg[:, hp, :, :].rearrange("p a n -> p (a n)"), start=True, stop=True)
                        ins.then_inc(s.scores0, 1)

                    def values(t):
                        pe.wait_ge(s.probs0, primed(at(KT0 * it, g, KT0, t + 1)))
                        if t == 0:
                            pe.wait_ge(s.o0_read, primed(at(it, g, 1, 0)))
                        dca = t == KT0 - 1
                        for h in range(HG):
                            ins = nc.tensor.matmul(ps[32 * h:32 * h + 32, 5 if dca else 4, 0:SQ], vg[:, t, h, :],
                                                   p0[:, t % 2, h * SQ:(h + 1) * SQ], start=t == 0 or dca,
                                                   stop=t >= KT0 - 2, skip_group_check=True)
                        ins.then_inc(s.pv0, 1)

                    scores(0)
                    for t in range(KT0):
                        if t + 1 < KT0:
                            scores(t + 1)
                        values(t)
                    pe.wait_ge(s.o0_read, primed(at(it, g, 1, 1)))
                    for j in range(4):
                        ins = nc.tensor.transpose(ps[:, 6, j * P:(j + 1) * P], oT0[:, j // 2, (j % 2) * P:(j % 2 + 1) * P], ident[:])
                    ins.then_inc(s.o0_turned, 1)
            pe.wait_ge(s.ctx_made, primed(NG * B))
            for j in range(4):
                for t in range(4):
                    tt = 4 * (j % 2) + t
                    nc.tensor.transpose(ps[:, j, t * P:(t + 1) * P], xn[:, tt, (j // 2) * P:(j // 2 + 1) * P],
                                        ident[:]).then_inc(s.cx_turned, 1)
            pe.wait_ge(s.cxT_act, 4)
            for t in range(NT):
                for k in range(KD):
                    ins = nc.tensor.matmul(ps[:, t // 2, (t % 2) * D:(t % 2 + 1) * D], xnT[:, k, t * P:(t + 1) * P],
                                           wo0[:, k, :], start=k == 0, stop=k == KD - 1)
            ins.then_inc(s.y0_made, 1)
            if stages < 2:
                return

            pe_turn(pe, 1)
            pe.wait_ge(s.consts_made, 6)
            pe.wait_ge(s.router_loaded, 16 * 8)
            for t in range(NT):
                for k in range(KD):
                    ins = nc.tensor.matmul(ps[:, 7, t * E0:(t + 1) * E0], xnT[:, k, t * P:(t + 1) * P], gatew[:, k, :],
                                           start=k == 0, stop=k == KD - 1)
            ins.then_inc(s.logits_made, 1)
            pe.wait_ge(s.sel_ready, 1)
            for t in range(NT):
                nc.tensor.matmul(ps[:, 7, t * E0:(t + 1) * E0], tri[:], selb[:, t, :], start=True, stop=False)
                ins = nc.tensor.matmul(ps[:, 7, t * E0:(t + 1) * E0], onesb[:], pre[:, t, :], start=False, stop=True)
            ins.then_inc(s.pos_made, 1)
            pe.wait_ge(s.w_ready, 1)
            for t in range(NT):
                ins = nc.tensor.transpose(ps[0:E0, 4 + t // 4, (t % 4) * P:(t % 4 + 1) * P], rw[:, t, 0:E0], ident[:])
            ins.then_inc(s.w_turned, 1)
            pe.wait_ge(s.wT_ready, 1)
            pe_zero(pe)

            def weight0(i, j):
                e = i * 2 + j // 2
                return [(sel0[:, bass.ds(e, 1), :].rearrange("p e n -> p (e n)"), wT0)]

            pe_up(pe, 0, 0, 0, I0, weight0, 48)
            last = E0 // 2 - 1
            with pe.Fori(0, last) as i:
                for j in range(4):
                    if j < 3:
                        pe_up(pe, 0, i, j + 1, I0, weight0, i * 48 + 48)
                    else:
                        pe_up4(pe, i, weight0)
                    pe_down(pe, 0, i, j, I0)
            for j in range(4):
                if j < 3:
                    pe_up(pe, 4 * last, None, j + 1, I0, lambda _, jj: weight0(last, jj), 48 * (last + 1))
                pe_down(pe, 4 * last, None, j, I0)
            if stages < 3:
                return

            pe_turn(pe, 2)
            pe.wait_ge(s.w1_loaded, 16 * 7)
            for h in range(H1):
                if h >= 8 and h % 2 == 0:
                    pe.wait_ge(s.m1_read, h // 2 - 3)
                ins = nc.tensor.matmul(ps[:, 4 + h // 2 % 4, (h % 2) * D:(h % 2 + 1) * D], wvT1[:, h, :], wo1[:, h, :],
                                       start=True, stop=True)
                if h % 2:
                    ins.then_inc(s.m1_made, 1)
            pe.wait_ge(s.m1_read, 8)
            for b in range(B):
                pe.wait_ge(s.ctx1_loaded1 if b % 2 else s.ctx1_loaded0, 48 * (b // 2 + 1))
                with pe.Fori(0, 4) as i:
                    for t in range(KT):
                        pe.wait_ge(s.k1_squared, primed(at(4 * KT * b, i, KT, max(t - 3, 0))))
                        if t == 0 and b:
                            pe.wait_ge(s.probs1, primed(KT * 8 * b))
                        nc.tensor.matmul(ps[0:ROWS1[t], t % 4, :], ctxT1[:, b % 2, t * P:t * P + ROWS1[t]],
                                         wk1[:, bass.ts(i, 512)], start=True, stop=True).then_inc(s.k1_made, 1)
                for t in range(TB):
                    tt = TB * b + t
                    if b and t == 0:
                        pe.wait_ge(s.y1_added, primed(8 * b))
                    if t:
                        pe.wait_ge(s.q1T_ready, tt * 4)
                    for j in range(4):
                        for k in range(KD):
                            ins = nc.tensor.matmul(ps[:, 4 + j, :], xnT[:, k, tt * P:(tt + 1) * P], wq1[:, k, j * 512:(j + 1) * 512],
                                                   start=k == 0, stop=k == KD - 1)
                    ins.then_inc(s.q1_made, 1)
                    pe.wait_ge(s.q1_normed, tt + 1)
                    for j in range(4):
                        for h in range(4):
                            ins = nc.tensor.transpose(ps[:, 4 + j, h * P:(h + 1) * P], q1[:, 4 * j + h, :], ident[:])
                        ins.then_inc(s.q1_turned, 1)
                pe.wait_ge(s.q1T_ready, TB * 4 * (b + 1))
                pe.wait_ge(s.k1_squared, primed(4 * KT * (b + 1)))
                for j in range(H1 // 2):
                    if j >= 4:
                        pe.wait_ge(s.qq_read, 8 * b + j - 3)
                    for h in range(2):
                        ins = nc.tensor.matmul(ps[:, j % 4, h * SQ:(h + 1) * SQ], wkT1[:, 2 * j + h, :],
                                               q1T[:, 2 * j + h, :, :].rearrange("p t n -> p (t n)"), start=True, stop=True)
                    ins.then_inc(s.qq_made, 1)
                pe.wait_ge(s.qq_read, 8 * (b + 1))
                with pe.Fori(0, H1 // 2) as hp:
                    k0 = KT * 8 * b

                    def scores1(t):
                        pe.wait_ge(s.probs1, primed(at(k0, hp, KT, max(t - 2, 0))))
                        nc.tensor.matmul(ps[0:ROWS1[t], t % 3, :], ctxT1[:, b % 2, t * P:t * P + ROWS1[t]],
                                         qq1[:].rearrange("p h n -> p (h n)")[:, bass.ts(hp, 2 * SQ)],
                                         start=True, stop=True).then_inc(s.scores1, 1)

                    scores1(0)
                    for t in range(KT):
                        if t + 1 < KT:
                            scores1(t + 1)
                        pe.wait_ge(s.probs1, primed(at(k0, hp, KT, t + 1)))
                        if t == 0:
                            pe.wait_ge(s.o1_read, primed(at(8 * b, hp, 1, 0)))
                        nc.tensor.matmul(ps[:, 3, :], ctx1[0:ROWS1[t], b % 2, t, :],
                                         p1[0:ROWS1[t], t % 3, :, :].rearrange("p a n -> p (a n)"),
                                         start=t == 0, stop=t == KT - 1).then_inc(s.pv1, 1)
                    pe.wait_ge(s.summed, primed(at(k0, hp, KT, KT)))
                    pe.wait_ge(s.den_read, primed(at(8 * b, hp, 1, 0)))
                    for j in range(4):
                        ins = nc.tensor.matmul(ps[:, 4, j:j + 1], dsum[:, j * P:(j + 1) * P], ones[:, 0:1], start=True, stop=True)
                    ins.then_inc(s.den_made, 1)
                    pe.wait_ge(s.o1_read, primed(at(8 * b, hp, 1, 1)))
                    pe.wait_ge(s.y1_added, primed(at(8 * b, hp, 1, 0)))
                    for j in range(4):
                        ins = nc.tensor.matmul(ps[:, 5 + j // 2, (j % 2) * D:(j % 2 + 1) * D], oT1[:, j * P:(j + 1) * P],
                                               m1[:].rearrange("p h n -> p (h n)")[:, bass.ds(hp * (2 * D) + (j // 2) * D, D)],
                                               start=True, stop=True)
                    ins.then_inc(s.y1_made, 1)
            if stages < 4:
                return

            pe.wait_ge(s.probs1, primed(KT * 8 * B))
            pe_turn(pe, 3)
            pe.wait_ge(s.router_loaded, 16 * 16)
            pe.wait_ge(s.xm_ready, 1)
            for k in range(KD):
                ins = nc.tensor.matmul(ps[:, 6, 0:B], te1[:, k, :], xm[:, k * B:(k + 1) * B], start=k == 0, stop=k == KD - 1)
            ins.then_inc(s.te_made, 1)
            pe.wait_ge(s.te_gelu, 1)
            nc.tensor.matmul(ps[0:B, 6, 0:ND], h1t[:], te2[:], start=True, stop=True).then_inc(s.tl_made, 1)
            pe.wait_ge(s.td_ready, 1)
            nc.tensor.transpose(ps[0:ND, 6, 0:B], td[:, 3, :], ident[0:B, 0:B]).then_inc(s.td_turned, 1)
            pe.wait_ge(s.tdT_ready, 1)
            for t in range(NT):
                for k in range(KD):
                    nc.tensor.matmul(ps[:, 7, t * E1:(t + 1) * E1], xnT[:, k, t * P:(t + 1) * P], wr1[:, k, :],
                                     start=k == 0, stop=False)
                ins = nc.tensor.matmul(ps[:, 7, t * E1:(t + 1) * E1], tdT[:, t // TB, :], aff1[:], start=False, stop=True)
            ins.then_inc(s.logits_made, 1)
            pe.wait_ge(s.w_ready, 2)
            for t in range(NT):
                ins = nc.tensor.transpose(ps[0:E1, 4 + t // 4, (t % 4) * P:(t % 4 + 1) * P], rw[:, t, :], ident[:])
            ins.then_inc(s.w_turned, 1)
            pe.wait_ge(s.wT_ready, 2)
            pe_zero(pe)
            u0 = 2 * E0
            base = 48 * E0 // 2

            def weight_one(i, j):
                return [(onesb[0:1, :], ones512)]

            def weight1(i, j):
                e = i * 4 + j // 2 * 2
                sel = sel1[:].rearrange("p e n -> p (e n)")[:, bass.ds(e * F1, 2 * F1)]
                return [(sel, wT1a), (sel, wT1b)]

            pe_up(pe, u0, None, 0, P, weight_one, base + 48)
            for j in range(8):
                if j < 7:
                    pe_up(pe, u0, None, j + 1, P, weight_one, base + 48 * ((j + 1) // 4 + 1))
                else:
                    pe_up(pe, u0 + 8, None, 0, P, lambda i, jj: weight1(0, jj), base + 96 + 96)
                pe_down(pe, u0, None, j, P)
            last = E1 // 4 - 1
            with pe.Fori(0, last) as i:
                for j in range(4):
                    if j < 3:
                        pe_up(pe, u0 + 8, i, j + 1, P, weight1, i * 96 + (base + 96 + 96))
                    else:
                        i1 = i + 1
                        pe_up(pe, u0 + 8, i1, 0, P, weight1, i1 * 96 + (base + 96 + 96))
                    pe_down(pe, u0 + 8, i, j, P)
            for j in range(4):
                if j < 3:
                    pe_up(pe, u0 + 8 + 4 * last, None, j + 1, P, lambda _, jj: weight1(last, jj), 96 * last + (base + 96 + 96))
                pe_down(pe, u0 + 8 + 4 * last, None, j, P)


        @block.vector
        def _(dve):
            v = nc.vector
            me = Steps(dve, s.dve_steps)

            def norm(k):
                for t in range(NT):
                    me.did(v.bn_stats(bn[:, t, :], x[:, t, :]))
                me.wait()
                for t in range(NT):
                    me.did(v.bn_aggr(mv[:, t, :], bn[:, t, :]))
                me.wait()
                v.tensor_scalar(lnv[:], mv[:, :, 1], 1e-5, None, ALU.add).then_inc(s.ln_var, 1)
                dve.wait_ge(s.ln_std, k + 1)
                me.do(v.reciprocal(lnv[:], lnr[:]))
                for t in range(NT):
                    v.tensor_scalar(xn[:, t, :], x[:, t, :], mv[:, t, 0:1], lnv[:, t:t + 1],
                                    ALU.subtract, ALU.mult).then_inc(s.ln_done, 1)
                dve.wait_ge(s.ln_turned, 16 * (k + 1))
                for j in range(2):
                    v.tensor_copy(xnT[:, 1, j * HALF:(j + 1) * HALF], ps[:, 2 + j, :]).then_inc(s.xnT_dve, 1)

            def bc(ap, n):
                return ap.unsqueeze(2).to_broadcast([ap.shape[0], ap.shape[1], n])

            me.did(v.memset(ones512[:], 1.0))
            me.did(v.memset(kvp[:], 0.0))
            me.did(v.memset(qg[:].bitcast(F32), 0.0))
            dve.wait_ge(s.x_loaded, 16)
            dve.wait_ge(s.small0_loaded, 96)
            me.do(v.tensor_tensor(on0[:, 0:6, :], bnd[:], bnd[:], ALU.mult))
            v.tensor_reduce(bsm[:, 0:6], on0[:, 0:6, :], AX, ALU.add).then_inc(s.bound_sq, 1)
            me.do(v.tensor_reduce(bsm[:, 12:18], bnd[:], AX, ALU.max, apply_absolute_value=True))
            dve.wait_ge(s.bound_root, 1)
            pair = bsm[:, 12:18].rearrange("p (n two) -> p n two", two=2)
            root = bsm[:, 6:12].rearrange("p (n two) -> p n two", two=2)
            me.do(v.scalar_tensor_tensor(out=bsm[:, 18:21], in0=pair[:, :, 0], scalar=float(D0) ** 0.5, in1=root[:, :, 1],
                                         op0=ALU.mult, op1=ALU.add))
            me.do(v.tensor_scalar(bsm[:, 22:24], bsm[:, 19:21], bsm[:, 18:19], SCALE0, ALU.mult, ALU.mult))
            me.do(v.tensor_scalar(bsm[:, 22:24], bsm[:, 22:24], EXP_ROOM, 0.0, ALU.subtract, ALU.max))
            v.tensor_scalar(bsm[:, 24:26], bsm[:, 22:24], -1.0, None, ALU.mult).then_inc(s.bound0_ready, 1)
            norm(0)
            for j in range(4):
                dve.wait_ge(s.q0_made, j + 1)
                v.tensor_tensor(qn[:, 2 * j:2 * j + 2, :, :].rearrange("p t h d -> p t (h d)"),
                                ps[:, 4 + j, :].rearrange("p (t n) -> p t n", t=2),
                                bq0[:].unsqueeze(1).to_broadcast([P, 2, D]), ALU.add).then_inc(s.q0_read, 1)
            dve.wait_ge(s.q0_read, 4)
            NQ = NT * H0
            qf = qn.rearrange("p t h d -> p (t h) d")
            qtmp = kc[:].rearrange("p g t h d -> p (g t h) d")[:, 0:NQ, :]
            me.do(v.tensor_reduce(s2[:, 0:NQ], qf, AX, ALU.add))
            me.do(v.tensor_scalar(s2[:, 0:NQ], s2[:, 0:NQ], 1.0 / D0, None, ALU.mult))
            me.do(v.tensor_tensor(qf, qf, bc(s2[:, 0:NQ], D0), ALU.subtract))
            me.do(v.tensor_tensor(qtmp, qf, qf, ALU.mult))
            me.do(v.tensor_reduce(s1[:, 0:NQ], qtmp, AX, ALU.add))
            v.tensor_scalar(s1[:, 0:NQ], s1[:, 0:NQ], 1.0 / D0, 1e-6, ALU.mult, ALU.add).then_inc(s.q0_var, 1)
            dve.wait_ge(s.q0_std, 1)
            me.do(v.reciprocal(s2[:, 0:NQ], s1[:, 0:NQ]))
            me.do(v.tensor_tensor(qf, qf, bc(s2[:, 0:NQ], D0), ALU.mult))
            q3 = qn.rearrange("p t h d -> p t (h d)")
            me.do(v.tensor_tensor(q3, q3, qnw[:, 0, :].unsqueeze(1).to_broadcast([P, NT, D]), ALU.mult))
            me.do(v.tensor_tensor(q3, q3, qnw[:, 1, :].unsqueeze(1).to_broadcast([P, NT, D]), ALU.add))
            for t in range(NT):
                if t:
                    dve.wait_ge(s.qT0_turned, 2 * t)
                for r in range(0, 4, 2):
                    me.did(v.tensor_copy(qst[:, :, r, :], qn[:, t, :, :]))
                me.wait()
                me.did(v.tensor_tensor(qst[:, :, 1, :], qn[:, t, :, :], qst[:, :, 0, :].bitcast(F32), ALU.subtract))
                v.tensor_tensor(qst[:, :, 3, :], qn[:, t, :, :], qst[:, :, 0, :].bitcast(F32), ALU.subtract).then_inc(s.qst_ready, 1)
            dve.wait_ge(s.qT0_act, NT)
            for b in range(B):
                if b:
                    dve.wait_ge(s.vg_ready, NG * b)
                for t in range(KT0):
                    dve.wait_ge(s.kv_made, KT0 * b + t + 1)
                    r = ROWS0[t]
                    v.tensor_tensor(kvp[0:r, t].rearrange("p h two d -> p (h two d)"), ps[0:r, t % 4, :],
                                    bkv0[0:r, 1 if t == KT0 - 1 else 0, :], ALU.add).then_inc(s.kv_read, 1)
                dve.wait_ge(s.kv_read, KT0 * (b + 1))
                kview = kvp[:].rearrange("p t h two d -> p (t h) two d")[:, :, 0, :]
                me.do(v.tensor_reduce(s1[:], kview, AX, ALU.add))
                me.do(v.tensor_scalar(s1[:], s1[:], 1.0 / D0, None, ALU.mult))
                s1v = s1[:].rearrange("p (t h) -> p t h", t=KT0)
                for g in range(NG):
                    ins = v.tensor_tensor(kc[:, g], kvp[:, :, g * HG:(g + 1) * HG, 0, :],
                                          s1v[:, :, g * HG:(g + 1) * HG].unsqueeze(3).to_broadcast([P, KT0, HG, D0]),
                                          ALU.subtract)
                ins.then_inc(s.k_centered, 1)
                dve.wait_ge(s.k_squared, b + 1)
                me.do(v.tensor_reduce(s2[:], ksq.rearrange("p (m d) -> p m d", d=D0), AX, ALU.add))
                v.tensor_scalar(s2[:], s2[:], 1.0 / D0, 1e-6, ALU.mult, ALU.add).then_inc(s.k_var, 1)
                dve.wait_ge(s.k_std, b + 1)
                me.do(v.reciprocal(s1[:], s2[:]))
                kf = kc[:].rearrange("p g t h d -> p (g t h) d")
                v.tensor_tensor(kf, kf, bc(s1[:], D0), ALU.mult).then_inc(s.k_normed, 1)
                dve.wait_ge(s.k_ready, b + 1)
                with dve.Fori(0, NG) as g:
                    it = NG * b
                    me.enter(g, 6)
                    dve.wait_ge(s.scores0, primed(at(KT0 * it, g, KT0, 0)))
                    me.did(v.tensor_copy(qg[0:64, :, 0, :], qT0[0:64, bass.ds(g * 2, 2), b * SQ:(b + 1) * SQ]))
                    v.tensor_copy(qg[64:P, :, 1, :], qT0[64:P, bass.ds(g * 2, 2), b * SQ:(b + 1) * SQ]).then_inc(s.qg_ready, 1)
                    dve.wait_ge(s.hi_ready, at(it, g, 1, 1))
                    v.tensor_tensor(kst[:, :, 2:4, :].bitcast(F32R), kc_group(g).unsqueeze(2).to_broadcast([P, KT0 * HG, 2, D0]),
                                    kst[:, :, 0:2, :], ALU.subtract).then_inc(s.kst_ready, 1)
                    for j in range(1, 7, 2):
                        dve.wait_ge(s.k_turned, primed(at(7 * it, g, 7, j + 1)))
                        v.tensor_copy(kT0[:, j * 512:(j + 1) * 512], ps[:, 7, :]).then_inc(s.kT_dve, 1)
                    dve.wait_ge(s.pv0, primed(at(KT0 * it, g, KT0, KT0)))
                    v.tensor_copy(oT0[:], ps[:, 4:6, 0:SQ]).then_inc(s.o0_read, 1)
                    dve.wait_ge(s.o0_turned, at(it, g, 1, 1))
                    o = ps[:, 6, :].rearrange("p (n d) -> p n d", d=2 * D0)
                    me.do(v.tensor_copy(rd0[:], o[:, :, D0]))
                    me.do(v.reciprocal(rd0[:], rd0[:]))
                    me.do(v.tensor_tensor(on0[:], o[:, :, 0:D0], bc(rd0[:], D0), ALU.mult))
                    me.do(v.tensor_tensor(on0[:, 0:2 * HG, :], on0[:, 0:2 * HG, :], on0[:, 2 * HG:4 * HG, :], ALU.add))
                    me.did(v.tensor_copy(xn[:, TB * b:TB * b + TB, bass.ds(g * (HG * D0), HG * D0)],
                                  on0[:, 0:2 * HG, :].rearrange("p (t h) d -> p t (h d)", t=TB)))
                    v.tensor_copy(rd0[:, 0:1], ones_src(rd0)).then_inc(s.ctx_made, 1)
                    me.leave(NG)
            dve.wait_ge(s.y0_made, 1)
            ks = ksq[:, 0:NT * D]
            me.do(v.tensor_tensor(ks.rearrange("p (t n) -> p t n", t=NT), ps[:, 0:4, :].rearrange("p a (b n) -> p (a b) n", b=2),
                                  bo0[:].unsqueeze(1).to_broadcast([P, NT, D]), ALU.add))
            dve.wait_ge(s.tanh_made, 1)
            xflat = x[:].rearrange("p t n -> p (t n)")
            v.scalar_tensor_tensor(out=xflat, in0=ks, scalar=tg[:, 0:1], in1=xflat, op0=ALU.mult, op1=ALU.add).then_inc(s.x_updated, 1)
            dve.wait_ge(s.x_updated, 1)
            if stages < 2:
                return

            def shifted(E, k):
                dve.wait_ge(s.logits_made, k)
                lg = ps[:, 7, 0:NT * E].rearrange("p (t e) -> p t e", t=NT)
                me.do(v.tensor_copy(rr[:, :, 0:E], lg))
                me.do(v.tensor_reduce(rsm[:, 0, :], rr[:, :, 0:E], AX, ALU.max))
                v.tensor_tensor(rl[:, :, 0:E], rr[:, :, 0:E], bc(rsm[:, 0, :], E), ALU.subtract).then_inc(s.r_shifted, 1)
                dve.wait_ge(s.r_exp, k)

            def weights_parts(E, dsts, k):
                dve.wait_ge(s.w_turned, k)
                wt = ps[0:E, 4:6, :].rearrange("p a n -> p (a n)")
                me.do(v.tensor_copy(hi0[0:E, :], wt))
                me.do(v.tensor_tensor(rem1[0:E, :], wt, hi0[0:E, :], ALU.subtract))
                me.do(v.tensor_copy(mid0[0:E, :], rem1[0:E, :]))
                me.do(v.tensor_tensor(rem2[0:E, :], rem1[0:E, :], mid0[0:E, :], ALU.subtract))
                me.did(v.tensor_copy(dsts[0], hi0[0:E, :]))
                me.did(v.tensor_copy(dsts[1], mid0[0:E, :]))
                me.do(v.tensor_copy(dsts[2], rem2[0:E, :]))
                v.tensor_copy(rem1[0:1, 0:1], rem2[0:1, 0:1]).then_inc(s.wT_ready, 1)

            def ffn(u0, i, units, rows):
                for j in range(units):
                    dve.wait_ge(s.silu_made, at(u0, i, 4, j + 1))
                    dve.wait_ge(s.u_made, at(u0, i, 4, j + 1))
                    dve.wait_ge(s.h_made, primed(at(u0, i, 4, j)))
                    v.tensor_tensor(hh[0:rows, :], sg[0:rows, :], ps[0:rows, 5, :], ALU.mult).then_inc(s.h1_made, 1)
                    dve.wait_ge(s.h1_made, primed(at(u0, i, 4, j + 1)))
                    dve.wait_ge(s.w_made, at(u0, i, 4, j + 1))
                    dve.wait_ge(s.down_done, primed(at(u0 + (2 if u0 >= 2 * E0 else 1), i, 4, j - 1)))
                    v.tensor_tensor(hw[0:rows, j % 2, :], hh[0:rows, :], ps[0:rows, 6, :], ALU.mult).then_inc(s.h_made, 1)

            norm(1)
            shifted(E0, 1)
            for t in range(NT):
                me.did(v.max(m8[:, t, :], re[:, t, 0:E0]))
            me.wait()
            for t in range(NT):
                me.did(v.match_replace(rr[:, t, 0:E0], m8[:, t, :], re[:, t, 0:E0], -1.0))
            me.wait()
            me.do(v.tensor_scalar(selb[:], rr[:, :, 0:E0], 0.0, None, ALU.is_lt))
            me.do(v.tensor_scalar(pre[:, 0, :], selb[:, 0, :], 0.0, None, ALU.mult))
            for t in range(1, NT):
                me.do(v.tensor_tensor(pre[:, t, :], pre[:, t - 1, :], selb[:, t - 1, :], ALU.add))
            v.tensor_tensor(rw[:, :, 0:E0], re[:, :, 0:E0], selb[:], ALU.mult).then_inc(s.sel_ready, 1)
            dve.wait_ge(s.sel_ready, 1)
            me.do(v.tensor_reduce(rsm[:, 1, :], rw[:, :, 0:E0], AX, ALU.add))
            me.do(v.reciprocal(rsm[:, 2, :], rsm[:, 1, :]))
            me.do(v.tensor_tensor(rw[:, :, 0:E0], rw[:, :, 0:E0], bc(rsm[:, 2, :], E0), ALU.mult))
            dve.wait_ge(s.pos_made, 1)
            wf = rw[:, :, 0:E0]
            v.scalar_tensor_tensor(out=wf, in0=ps[:, 7, 0:NT * E0].rearrange("p (t e) -> p t e", t=NT), scalar=float(CAP),
                                   in1=wf, op0=ALU.is_lt, op1=ALU.mult).then_inc(s.w_ready, 1)
            weights_parts(E0, [wT0[0:E0, :], wT0[E0:2 * E0, :], wT0[2 * E0:3 * E0, :]], 1)
            with dve.Fori(0, E0 // 2) as i:
                ffn(0, i, 4, I0)
            dve.wait_ge(s.down_done, primed(1 + 2 * E0))
            v.scalar_tensor_tensor(out=xflat, in0=ps[:, 0:4, :].rearrange("p a n -> p (a n)"), scalar=tg[:, 2:3], in1=xflat,
                                   op0=ALU.mult, op1=ALU.add).then_inc(s.x_updated, 1)
            dve.wait_ge(s.x_updated, 2)
            if stages < 3:
                return

            norm(2)
            dve.wait_ge(s.w1_loaded, 16 * 7)
            me.do(v.scalar_tensor_tensor(out=g1[:, 2:3], in0=g1[:, 0:1], scalar=float(D1) ** -0.5, in1=g1[:, 1:2],
                                         op0=ALU.mult, op1=ALU.mult))
            me.do(v.tensor_tensor(g1r[:, 2, :], g1r[:, 0, :], g1r[:, 1, :], ALU.mult))
            me.do(v.tensor_reduce(g1[:, 3:4], g1r[:, 2, :], AX, ALU.max, apply_absolute_value=True))
            me.do(v.tensor_scalar(g1[:, 3:4], g1[:, 3:4], float(D1) ** 0.5, -EXP_ROOM, ALU.mult, ALU.add))
            v.tensor_scalar(g1[:, 3:4], g1[:, 3:4], 0.0, -1.0, ALU.max, ALU.mult).then_inc(s.bound1_ready, 1)
            for j in range(8):
                dve.wait_ge(s.m1_made, j + 1)
                v.tensor_copy(m1[:, 2 * j:2 * j + 2, :].rearrange("p h n -> p (h n)"), ps[:, 4 + j % 4, :]).then_inc(s.m1_read, 1)
            for b in range(B):
                if b == 0:
                    me.do(v.memset(rk1[:], 1.0))
                    me.do(v.memset(acc1[:], 0.0))
                else:
                    dve.wait_ge(s.probs1, primed(KT * 8 * b))
                with dve.Fori(0, 4) as i:
                    for t in range(KT):
                        dve.wait_ge(s.k1_squared, primed(at(4 * KT * b, i, KT, t + 1)))
                        r = ROWS1[t]
                        v.tensor_reduce(rk1[0:r, t, bass.ts(i, 4)], ksq1[0:r, t % 2, :].rearrange("p (h d) -> p h d", h=4),
                                        AX, ALU.add).then_inc(s.k1_reduced, 1)
                dve.wait_ge(s.k1_reduced, primed(4 * KT * (b + 1)))
                v.tensor_scalar(rk1[:], rk1[:], 1.0 / D1, 1e-5, ALU.mult, ALU.add).then_inc(s.k1_var, 1)
                dve.wait_ge(s.k1_std, b + 1)
                v.reciprocal(rk1[:], rk1[:]).then_inc(s.rk1_ready, 1)
                for t in range(TB):
                    tt = TB * b + t
                    dve.wait_ge(s.q1_read, tt + 1)
                    sq = q1T[:].rearrange("p h t n -> p (h t n)")
                    sqv = ksq1v(q1T, t)
                    me.do(v.tensor_tensor(sqv, q1[:], q1[:], ALU.mult))
                    me.do(v.tensor_reduce(rq1[:, 1, :], sqv, AX, ALU.add))
                    v.tensor_scalar(rq1[:, 0, :], rq1[:, 1, :], 1.0 / D1, 1e-5, ALU.mult, ALU.add).then_inc(s.q1_var, 1)
                    dve.wait_ge(s.q1_std, tt + 1)
                    me.do(v.reciprocal(rq1[:, 1, :], rq1[:, 0, :]))
                    v.tensor_tensor(q1[:], q1[:], bc(rq1[:, 1, :], D1), ALU.mult).then_inc(s.q1_normed, 1)
                    for j in range(4):
                        dve.wait_ge(s.q1_turned, 4 * tt + j + 1)
                        v.tensor_scalar(q1T[:, 4 * j:4 * j + 4, t, :], ps[:, 4 + j, :].rearrange("p (h n) -> p h n", h=4),
                                        g1[:, 2:3], None, ALU.mult).then_inc(s.q1T_ready, 1)
                with dve.Fori(0, H1 // 2) as hp:
                    me.enter(hp, 3)
                    k0 = KT * 8 * b
                    for t in range(KT):
                        dve.wait_ge(s.probs1, primed(at(k0, hp, KT, t + 1)))
                        pt = p1[:, t % 3, :, :].rearrange("p a n -> p (a n)")
                        r = ROWS1[t]
                        if t == 0:
                            dve.wait_ge(s.den_made, primed(at(8 * b, hp, 1, 0)))
                            v.tensor_copy(dsum[:], pt).then_inc(s.summed, 1)
                        else:
                            dve.wait_ge(s.summed, primed(at(k0, hp, KT, t)))
                            v.tensor_tensor(dsum[0:r, :], dsum[0:r, :], pt[0:r, :], ALU.add).then_inc(s.summed, 1)
                    dve.wait_ge(s.pv1, primed(at(k0, hp, KT, KT)))
                    v.tensor_copy(oT1[:], ps[:, 3, :]).then_inc(s.o1_read, 1)
                    dve.wait_ge(s.den_made, primed(at(8 * b, hp, 1, 1)))
                    v.reciprocal(rd1[:], ps[:, 4, 0:4]).then_inc(s.den_read, 1)
                    dve.wait_ge(s.den_read, primed(at(8 * b, hp, 1, 1)))
                    dve.wait_ge(s.y1_made, at(8 * b, hp, 1, 1))
                    for j in range(4):
                        o = acc1[:, TB * b + j % 2, :]
                        if j == 2:
                            me.wait()
                        ins = v.scalar_tensor_tensor(out=o, in0=ps[:, 5 + j // 2, (j % 2) * D:(j % 2 + 1) * D], scalar=rd1[:, j:j + 1],
                                                     in1=o, op0=ALU.mult, op1=ALU.add)
                        if j < 3:
                            me.did(ins)
                        else:
                            ins.then_inc(s.y1_added, 1)
                    me.wait()
                    dve.wait_ge(s.y1_added, primed(at(8 * b, hp, 1, 1)))
                    me.leave(H1 // 2)
            v.scalar_tensor_tensor(out=xflat, in0=acc1[:].rearrange("p t n -> p (t n)"), scalar=tg[:, 1:2], in1=xflat,
                                   op0=ALU.mult, op1=ALU.add).then_inc(s.x_updated, 1)
            dve.wait_ge(s.x_updated, 3)
            if stages < 4:
                return

            norm(3)
            dve.wait_ge(s.xnT_act, 8)
            dve.wait_ge(s.xnT_dve, 8)
            dve.wait_ge(s.router_loaded, 16 * 16)
            me.do(v.tensor_reduce(xm[:], xnT[:].rearrange("p k (b n) -> p (k b) n", b=B), AX, ALU.add))
            v.tensor_scalar(xm[:], xm[:], 1.0 / SQ, None, ALU.mult).then_inc(s.xm_ready, 1)
            dve.wait_ge(s.tl_made, 1)
            me.do(v.tensor_tensor(td[:, 1, :], ps[0:B, 6, 0:ND], teb2[:], ALU.add))
            me.do(v.tensor_reduce(td[:, 2, 0:1], td[:, 1, :], AX, ALU.max))
            v.tensor_scalar(td[:, 0, :], td[:, 1, :], td[:, 2, 0:1], None, ALU.subtract).then_inc(s.tl_shifted, 1)
            dve.wait_ge(s.tl_exp, 1)
            me.do(v.tensor_reduce(td[:, 2, 0:1], td[:, 1, :], AX, ALU.add))
            me.do(v.reciprocal(td[:, 2, 1:2], td[:, 2, 0:1]))
            v.tensor_scalar(td[:, 3, :], td[:, 1, :], td[:, 2, 1:2], 0.5, ALU.mult, ALU.mult).then_inc(s.td_ready, 1)
            dve.wait_ge(s.td_turned, 1)
            v.tensor_copy(tdT[:], bc(ps[0:ND, 6, 0:B], P)).then_inc(s.tdT_ready, 1)
            shifted(E1, 2)
            me.did(v.tensor_reduce(rsm[:, 3, :], re[:], AX, ALU.add))
            me.did(v.tensor_tensor(rl[:, :, 0:E1], rr[:, :, 0:E1], rb1[:].unsqueeze(1).to_broadcast([P, NT, E1]), ALU.add))
            me.do(v.memset(rl[:, :, E1:E1 + TOPS - TOP1], -FAR))
            for t in range(NT):
                me.did(v.max(m8[:, t, :], rl[:, t, 0:E1]))
            me.wait()
            me.do(v.memset(m8[:, :, TOP1:TOPS], -FAR))
            for t in range(NT):
                me.did(v.match_replace(rr[:, t, :], m8[:, t, :], rl[:, t, :], FAR))
            me.wait()
            me.do(v.tensor_scalar(rr[:, :, 0:E1], rr[:, :, 0:E1], 0.5 * FAR, None, ALU.is_gt))
            me.do(v.tensor_tensor(rw[:], re[:], rr[:, :, 0:E1], ALU.mult))
            me.do(v.tensor_reduce(rsm[:, 1, :], rw[:], AX, ALU.add))
            me.do(v.scalar_tensor_tensor(out=rsm[:, 2, :], in0=rsm[:, 3, :], scalar=1e-8, in1=rsm[:, 1, :],
                                         op0=ALU.mult, op1=ALU.add))
            me.do(v.reciprocal(rsm[:, 4, :], rsm[:, 2, :]))
            v.tensor_tensor(rw[:], rw[:], bc(rsm[:, 4, :], E1), ALU.mult).then_inc(s.w_ready, 1)
            weights_parts(E1, [wT1a[0:E1, :], wT1a[E1:2 * E1, :], wT1b[0:E1, :]], 2)
            u0 = 2 * E0
            ffn(u0, None, 8, P)
            with dve.Fori(0, E1 // 4) as i:
                ffn(u0 + 8, i, 4, P)
            dve.wait_ge(s.down_done, primed(2 + 2 * E0 + 8 + E1))
            v.scalar_tensor_tensor(out=xflat, in0=ps[:, 0:4, :].rearrange("p a n -> p (a n)"), scalar=tg[:, 3:4], in1=xflat,
                                   op0=ALU.mult, op1=ALU.add).then_inc(s.x_updated, 1)


def _layout(i):
    import numpy as np
    def rows(v, n=128):
        return np.ascontiguousarray(np.broadcast_to(v, (n,) + v.shape))
    g = lambda n: i["L0_xattn_" + n]
    h = lambda n: i["L1_xattn_" + n]
    f = lambda n: i["L1_ffn_" + n]
    dca = lambda w: w.reshape(-1, 2, 16, 16).transpose(0, 2, 1, 3).reshape(-1, 512)
    tile = lambda w, n: np.tile(w, n)
    main, extra = 13 * 4, 4
    knwb = np.stack([np.concatenate([tile(g("kn_w"), main), tile(g("kn_dca_w"), extra)]),
                     np.concatenate([tile(g("kn_b"), main), tile(g("kn_dca_b"), extra)])])
    new = {
        "gates": rows(np.concatenate([i["g_xattn"], i["g_ffn"]])),
        "Wkv0": np.concatenate([g("Wk"), g("Wv")], axis=1),
        "Wdca0": dca(g("Wkv_dca")),
        "bq0": rows(g("bq")),
        "bkv0": rows(np.stack([np.concatenate([g("bk"), g("bv")]), dca(g("bkv_dca")[None])[0]])),
        "bo0": rows(g("bo")),
        "qnw": rows(np.stack([tile(g("qn_w"), 16), tile(g("qn_b"), 16)])),
        "knwb": rows(knwb),
        "bnd": rows(np.stack([g(n) for n in ("qn_w", "qn_b", "kn_w", "kn_b", "kn_dca_w", "kn_dca_b")])),
        "ctxT": i["ctx_1024"].transpose(0, 2, 1),
        "WrT": f("Wr").T, "rb1": rows(f("router_bias")), "affT": f("affinity").T,
        "te_W1T": f("te_W1").T, "teb1": f("te_b1")[:, None], "te_W2T": f("te_W2").T, "teb2": rows(f("te_b2"), 4),
        "WkT1": h("Wk").reshape(128, 16, 128).transpose(2, 1, 0),
        "WvT1": h("Wv").reshape(128, 16, 128).transpose(2, 1, 0),
        "g1": np.stack([h("gq"), h("gk")], axis=1),
        "g1r": rows(np.stack([h("gq"), h("gk")])),
    }
    for n in ("x", "ctx_1024", "L0_xattn_Wq", "L0_xattn_Wo", "L0_ffn_gate_w", "L0_ffn_w_gate", "L0_ffn_w_up", "L0_ffn_w_down",
              "L1_xattn_Wq", "L1_xattn_Wk", "L1_xattn_Wo", "L1_ffn_Wg", "L1_ffn_Wu", "L1_ffn_Wd", "L1_ffn_Sg", "L1_ffn_Su", "L1_ffn_Sd"):
        new[n] = i[n]
    return {k: np.ascontiguousarray(v) for k, v in new.items()}


def kernel(**inputs):
    import numpy as _np
    import concourse.bacc as _bacc
    from concourse import mybir as _mybir
    from concourse.bass_utils import run_bass_kernel_spmd as _run

    nc = _bacc.Bacc("TRN2", target_bir_lowering=False, num_devices=1)
    laid = _layout({k: _np.asarray(v) for k, v in inputs.items()})
    arrays, args = {}, {}
    for name, v in laid.items():
        arrays[f"in_{name}_dram"] = v
        args[name] = nc.dram_tensor(f"in_{name}_dram", v.shape, _mybir.dt.from_np(v.dtype), kind="ExternalInput").ap()
    out = nc.dram_tensor("out_0_dram", (4, 256, 256), _mybir.dt.float32, kind="ExternalOutput").ap()
    program(nc, args, out)
    r = _run(nc, [arrays], core_ids=[0])
    return r.results[0]["out_0_dram"]
```

```python
from contextlib import ExitStack

import concourse.bass as bass
from concourse import mybir

F32 = mybir.dt.float32
F32R = mybir.dt.float32r
BF16 = mybir.dt.bfloat16
ALU = mybir.AluOpType
ACT = mybir.ActivationFunctionType
AX = mybir.AxisListType.X

P = 128
B, SQ, D = 4, 256, 256
KV, C = 1601, 128
NT = B * SQ // P
KD = D // P
TB = SQ // P
KT = -(-KV // P)
KPAD = KT * P
HALF = 512

H0, D0 = 16, 16
DCA = 16
KMAIN = KV - DCA
KT0 = KT + 1
ROWS0 = [P] * (KT - 1) + [KMAIN - P * (KT - 1), DCA]
COL0 = [P * t for t in range(KT)] + [KMAIN]
HG = 4
NG = H0 // HG
SCALE0 = D0 ** -0.5
E0, I0, TOP0 = 32, 96, 8
CAP = 2 * (B * SQ * TOP0 // E0)
H1, D1 = 16, 128
ROWS1 = [P] * (KT - 1) + [KV - P * (KT - 1)]
BANK1 = [t % 3 for t in range(KT - 1)] + [3]
E1, F1, TOP1, ND = 64, 64, 4, 4
NSH = 2
TOPS = 8
EXP_ROOM = 70.0
FAR = 3.0e38

NAMES = {}


PRIMED = ("probs0 pv0 o0_read misc_read h1_made h_made hs_hi hs_lo down_done k1_reduced k1_squared "
          "probs1 pv1 summed den_made den_read o1_read y1_added scores0 scores1").split()


PRIME = 4


def primed(count):
    return count + PRIME


class Steps:

    def __init__(self, eng, sem):
        self.eng, self.sem, self.n, self.i, self.per = eng, sem, 0, None, 0

    def did(self, ins):
        ins.then_inc(self.sem, 1)
        self.n += 1

    def wait(self):
        self.eng.wait_ge(self.sem, self.n if self.i is None else self.i * self.per + self.n)

    def do(self, ins):
        self.did(ins)
        self.wait()

    def enter(self, i, per):
        self.i, self.per, self.first = i, per, self.n

    def leave(self, rounds):
        assert self.n - self.first == self.per, (self.n - self.first, self.per)
        self.n = self.first + self.per * rounds
        self.i = None


def at(base, i, per, k):
    return base + k if i is None else i * per + (base + k)


PER0 = 45


def program(nc, a, out, stages=4):
    ctx = ExitStack()
    with ctx:
        def sem(name):
            return ctx.enter_context(nc.semaphore(name))

        def sb(name, shape, dt=F32, scope=ctx):
            return scope.enter_context(nc.sbuf_tensor("s_" + name, shape, dt))

        ps = ctx.enter_context(nc.psum_tensor("ps", [P, 8, 512], F32))
        x = sb("x", [P, NT, D])
        xn = sb("xn", [P, NT, D])
        xnT = sb("xnT", [P, KD, NT * P])
        ident = sb("ident", [P, P])
        ones = sb("ones", [P, 8])
        tg = sb("tg", [P, 4])
        bn = sb("bn", [P, NT, 6])
        mv = sb("mv", [P, NT, 2])
        lnv = sb("lnv", [P, NT])
        lnr = sb("lnr", [P, NT])
        sa = ExitStack()
        wq0 = sb("wq0", [P, KD, D], scope=sa)
        wkv0 = sb("wkv0", [P, 2 * D], scope=sa)
        wdca0 = sb("wdca0", [P, 2 * D], scope=sa)
        wo0 = sb("wo0", [P, KD, D], scope=sa)
        bq0 = sb("bq0", [P, D], scope=sa)
        bkv0 = sb("bkv0", [P, 2, 2 * D], scope=sa)
        bo0 = sb("bo0", [P, D], scope=sa)
        qnw = sb("qnw", [P, 2, H0 * D0], scope=sa)
        knwb = sb("knwb", [P, 2, KT0 * HG * D0], scope=sa)
        bnd = sb("bnd", [P, 6, D0], scope=sa)
        bsm = sb("bsm", [P, 32], scope=sa)
        ctxT0 = sb("ctxT0", [P, KV], scope=sa)
        qn = sb("qn", [P, NT, H0, D0], scope=sa)
        qst = sb("qst", [P, TB, HG, 4, D0], scope=sa)
        qg = sb("qg", [P, 2, 2, 2, SQ], F32R, scope=sa)
        kst = sb("kst", [P, KT0 * HG, 4, D0], scope=sa)
        kT0 = sb("kT0", [P, 2, KT0 * 2 * P], F32R, scope=sa)
        vg = sb("vg", [P, 2, KT0, HG, 2 * D0], scope=sa)
        kc = sb("kc", [P, NG, KT0, HG, D0], scope=sa)
        kx = sb("kx", [P, NG, KT0, HG, D0], scope=sa)
        vc = sb("vc", [P, NG, KT0, HG, D0], scope=sa)
        vx = sb("vx", [P, NG, KT0, HG, D0], scope=sa)
        ksq = sb("ksq", [P, KT0 * HG * D0], scope=sa)
        p0 = sb("p0", [P, 2, 4 * SQ], scope=sa)
        s1 = sb("s1", [P, KT0 * H0], scope=sa)
        s2 = sb("s2", [P, KT0 * H0], scope=sa)
        oT0 = qnw
        rd0 = sb("rd0", [P, 4 * HG], scope=sa)
        on0 = sb("on0", [P, 4 * HG, D0], scope=sa)
        sa.close()

        tri = sb("tri", [P, P], BF16)
        onesb = sb("onesb", [P, P], BF16)
        sel1 = sb("sel1", [P, E1, F1], BF16)
        wT1a = sb("wT1a", [P, NT * P], BF16)
        wT1b = sb("wT1b", [P, NT * P], BF16)
        zb = sb("zb", [P, HALF], BF16)
        ones512 = sb("ones512", [1, NT * P], BF16)

        sc = ExitStack()
        sel0 = sb("sel0", [3 * E0, E0, I0], BF16, scope=sc)
        wT0 = sb("wT0", [3 * E0, NT * P], BF16, scope=sc)
        gatew = sb("gatew", [P, KD, E0], scope=sc)
        wr1 = sb("wr1", [P, KD, E1], scope=sc)
        rb1 = sb("rb1", [P, E1], scope=sc)
        aff1 = sb("aff1", [ND, E1], scope=sc)
        te1 = sb("te1", [P, KD, P], scope=sc)
        teb1 = sb("teb1", [P, 1], scope=sc)
        te2 = sb("te2", [P, ND], scope=sc)
        teb2 = sb("teb2", [B, ND], scope=sc)
        xm = sb("xm", [P, KD * B], scope=sc)
        h1t = sb("h1t", [P, B], scope=sc)
        td = sb("td", [B, 4, ND], scope=sc)
        tdT = sb("tdT", [ND, B, P], scope=sc)
        rl = sb("rl", [P, NT, E1 + TOPS - TOP1], scope=sc)
        rr = sb("rr", [P, NT, E1 + TOPS - TOP1], scope=sc)
        re = sb("re", [P, NT, E1], scope=sc)
        rw = sb("rw", [P, NT, E1], scope=sc)
        m8 = sb("m8", [P, NT, TOPS], scope=sc)
        rsm = sb("rsm", [P, 6, NT], scope=sc)
        selb = sb("selb", [P, NT, E0], BF16, scope=sc)
        pre = sb("pre", [P, NT, E0], BF16, scope=sc)
        hi0 = sb("hi0", [E1, NT * P], BF16, scope=sc)
        mid0 = sb("mid0", [E1, NT * P], BF16, scope=sc)
        rem1 = sb("rem1", [E1, NT * P], scope=sc)
        rem2 = sb("rem2", [E1, NT * P], scope=sc)
        wgu = sb("wgu", [P, 2, 2, KD, P], scope=sc)
        wd = sb("wd", [P, 2, D], scope=sc)
        wgus = sb("wgus", [P, 2, 2, 2, KD, P], F32R, scope=sc)
        wds = sb("wds", [P, 2, 2, D], F32R, scope=sc)
        xT = sb("xT", [P, 2, KD, NT * P], F32R, scope=sc)
        sg = sb("sg", [P, HALF], scope=sc)
        hh = sb("hh", [P, HALF], scope=sc)
        hw = sb("hw", [P, 2, HALF], scope=sc)
        hs = sb("hs", [P, 2, 2, HALF], F32R, scope=sc)
        sc.close()

        sw = ExitStack()
        wkv1 = sb("wkv1", [P, H1 * (C + D)], scope=sw)
        sw.close()
        se = ExitStack()
        qq1 = sb("qq1", [P, 2, H1 * SQ], F32R, scope=se)
        wq1 = sb("wq1", [P, KD, H1 * D1], scope=se)
        wk1 = sb("wk1", [P, 2, H1 * D1], F32R, scope=se)
        wkT1 = sb("wkT1", [P, H1, C], scope=se)
        m1 = sb("m1", [P, H1, D], scope=se)
        stage = sb("stage", [P, KV + KT * C], scope=se)
        q1 = stage[:, 0:H1 * D1].rearrange("p (h d) -> p h d", h=H1)
        ctxT1 = sb("ctxT1", [P, 2, KV + 1], F32R, scope=se)
        ctx1 = sb("ctx1", [P, KT, C], scope=se)
        rk1 = sb("rk1", [P, KT, H1], scope=se)
        g1 = sb("g1", [P, 4], scope=se)
        g1r = sb("g1r", [P, 3, D1], scope=se)
        q1T = sb("q1T", [P, H1, P], scope=se)
        rq1 = sb("rq1", [P, 2, H1], scope=se)
        ksq1 = sb("ksq1", [P, 2, HALF], scope=se)
        p1 = sb("p1", [P, 4, 2, SQ], scope=se)
        dsum = sb("dsum", [P, 2 * SQ], scope=se)
        oT1 = sb("oT1", [P, 2 * SQ], scope=se)
        rd1 = sb("rd1", [P, 4], scope=se)
        se.close()
        acc1 = xn
        wvT1 = wkv1[:, 0:H1 * C].rearrange("p (h c) -> p h c", h=H1)
        wo1 = wkv1[:, H1 * C:].rearrange("p (h n) -> p h n", h=H1)

        S = {n: sem(n) for n in (
            "x_loaded gates_loaded w0_loaded small0_loaded ctxT0_loaded experts0_loaded experts1_loaded "
            "router_loaded w1_loaded ctx1_loaded0 ctx1_loaded1 stored "
            "consts_made ident_made dve_steps act_steps pool_steps tanh_made "
            "ln_var ln_std ln_done ln_turned xnT_act xnT_dve "
            "q0_made q0_read q0_var q0_std qst_ready bound_sq bound_root bound0_ready "
            "misc_made misc_read k_centered k_squared k_sq_read k_var k_std k_normed "
            "hi_ready kst_ready vc_ready vg_ready scores0 probs0 pv0 o0_read "
            "ctx_made cx_turned cxT_act y0_made x_updated "
            "logits_made logits_read r_shifted r_exp sel_ready pos_made w_ready w_turned wT_ready "
            "xm_ready te_made te_gelu tl_made tl_shifted tl_exp td_ready td_turned tdT_ready "
            "g_made u_made w_made silu_made h1_made h_made hs_hi hs_lo down_done wslot0 wslot1 w_split xT_hi xT_lo "
            "m1_made m1_read bound1_ready "
            "k1_made k1_squared k1_reduced k1_var k1_std rk1_ready wk_hi wk_lo ctxT_hi ctxT_lo ctx_kept "
            "q1_made q1_read q1_var q1_std q1_normed q1_turned q1T_ready qq_made qq_hi qq_read "
            "scores1 probs1 pv1 summed o1_read den_made den_read y1_made y1_added").split()}
        s = type("Sems", (), S)

        xf = a["x"].rearrange("b s d -> (b s) d").rearrange("(t p) d -> p t d", p=P)
        of = out.rearrange("b s d -> (b s) d").rearrange("(t p) d -> p t d", p=P)

        def act_turn(act, k):
            act.wait_ge(s.ln_var, k + 1)
            nc.scalar.activation(lnr[:], lnv[:], ACT.Sqrt).then_inc(s.ln_std, 1)
            act.wait_ge(s.ln_turned, 16 * (k + 1) - 8)
            for j in range(2):
                nc.scalar.copy(xnT[:, 0, j * HALF:(j + 1) * HALF], ps[:, j, :]).then_inc(s.xnT_act, 1)

        def act_split(act, k):
            for j in range(KD):
                act.wait_ge(s.xnT_dve if j else s.xnT_act, 2 * (k + 1))
                nc.scalar.copy(xT[:, 0, j, :], xnT[:, j, :]).then_inc(s.xT_hi, 1)

        def act_ffn(act, u0, i, units):
            rows = act_rows[0]
            for j in range(units):
                u = at(u0, i, 4, j)
                act.wait_ge(s.g_made, at(u0, i, 4, j + 1))
                act.wait_ge(s.h1_made, primed(u))
                nc.scalar.activation(sg[0:rows, :], ps[0:rows, 4, :], ACT.Silu).then_inc(s.silu_made, 1)
                act.wait_ge(s.h_made, primed(at(u0, i, 4, j + 1)))
                act.wait_ge(s.down_done, primed(at(u0 + (2 if u0 >= 2 * E0 else 1), i, 4, j - 1)))
                nc.scalar.copy(hs[0:rows, j % 2, 0, :], hw[0:rows, j % 2, :]).then_inc(s.hs_hi, 1)

        act_rows = [I0]

        def qq_out(part, j, t):
            return qq1[:, part, :].rearrange("p (h t n) -> p h t n", t=TB, n=P)[:, 4 * j:4 * j + 4, t, :]

        def rk_col(t, hp, j, r):
            return rk1[0:r, t, bass.ds(hp * 2 + j, 1)]

        def pe_turn(pe, k):
            pe.wait_ge(s.ln_done, NT * (k + 1))
            for j in range(4):
                for t in range(4):
                    tt = 4 * (j % 2) + t
                    nc.tensor.transpose(ps[:, j, t * P:(t + 1) * P], xn[:, tt, (j // 2) * P:(j // 2 + 1) * P],
                                        ident[:]).then_inc(s.ln_turned, 1)
            pe.wait_ge(s.xnT_act, 2 * (k + 1))
            pe.wait_ge(s.xnT_dve, 2 * (k + 1))

        def pe_zero(pe):
            for j in range(4):
                ins = nc.tensor.matmul(ps[:, j, :], zb[:, 0:P], zb[:], start=True, stop=False, skip_group_check=True)
            ins.then_inc(s.down_done, 1)

        PRODUCT = ((0, 0), (0, 1), (1, 0))

        def pe_up(pe, u0, i, j, rows, weight, loaded):
            slot, half = j // 2 % 2, j % 2
            n = slice(half * HALF, (half + 1) * HALF)
            if half == 0:
                pe.wait_ge(s.w_split, loaded)
            for g in range(2):
                if g == 0:
                    pe.wait_ge(s.silu_made, at(u0, i, 4, j))
                else:
                    pe.wait_ge(s.h1_made, primed(at(u0, i, 4, j)))
                ops = [(k, w, x_) for k in range(KD) for w, x_ in PRODUCT]
                for c, (k, w, x_) in enumerate(ops):
                    ins = nc.tensor.matmul(ps[0:rows, 4 + g, :], wgus[:, slot, w, g, k, 0:rows], xT[:, x_, k, n],
                                           start=c == 0, stop=c == len(ops) - 1)
                ins.then_inc(s.u_made if g else s.g_made, 1)
            pe.wait_ge(s.h_made, primed(at(u0, i, 4, j)))
            parts = weight(i, j)
            for k, (sel, wt) in enumerate(parts):
                ins = nc.tensor.matmul(ps[0:rows, 6, :], sel, wt[:, n], start=k == 0, stop=k == len(parts) - 1)
            ins.then_inc(s.w_made, 1)

        def pe_down(pe, u0, i, j, rows):
            slot, half = j // 2 % 2, j % 2
            pe.wait_ge(s.hs_lo, primed(at(u0, i, 4, j + 1)))
            for t in range(4):
                tt = half * 4 + t
                for h, w in PRODUCT:
                    ins = nc.tensor.matmul(ps[:, tt // 2, (tt % 2) * D:(tt % 2 + 1) * D],
                                           hs[0:rows, j % 2, h, t * P:(t + 1) * P], wds[0:rows, slot, w, :],
                                           start=False, stop=False, skip_group_check=True)
            ins.then_inc(s.down_done, 1)

        MISC0 = KT0 + 1 + 7
        MISC = [0, KT0 + 9, KT0 + 18, KT0 + 27]
        MISCB = KT0 + 36

        def misc(b, st, k, last=False):
            return b * MISCB + (MISC0 + MISC[st] + k - (KT0 if last and st else 0))

        def parts(ap):
            return ap.unsqueeze(2).to_broadcast([P, ap.shape[1], 2, D0])

        def kgroup(t, g):
            return t[:, g].rearrange("p t h d -> p (t h) d")

        block = ctx.enter_context(nc.Block())
        NW0 = 13

        def store(sp):
            sp.wait_ge(s.x_updated, stages)
            sp.dma_start(of, x[:]).then_inc(s.stored, 16)
            sp.wait_ge(s.stored, 16)

        @block.sync
        def _(sp):
            for name in PRIMED:
                sp.sem_inc(S[name], PRIME)
            sp.dma_start(x[:], xf).then_inc(s.x_loaded, 16)
            sp.dma_start(wq0[:], a["L0_xattn_Wq"].rearrange("(k p) n -> p k n", p=P)).then_inc(s.w0_loaded, 16)
            sp.dma_start(wkv0[:], a["Wkv0"]).then_inc(s.w0_loaded, 16)
            sp.dma_start(wdca0[:], a["Wdca0"]).then_inc(s.w0_loaded, 16)
            sp.dma_start(ctxT0[:], a["ctxT"][0]).then_inc(s.ctxT0_loaded, 16)
            sp.dma_start(wo0[:], a["L0_xattn_Wo"].rearrange("(k p) n -> p k n", p=P)).then_inc(s.w0_loaded, 16)
            for dst, name in ((bq0[:], "bq0"), (bkv0[:], "bkv0"), (bo0[:], "bo0"), (qnw[:], "qnw"),
                              (knwb[:], "knwb"), (bnd[:], "bnd")):
                sp.dma_start(dst, a[name]).then_inc(s.small0_loaded, 16)
            sp.dma_start(tg[:], a["gates"]).then_inc(s.gates_loaded, 16)
            for b in range(1, B):
                sp.wait_ge(s.misc_made, KT0 if b == 1 else misc(b - 2, 0, 1 + KT0))
                sp.dma_start(ctxT0[:], a["ctxT"][b]).then_inc(s.ctxT0_loaded, 16)

            def weights(slot, split, g_src, u_src, d_src, rows):
                if split is not None:
                    sp.wait_ge(s.w_split, split)
                w = s.wslot1 if slot else s.wslot0
                cols = slice(0, rows)
                for j, src in enumerate((g_src, u_src)):
                    sp.dma_start(wgu[:, slot, j, :, cols], src.rearrange("(k p) n -> p k n", p=P)).then_inc(w, 16)
                sp.dma_start(wd[cols, slot, :], d_src).then_inc(w, 16)

            def expert0(e, slot, split):
                weights(slot, split, a["L0_ffn_w_gate"][e], a["L0_ffn_w_up"][e], a["L0_ffn_w_down"][e], I0)

            def load_router():
                for dst, src in ((gatew[:], a["L0_ffn_gate_w"].rearrange("(k p) n -> p k n", p=P)),
                                 (wr1[:], a["WrT"].rearrange("(k p) n -> p k n", p=P)),
                                 (rb1[:], a["rb1"]), (aff1[:], a["affT"]),
                                 (te1[:], a["te_W1T"].rearrange("(k p) n -> p k n", p=P)),
                                 (teb1[:], a["teb1"]), (te2[:], a["te_W2T"]), (teb2[:], a["teb2"])):
                    sp.dma_start(dst, src).then_inc(s.router_loaded, 16)

            if stages < 2:
                return store(sp)
            sp.wait_ge(s.x_updated, 1)
            load_router()
            expert0(0, 0, None)
            expert0(1, 1, None)
            with sp.Fori(1, E0 // 2) as i:
                for slot in range(2):
                    expert0(i * 2 + slot, slot, i * 2 + (slot - 1))

            if stages < 3:
                return store(sp)
            sp.wait_ge(s.x_updated, 2)
            for dst, src in ((stage[:, 0:H1 * D1], a["L1_xattn_Wk"]), (wvT1, a["WvT1"]),
                             (wo1, a["L1_xattn_Wo"].rearrange("(h d) n -> d h n", d=D1)),
                             (wkT1[:], a["WkT1"]),
                             (wq1[:], a["L1_xattn_Wq"].rearrange("(k p) n -> p k n", p=P)),
                             (g1[:, 0:2], a["g1"]), (g1r[:, 0:2, :], a["g1r"])):
                sp.dma_start(dst, src).then_inc(s.w1_loaded, 16)
            for b in range(B):
                if b == 0:
                    sp.wait_ge(s.wk_lo, 1)
                else:
                    sp.wait_ge(s.q1_turned, 4 * TB * b)
                sp.dma_start(stage[:, 0:KV], a["ctxT"][b]).then_inc(s.ctx1_loaded0, 16)
                st = stage[:, KV:].rearrange("p (t c) -> p t c", c=C)
                sp.dma_start(st[:, 0:KT - 1, :],
                             a["ctx_1024"][b, 0:P * (KT - 1), :].rearrange("(t p) c -> p t c", p=P)).then_inc(s.ctx1_loaded1, 16)
                sp.dma_start(st[0:ROWS1[-1], KT - 1, :], a["ctx_1024"][b, P * (KT - 1):KV, :]).then_inc(s.ctx1_loaded1, 16)

            if stages < 4:
                return store(sp)
            sp.wait_ge(s.x_updated, 3)
            load_router()

            def shared(j, slot, split):
                i, cols = j // 2, slice(j % 2 * P, (j % 2 + 1) * P)
                weights(slot, split, a["L1_ffn_Sg"][i, :, cols], a["L1_ffn_Su"][i, :, cols], a["L1_ffn_Sd"][i, cols, :], P)

            def pair1(e, slot, split):
                sp.wait_ge(s.w_split, split)
                w = s.wslot1 if slot else s.wslot0
                for j in range(2):
                    n = slice(j * F1, (j + 1) * F1)
                    for k, name in enumerate(("L1_ffn_Wg", "L1_ffn_Wu")):
                        sp.dma_start(wgu[:, slot, k, :, n], a[name][e * 2 + j].rearrange("(k p) n -> p k n", p=P)).then_inc(w, 16)
                    sp.dma_start(wd[n, slot, :], a["L1_ffn_Wd"][e * 2 + j]).then_inc(w, 16)

            for j in range(2 * NSH):
                shared(j, j % 2, None if j < 2 else E0 + j - 1)
            with sp.Fori(0, E1 // 4) as i:
                for slot in range(2):
                    pair1(i * 2 + slot, slot, i * 2 + (E0 + 2 * NSH + slot - 1))

            store(sp)

        @block.gpsimd
        def _(pool):
            me = Steps(pool, s.pool_steps)
            g_ = nc.gpsimd
            me.do(g_.memset(ident[:], 0.0))
            g_.affine_select(out=ident[:], in_=ident[:], compare_op=ALU.not_equal, fill=1.0, base=0,
                             pattern=[[-1, P]], channel_multiplier=1).then_inc(s.ident_made, 1)
            me.did(g_.memset(ones[:], 1.0))
            me.do(g_.memset(vg[:], 1.0))
            for j in range(2):
                for t in (KT0 - 2, KT0 - 1):
                    me.did(g_.affine_select(out=vg[:, j, t], in_=vg[:, j, t], compare_op=ALU.is_gt, fill=0.0, base=ROWS0[t],
                                            pattern=[[0, HG], [0, 2 * D0]], channel_multiplier=-1))
            me.wait()
            pool.wait_ge(s.small0_loaded, 16 * 6)

            def unit(ap):
                return ones[:, 0:1].unsqueeze(2).unsqueeze(3).to_broadcast(list(ap.shape))

            def keys_hi(g, normed, kst_free):
                pool.wait_ge(s.k_normed, normed)
                flat = kc[:, g].rearrange("p t h d -> p (t h d)")
                me.do(g_.tensor_tensor(flat, flat, knwb[:, 0, :], ALU.mult))
                if kst_free is not None:
                    pool.wait_ge(s.misc_made, kst_free)
                bias = knwb[:, 1, :].rearrange("p (r d) -> p r d", d=D0)
                me.do(g_.tensor_tensor(kst[:, :, 0:2, :].bitcast(F32R), parts(kgroup(kc, g)), parts(bias), ALU.add))
                g_.tensor_tensor(flat, flat, knwb[:, 1, :], ALU.add).then_inc(s.hi_ready, 1)

            def values_group(g, slot, pv, copied):
                pool.wait_ge(s.vc_ready, copied)
                if pv is not None:
                    pool.wait_ge(s.pv0, primed(pv))
                g_.tensor_tensor(vg[:, slot, :, :, 0:D0], vc[:, g], unit(vc[:, g]), ALU.mult).then_inc(s.vg_ready, 1)

            def take_values(g, read):
                pool.wait_ge(s.misc_read, primed(read))
                g_.tensor_tensor(vc[:, g], vx[:, g], unit(vx[:, g]), ALU.mult).then_inc(s.vc_ready, 1)

            for g in range(NG):
                take_values(g, KT0)
            keys_hi(0, 1, None)
            values_group(0, 0, None, 4)

            def step(b, st, last):
                if st < 3:
                    keys_hi(st + 1, b * 4 + (st + 2), misc(b, 0, 0) if st == 0 else misc(b, st - 1, (KT0 if st == 1 and not last else 0) + 8, last))
                    values_group(st + 1, (st + 1) % 2, b * (4 * KT0) + st * KT0, b * 4 + 4)
                    if st == 2 and not last:
                        pool.wait_ge(s.vg_ready, b * 4 + 4)
                        for g in range(NG):
                            take_values(g, misc(b, 0, 1 + KT0))
                elif not last:
                    keys_hi(0, b * 4 + 5, misc(b, 2, 8))
                    values_group(0, 0, b * (4 * KT0) + 3 * KT0, b * 4 + 8)

            with pool.Fori(0, B - 1) as b:
                me.enter(b, 8)
                for st in range(NG):
                    step(b, st, False)
                me.leave(B - 1)
            for st in range(NG):
                step(B - 1, st, True)

            pool.wait_ge(s.x_updated, 1)
            me.did(g_.memset(tri[:], 1.0))
            me.did(g_.memset(sel0[:], 0.0))
            me.do(g_.memset(sel1[:], 0.0))
            g_.affine_select(out=tri[:], in_=tri[:], compare_op=ALU.is_gt, fill=0.0, base=0,
                             pattern=[[1, P]], channel_multiplier=-1).then_inc(s.consts_made, 1)
            g_.memset(onesb[:], 1.0).then_inc(s.consts_made, 1)
            g_.memset(ones512[:], 1.0).then_inc(s.consts_made, 1)
            g_.memset(zb[:], 0.0).then_inc(s.consts_made, 1)
            g_.memset(wT1b[:], 0.0).then_inc(s.consts_made, 1)
            for j in range(3):
                me.do(g_.affine_select(out=sel0[:], in_=sel0[:], compare_op=ALU.not_equal, fill=1.0, base=-j * E0,
                                       pattern=[[-1, E0], [0, I0]], channel_multiplier=1))
            for j in range(2):
                me.do(g_.affine_select(out=sel1[:], in_=sel1[:], compare_op=ALU.not_equal, fill=1.0, base=-j * E1,
                                       pattern=[[-1, E1], [0, F1]], channel_multiplier=1))
            g_.memset(onesb[0:1, 0:1], 1.0).then_inc(s.consts_made, 1)

            def stream_rest(k):
                pool.wait_ge(s.xT_hi, KD * k)
                g_.tensor_tensor(xT[:, 1], xnT[:], xT[:, 0].bitcast(F32), ALU.subtract).then_inc(s.xT_lo, 1)

            def split_weights(slot, loaded, free, rows):
                pool.wait_ge(s.wslot1 if slot else s.wslot0, loaded)
                if free is not None:
                    pool.wait_ge(s.down_done, primed(free))
                cols = slice(0, rows)
                gu = wgu[:, slot].rearrange("p g k n -> p (g k) n")[:, :, cols]
                gus = [wgus[:, slot, part].rearrange("p g k n -> p (g k) n")[:, :, cols] for part in range(2)]
                d, ds = wd[cols, slot, :], [wds[cols, slot, part, :] for part in range(2)]
                me.did(g_.tensor_tensor(gus[0], gu, ones[:, 0:1].unsqueeze(2).to_broadcast(list(gu.shape)), ALU.mult))
                me.do(g_.tensor_tensor(ds[0], d, ones[cols, 0:1].to_broadcast(list(d.shape)), ALU.mult))
                me.did(g_.tensor_tensor(gus[1], gu, gus[0].bitcast(F32), ALU.subtract))
                g_.tensor_tensor(ds[1], d, ds[0].bitcast(F32), ALU.subtract).then_inc(s.w_split, 1)

            if stages < 2:
                return
            for e in range(2):
                split_weights(e, 48, None, I0)
                if e == 0:
                    stream_rest(1)
            with pool.Fori(1, E0 // 2) as i:
                me.enter(i - 1, 6)
                for slot in range(2):
                    split_weights(slot, i * 48 + 48, i * 4 + (2 * slot - 1), I0)
                me.leave(E0 // 2 - 1)
            if stages < 4:
                return
            base, m0 = 48 * E0 // 2, 2 + 2 * E0
            for j in range(2 * NSH):
                split_weights(j % 2, base + 48 * (j // 2 + 1), None if j < 2 else m0 + 2 * (j - 1), P)
                if j == 0:
                    stream_rest(2)
            with pool.Fori(0, E1 // 4) as i:
                me.enter(i, 6)
                for slot in range(2):
                    split_weights(slot, i * 96 + (base + 96 + 96), i * 4 + (m0 + 2 * (2 * NSH + slot - 1)), P)
                me.leave(E1 // 4)

        @block.scalar
        def _(act):
            act.wait_ge(s.gates_loaded, 16)
            nc.scalar.activation(tg[:], tg[:], ACT.Tanh).then_inc(s.tanh_made, 1)
            act.wait_ge(s.bound_sq, 1)
            nc.scalar.activation(bsm[:, 6:12], bsm[:, 0:6], ACT.Sqrt).then_inc(s.bound_root, 1)
            act_turn(act, 0)
            act.wait_ge(s.q0_var, 1)
            nc.scalar.activation(s1[:, 0:NT * H0], s1[:, 0:NT * H0], ACT.Sqrt).then_inc(s.q0_std, 1)

            def square_keys(g, k):
                act.wait_ge(s.k_centered, k + 1)
                act.wait_ge(s.k_sq_read, k * 4 + g)
                nc.scalar.activation(ksq[:], kx[:, g].rearrange("p t h d -> p (t h d)"), ACT.Square).then_inc(s.k_squared, 1)

            def key_std(k):
                act.wait_ge(s.k_var, k + 1)
                nc.scalar.activation(s2[:], s2[:], ACT.Sqrt).then_inc(s.k_std, 1)

            for g in range(NG):
                square_keys(g, 0)
            key_std(0)
            act.wait_ge(s.bound0_ready, 1)

            def act_step(b, st, last):
                for t in range(KT0):
                    n = st * KT0 + t
                    act.wait_ge(s.scores0, primed(b * (NG * KT0) + (n + 1)))
                    act.wait_ge(s.pv0, primed(b * (NG * KT0) + (n - 1)))
                    r, dca = ROWS0[t], t == KT0 - 1
                    nc.scalar.activation(p0[0:r, t % 2, :],
                                         ps[0:r, 2 * (t % 2):2 * (t % 2) + 2, :].rearrange("p a n -> p (a n)"),
                                         ACT.Exp, bias=bsm[0:r, 24 + dca:25 + dca], scale=SCALE0).then_inc(s.probs0, 1)
                    if st == 2 and not last:
                        if 3 <= t < 3 + NG:
                            square_keys(t - 3, b + 1)
                        if t == 9:
                            key_std(b + 1)

            with act.Fori(0, B - 1) as b:
                for st in range(NG):
                    act_step(b, st, False)
            for st in range(NG):
                act_step(B - 1, st, True)
            act.wait_ge(s.cx_turned, 16)
            for j in range(4):
                nc.scalar.copy(xnT[:, j // 2, (j % 2) * HALF:(j % 2 + 1) * HALF], ps[:, j, :]).then_inc(s.cxT_act, 1)
            if stages < 2:
                return
            act_turn(act, 1)
            act_split(act, 1)
            act.wait_ge(s.r_shifted, 1)
            nc.scalar.activation(re[:, :, 0:E0], rl[:, :, 0:E0], ACT.Exp).then_inc(s.r_exp, 1)
            act_rows[0] = I0
            with act.Fori(0, E0 // 2) as i:
                act_ffn(act, 0, i, 4)
            if stages < 3:
                return
            act_turn(act, 2)
            act.wait_ge(s.w1_loaded, 16 * 7)
            nc.scalar.copy(wk1[:, 0, :], stage[:, 0:H1 * D1]).then_inc(s.wk_hi, 1)
            for b in range(B):
                act.wait_ge(s.ctx1_loaded0, 16 * (b + 1))
                act.wait_ge(s.scores1, primed(KT * 8 * b))
                nc.scalar.copy(ctxT1[:, 0, 0:KV], stage[:, 0:KV]).then_inc(s.ctxT_hi, 1)
                act.wait_ge(s.ctx1_loaded1, 32 * (b + 1))
                act.wait_ge(s.pv1, primed(KT * 8 * b))
                st = stage[:, KV:].rearrange("p (t c) -> p t c", c=C)
                nc.scalar.copy(ctx1[:, 0:KT - 1, :], st[:, 0:KT - 1, :]).then_inc(s.ctx_kept, 1)
                nc.scalar.copy(ctx1[0:ROWS1[-1], KT - 1, :], st[0:ROWS1[-1], KT - 1, :]).then_inc(s.ctx_kept, 1)
                for t in range(TB):
                    tt = TB * b + t
                    act.wait_ge(s.q1_made, tt + 1)
                    q = ps[:, 4:8, :].rearrange("p a n -> p (a n)")
                    if t == 0:
                        act.wait_ge(s.ctxT_lo, b + 1)
                        act.wait_ge(s.ctx_kept, 2 * (b + 1))
                    nc.scalar.copy(q1.rearrange("p h d -> p (h d)"), q).then_inc(s.q1_read, 1)
                    act.wait_ge(s.qq_made, 4 * tt)
                    nc.scalar.activation(q1T[:].rearrange("p h n -> p (h n)"), q, ACT.Square).then_inc(s.q1_read, 1)
                    act.wait_ge(s.q1_var, tt + 1)
                    nc.scalar.activation(rq1[:, 0, :], rq1[:, 0, :], ACT.Sqrt).then_inc(s.q1_std, 1)
                    with act.Fori(0, 2) as i:
                        for u in range(KT):
                            k = 2 * KT * tt
                            act.wait_ge(s.k1_made, at(k, i, KT, u + 1))
                            act.wait_ge(s.k1_reduced, primed(at(k, i, KT, max(u - 1, 0))))
                            r = ROWS1[u]
                            nc.scalar.activation(ksq1[0:r, u % 2, :], ps[0:r, u % 4, :], ACT.Square).then_inc(s.k1_squared, 1)
                    for j in range(4):
                        act.wait_ge(s.qq_made, 4 * tt + j + 1)
                        nc.scalar.copy(qq_out(0, j, t), ps[:, 4 + j, :].rearrange("p (h n) -> p h n", h=4)).then_inc(s.qq_hi, 1)
                act.wait_ge(s.k1_var, b + 1)
                nc.scalar.activation(rk1[:], rk1[:], ACT.Sqrt).then_inc(s.k1_std, 1)
                act.wait_ge(s.rk1_ready, b + 1)
                act.wait_ge(s.bound1_ready, 1)
                nc.scalar.activation(rq1[0:1, 1, 0:1], ones[0:1, 0:1], ACT.Exp).then_inc(s.act_steps, 1)
                with act.Fori(0, H1 // 2) as hp:
                    k = KT * 8 * b

                    for t in range(KT):
                        act.wait_ge(s.scores1, primed(at(k, hp, KT, t + 1)))
                        act.wait_ge(s.pv1, primed(at(k, hp, KT, t - 2 if t >= 3 else t - 3)))
                        act.wait_ge(s.summed, primed(at(k, hp, KT, t - 2 if t >= 3 else t - 3)))
                        r = ROWS1[t]
                        for j in range(2):
                            ins = nc.scalar.activation(p1[0:r, BANK1[t], j, :], ps[0:r, BANK1[t], j * SQ:(j + 1) * SQ], ACT.Exp,
                                                       bias=g1[0:r, 3:4], scale=rk_col(t, hp, j, r))
                        ins.then_inc(s.probs1, 1)
            if stages < 4:
                return
            act_turn(act, 3)
            act_split(act, 3)
            act.wait_ge(s.te_made, 1)
            nc.scalar.activation(h1t[:], ps[:, 6, 0:B], ACT.Gelu, bias=teb1[:, 0:1]).then_inc(s.te_gelu, 1)
            act.wait_ge(s.tl_shifted, 1)
            nc.scalar.activation(td[:, 1, :], td[:, 0, :], ACT.Exp).then_inc(s.tl_exp, 1)
            act.wait_ge(s.r_shifted, 2)
            nc.scalar.activation(re[:], rl[:, :, 0:E1], ACT.Exp).then_inc(s.r_exp, 1)
            act_rows[0] = P
            u0 = 2 * E0
            act_ffn(act, u0, None, 8)
            with act.Fori(0, E1 // 4) as i:
                act_ffn(act, u0 + 8, i, 4)

        @block.tensor
        def _(pe):
            pe.wait_ge(s.ident_made, 1)
            pe_turn(pe, 0)
            pe.wait_ge(s.w0_loaded, 16 * 4)

            def bank_free(m):
                pe.wait_ge(s.misc_read, primed(m - 1))

            def project(t, m, par, loaded):
                if t == 0:
                    pe.wait_ge(s.ctxT0_loaded, loaded)
                bank_free(m)
                nc.tensor.matmul(ps[0:ROWS0[t], 6 + par, :], ctxT0[:, COL0[t]:COL0[t] + ROWS0[t]],
                                 (wdca0 if t == KT0 - 1 else wkv0)[:], start=True, stop=True).then_inc(s.misc_made, 1)

            pe.wait_ge(s.small0_loaded, 16 * 6)
            for t in range(KT0):
                project(t, t, t % 2, 16)
            pe.wait_ge(s.misc_read, primed(KT0))
            for t in range(NT):
                for k in range(KD):
                    ins = nc.tensor.matmul(ps[:, 4 + t // 2, (t % 2) * D:(t % 2 + 1) * D], xnT[:, k, t * P:(t + 1) * P],
                                           wq0[:, k, :], start=k == 0, stop=k == KD - 1)
                if t % 2:
                    ins.then_inc(s.q0_made, 1)
            def turn_queries(m, par, ready):
                pe.wait_ge(s.qst_ready, ready)
                bank_free(m)
                for k in range(4):
                    ins = nc.tensor.transpose(ps[:, 6 + par, k * P:(k + 1) * P],
                                              qst[:, k % 2, k // 2 * 2:k // 2 * 2 + 2, :, :].rearrange("p h r d -> p (h r d)"), ident[:])
                ins.then_inc(s.misc_made, 1)

            def turn_keys(j, m, par, ready):
                if j == 0:
                    pe.wait_ge(s.kst_ready, ready)
                bank_free(m)
                for k in range(4):
                    row = (2 * j + k // 2) * HG + 2 * (k % 2)
                    ins = nc.tensor.transpose(ps[:, 6 + par, k * P:(k + 1) * P],
                                              kst[:, row:row + 2, :, :].rearrange("p h r d -> p (h r d)"), ident[:])
                ins.then_inc(s.misc_made, 1)

            def turn_sums(m, par, read):
                pe.wait_ge(s.o0_read, primed(read))
                bank_free(m)
                for k in range(4):
                    ins = nc.tensor.transpose(ps[:, 6 + par, k * P:(k + 1) * P], oT0[:, k // 2, (k % 2) * P:(k % 2 + 1) * P], ident[:])
                ins.then_inc(s.misc_made, 1)

            def scores(b, st, t, ready=None):
                slot = st % 2
                if t or st or not isinstance(b, int) or b:
                    pe.wait_ge(s.probs0, primed(b * (NG * KT0) + (st * KT0 + t - 1)))
                if t == 0:
                    pe.wait_ge(s.misc_read, primed(ready))
                for hp in range(2):
                    c = (2 * t + hp) * P
                    ins = nc.tensor.matmul(ps[0:ROWS0[t], 2 * (t % 2) + hp, :], kT0[:, slot, c:c + ROWS0[t]],
                                           qg[:, slot, hp, :, :].rearrange("p a n -> p (a n)"), start=True, stop=True)
                ins.then_inc(s.scores0, 1)

            def values(b, st, t):
                slot = st % 2
                pe.wait_ge(s.probs0, primed(b * (NG * KT0) + (st * KT0 + t + 1)))
                if t == 0:
                    pe.wait_ge(s.o0_read, primed(b * NG + st))
                    pe.wait_ge(s.vg_ready, b * NG + (st + 1))
                dca = t == KT0 - 1
                for h in range(HG):
                    ins = nc.tensor.matmul(ps[32 * h:32 * h + 32, 5 if dca else 4, 0:SQ], vg[:, slot, t, h, :],
                                           p0[:, t % 2, h * SQ:(h + 1) * SQ], start=t == 0 or dca,
                                           stop=t >= KT0 - 2, skip_group_check=True)
                ins.then_inc(s.pv0, 1)

            def pe_step(b, st, last):
                over = last and st == NG - 1
                nkv = KT0 if st == 0 and not last else 0
                for t in range(KT0):
                    if t + 1 < KT0:
                        scores(b, st, t + 1)
                    if t == (1 if st == 0 else 2) and not over:
                        turn_queries(misc(b, st, 0, last), (MISC0 + MISC[st]) % 2, b * NG + (st + 2))
                    if st == 0 and 1 <= t <= 7 and not last:
                        for tt in (2 * t - 2, 2 * t - 1):
                            project(tt, misc(b, 0, 1 + tt), (MISC0 + 1 + tt) % 2, b * 16 + 32)
                    for j in range(max(2 * (t - 10), 0), min(2 * (t - 9), 7) if not over else 0):
                        turn_keys(j, misc(b, st, 1 + nkv + j, last), (MISC0 + MISC[st] + 1 + nkv + j) % 2, b * NG + (st + 2))
                    values(b, st, t)
                if not over:
                    ready = misc(b, st, 8 + nkv, last)
                    if st < NG - 1:
                        scores(b, st + 1, 0, ready)
                    else:
                        scores(b + 1, 0, 0, ready)
                k = 0 if over else 8 + nkv
                turn_sums(misc(b, st, k, last), (MISC0 + MISC[st] + k) % 2, b * NG + (st + 1))

            pe.wait_ge(s.q0_read, 4)
            turn_queries(KT0, KT0 % 2, 1)
            for j in range(7):
                turn_keys(j, KT0 + 1 + j, (KT0 + 1 + j) % 2, 1)
            scores(0, 0, 0, MISC0)
            with pe.Fori(0, B - 1) as b:
                for st in range(NG):
                    pe_step(b, st, False)
            for st in range(NG):
                pe_step(B - 1, st, True)
            pe.wait_ge(s.ctx_made, NG * B)
            for j in range(4):
                for t in range(4):
                    tt = 4 * (j % 2) + t
                    nc.tensor.transpose(ps[:, j, t * P:(t + 1) * P], xn[:, tt, (j // 2) * P:(j // 2 + 1) * P],
                                        ident[:]).then_inc(s.cx_turned, 1)
            pe.wait_ge(s.cxT_act, 4)
            for t in range(NT):
                for k in range(KD):
                    ins = nc.tensor.matmul(ps[:, t // 2, (t % 2) * D:(t % 2 + 1) * D], xnT[:, k, t * P:(t + 1) * P],
                                           wo0[:, k, :], start=k == 0, stop=k == KD - 1)
            ins.then_inc(s.y0_made, 1)
            if stages < 2:
                return

            pe_turn(pe, 1)
            pe.wait_ge(s.consts_made, 6)
            pe.wait_ge(s.router_loaded, 16 * 8)
            for t in range(NT):
                for k in range(KD):
                    ins = nc.tensor.matmul(ps[:, 7, t * E0:(t + 1) * E0], xnT[:, k, t * P:(t + 1) * P], gatew[:, k, :],
                                           start=k == 0, stop=k == KD - 1)
            ins.then_inc(s.logits_made, 1)
            pe.wait_ge(s.sel_ready, 1)
            for t in range(NT):
                nc.tensor.matmul(ps[:, 7, t * E0:(t + 1) * E0], tri[:], selb[:, t, :], start=True, stop=False)
                ins = nc.tensor.matmul(ps[:, 7, t * E0:(t + 1) * E0], onesb[:], pre[:, t, :], start=False, stop=True)
            ins.then_inc(s.pos_made, 1)
            pe.wait_ge(s.w_ready, 1)
            for t in range(NT):
                ins = nc.tensor.transpose(ps[0:E0, 4 + t // 4, (t % 4) * P:(t % 4 + 1) * P], rw[:, t, 0:E0], ident[:])
            ins.then_inc(s.w_turned, 1)
            pe.wait_ge(s.wT_ready, 1)
            pe_zero(pe)

            def weight0(i, j):
                e = i * 2 + j // 2
                return [(sel0[:, bass.ds(e, 1), :].rearrange("p e n -> p (e n)"), wT0)]

            pe.wait_ge(s.xT_lo, 1)
            pe_up(pe, 0, 0, 0, I0, weight0, 1)
            last = E0 // 2 - 1
            with pe.Fori(0, last) as i:
                for j in range(4):
                    if j < 3:
                        pe_up(pe, 0, i, j + 1, I0, weight0, i * 2 + ((j + 1) // 2 + 1))
                    else:
                        i1 = i + 1
                        pe_up(pe, 0, i1, 0, I0, weight0, i1 * 2 + 1)
                    pe_down(pe, 0, i, j, I0)
            for j in range(4):
                if j < 3:
                    pe_up(pe, 4 * last, None, j + 1, I0, lambda _, jj: weight0(last, jj), 2 * last + (j + 1) // 2 + 1)
                pe_down(pe, 4 * last, None, j, I0)
            if stages < 3:
                return

            pe_turn(pe, 2)
            pe.wait_ge(s.w1_loaded, 16 * 7)
            for h in range(H1):
                if h >= 8 and h % 2 == 0:
                    pe.wait_ge(s.m1_read, h // 2 - 3)
                ins = nc.tensor.matmul(ps[:, 4 + h // 2 % 4, (h % 2) * D:(h % 2 + 1) * D], wvT1[:, h, :], wo1[:, h, :],
                                       start=True, stop=True)
                if h % 2:
                    ins.then_inc(s.m1_made, 1)
            pe.wait_ge(s.m1_read, 8)
            pe.wait_ge(s.wk_lo, 1)

            def product(out, lhs, rhs, first=True, last=True):
                for n, (x_, y_) in enumerate(((0, 0), (0, 1), (1, 0))):
                    ins = nc.tensor.matmul(out, lhs(x_), rhs(y_), start=first and n == 0, stop=last and n == 2)
                return ins

            for b in range(B):
                def ctx_cols(t):
                    return lambda part: ctxT1[:, part, t * P:t * P + ROWS1[t]]

                for t in range(TB):
                    tt = TB * b + t
                    if b and t == 0:
                        pe.wait_ge(s.y1_added, primed(8 * b))
                        pe.wait_ge(s.o1_read, primed(8 * b))
                    if t:
                        pe.wait_ge(s.qq_read, 4 * tt)
                    for j in range(4):
                        for k in range(KD):
                            ins = nc.tensor.matmul(ps[:, 4 + j, :], xnT[:, k, tt * P:(tt + 1) * P], wq1[:, k, j * 512:(j + 1) * 512],
                                                   start=k == 0, stop=k == KD - 1)
                    ins.then_inc(s.q1_made, 1)
                    pe.wait_ge(s.ctxT_lo, b + 1)
                    if t == 0:
                        pe.wait_ge(s.probs1, primed(KT * 8 * b))
                    with pe.Fori(0, 2) as i:
                        for u in range(KT):
                            pe.wait_ge(s.k1_squared, primed(at(2 * KT * tt, i, KT, max(u - 3, 0))))
                            product(ps[0:ROWS1[u], u % 4, :], ctx_cols(u),
                                    lambda part: wk1[:, part, bass.ds(i * 512 + t * 1024, 512)]).then_inc(s.k1_made, 1)
                    pe.wait_ge(s.q1_normed, tt + 1)
                    for j in range(4):
                        for h in range(4):
                            ins = nc.tensor.transpose(ps[:, 4 + j, h * P:(h + 1) * P], q1[:, 4 * j + h, :], ident[:])
                        ins.then_inc(s.q1_turned, 1)
                    for j in range(4):
                        pe.wait_ge(s.q1T_ready, 4 * tt + j + 1)
                        for h in range(4):
                            ins = nc.tensor.matmul(ps[:, 4 + j, h * P:(h + 1) * P], wkT1[:, 4 * j + h, :], q1T[:, 4 * j + h, :],
                                                   start=True, stop=True)
                        ins.then_inc(s.qq_made, 1)
                pe.wait_ge(s.k1_squared, primed(4 * KT * (b + 1)))
                pe.wait_ge(s.qq_read, 4 * TB * (b + 1))
                pe.wait_ge(s.ctx_kept, 2 * (b + 1))
                k0 = KT * 8 * b

                def scores1(hp, t):
                    if t < KT - 1:
                        pe.wait_ge(s.probs1, primed(hp * KT + (k0 + (t - 2 if t >= 3 else t - 3))))
                    product(ps[0:ROWS1[t], BANK1[t], :], ctx_cols(t),
                            lambda part: qq1[:, part, bass.ds(hp * (2 * SQ), 2 * SQ)]).then_inc(s.scores1, 1)

                def pair(hp, following):
                    for t in range(KT):
                        if t + 2 < KT:
                            scores1(hp, t + 2)
                        if t == 0:
                            pe.wait_ge(s.o1_read, primed(hp + 8 * b))
                        pe.wait_ge(s.probs1, primed(hp * KT + (k0 + t + 1)))
                        nc.tensor.matmul(ps[:, 4, :], ctx1[0:ROWS1[t], t, :],
                                         p1[0:ROWS1[t], BANK1[t], :, :].rearrange("p a n -> p (a n)"),
                                         start=t == 0, stop=t == KT - 1).then_inc(s.pv1, 1)
                    if following:
                        scores1(hp + 1, 0)
                        scores1(hp + 1, 1)
                    pe.wait_ge(s.summed, primed(hp * KT + (k0 + KT)))
                    pe.wait_ge(s.den_read, primed(hp + 8 * b))
                    for j in range(4):
                        ins = nc.tensor.matmul(ps[:, 7, j:j + 1], dsum[:, j * P:(j + 1) * P], ones[:, 0:1], start=True, stop=True)
                    ins.then_inc(s.den_made, 1)
                    pe.wait_ge(s.o1_read, primed(hp + (8 * b + 1)))
                    pe.wait_ge(s.y1_added, primed(hp + 8 * b))
                    for j in range(4):
                        ins = nc.tensor.matmul(ps[:, 5 + j // 2, (j % 2) * D:(j % 2 + 1) * D], oT1[:, j * P:(j + 1) * P],
                                               m1[:].rearrange("p h n -> p (h n)")[:, bass.ds(hp * (2 * D) + (j // 2) * D, D)],
                                               start=True, stop=True)
                    ins.then_inc(s.y1_made, 1)

                scores1(0, 0)
                scores1(0, 1)
                with pe.Fori(0, H1 // 2 - 1) as hp:
                    pair(hp, True)
                pair(H1 // 2 - 1, False)
            if stages < 4:
                return

            pe_turn(pe, 3)
            pe.wait_ge(s.router_loaded, 16 * 16)
            pe.wait_ge(s.xm_ready, 1)
            for k in range(KD):
                ins = nc.tensor.matmul(ps[:, 6, 0:B], te1[:, k, :], xm[:, k * B:(k + 1) * B], start=k == 0, stop=k == KD - 1)
            ins.then_inc(s.te_made, 1)
            pe.wait_ge(s.te_gelu, 1)
            nc.tensor.matmul(ps[0:B, 6, 0:ND], h1t[:], te2[:], start=True, stop=True).then_inc(s.tl_made, 1)
            pe.wait_ge(s.td_ready, 1)
            nc.tensor.transpose(ps[0:ND, 6, 0:B], td[:, 3, :], ident[0:B, 0:B]).then_inc(s.td_turned, 1)
            pe.wait_ge(s.tdT_ready, 1)
            for t in range(NT):
                for k in range(KD):
                    nc.tensor.matmul(ps[:, 7, t * E1:(t + 1) * E1], xnT[:, k, t * P:(t + 1) * P], wr1[:, k, :],
                                     start=k == 0, stop=False)
                ins = nc.tensor.matmul(ps[:, 7, t * E1:(t + 1) * E1], tdT[:, t // TB, :], aff1[:], start=False, stop=True)
            ins.then_inc(s.logits_made, 1)
            pe.wait_ge(s.w_ready, 2)
            for t in range(NT):
                ins = nc.tensor.transpose(ps[0:E1, 4 + t // 4, (t % 4) * P:(t % 4 + 1) * P], rw[:, t, :], ident[:])
            ins.then_inc(s.w_turned, 1)
            pe.wait_ge(s.wT_ready, 2)
            pe_zero(pe)
            u0 = 2 * E0

            def weight_one(i, j):
                return [(onesb[0:1, :], ones512)]

            def weight1(i, j):
                e = i * 4 + j // 2 * 2
                sel = sel1[:].rearrange("p e n -> p (e n)")[:, bass.ds(e * F1, 2 * F1)]
                return [(sel, wT1a), (sel, wT1b)]

            pe.wait_ge(s.xT_lo, 2)
            pe_up(pe, u0, None, 0, P, weight_one, E0 + 1)
            for j in range(8):
                if j < 7:
                    pe_up(pe, u0, None, j + 1, P, weight_one, E0 + (j + 1) // 2 + 1)
                else:
                    pe_up(pe, u0 + 8, None, 0, P, lambda i, jj: weight1(0, jj), E0 + 2 * NSH + 1)
                pe_down(pe, u0, None, j, P)
            last = E1 // 4 - 1
            with pe.Fori(0, last) as i:
                for j in range(4):
                    if j < 3:
                        pe_up(pe, u0 + 8, i, j + 1, P, weight1, i * 2 + (E0 + 2 * NSH + (j + 1) // 2 + 1))
                    else:
                        i1 = i + 1
                        pe_up(pe, u0 + 8, i1, 0, P, weight1, i1 * 2 + (E0 + 2 * NSH + 1))
                    pe_down(pe, u0 + 8, i, j, P)
            for j in range(4):
                if j < 3:
                    pe_up(pe, u0 + 8 + 4 * last, None, j + 1, P, lambda _, jj: weight1(last, jj), 2 * last + (E0 + 2 * NSH + (j + 1) // 2 + 1))
                pe_down(pe, u0 + 8 + 4 * last, None, j, P)


        @block.vector
        def _(dve):
            v = nc.vector
            me = Steps(dve, s.dve_steps)

            def norm(k):
                for t in range(NT):
                    me.did(v.bn_stats(bn[:, t, :], x[:, t, :]))
                me.wait()
                for t in range(NT):
                    me.did(v.bn_aggr(mv[:, t, :], bn[:, t, :]))
                me.wait()
                v.tensor_scalar(lnv[:], mv[:, :, 1], 1e-5, None, ALU.add).then_inc(s.ln_var, 1)
                dve.wait_ge(s.ln_std, k + 1)
                me.do(v.reciprocal(lnv[:], lnr[:]))
                for t in range(NT):
                    v.tensor_scalar(xn[:, t, :], x[:, t, :], mv[:, t, 0:1], lnv[:, t:t + 1],
                                    ALU.subtract, ALU.mult).then_inc(s.ln_done, 1)
                dve.wait_ge(s.ln_turned, 16 * (k + 1))
                for j in range(2):
                    v.tensor_copy(xnT[:, 1, j * HALF:(j + 1) * HALF], ps[:, 2 + j, :]).then_inc(s.xnT_dve, 1)

            def bc(ap, n):
                return ap.unsqueeze(2).to_broadcast([ap.shape[0], ap.shape[1], n])

            def read_projected(t, m, par):
                dve.wait_ge(s.misc_made, m + 1)
                r, dca = ROWS0[t], t == KT0 - 1
                pv = ps[0:r, 6 + par, :].rearrange("p (g h two d) -> p g h two d", g=NG, h=HG, two=2)
                bv = bkv0[0:r, int(dca), :].rearrange("p (g h two d) -> p g h two d", g=NG, h=HG, two=2)
                me.did(v.tensor_tensor(kx[0:r, :, t], pv[:, :, :, 0, :], bv[:, :, :, 0, :], ALU.add))
                v.tensor_tensor(vx[0:r, :, t], pv[:, :, :, 1, :], bv[:, :, :, 1, :], ALU.add).then_inc(s.misc_read, 1)

            me.did(v.memset(kx[:, :, KT0 - 2:KT0], 0.0))
            me.did(v.memset(vx[:, :, KT0 - 2:KT0], 0.0))
            me.did(v.memset(qg[:].bitcast(F32), 0.0))
            dve.wait_ge(s.x_loaded, 16)
            dve.wait_ge(s.small0_loaded, 96)
            me.do(v.tensor_tensor(on0[:, 0:6, :], bnd[:], bnd[:], ALU.mult))
            v.tensor_reduce(bsm[:, 0:6], on0[:, 0:6, :], AX, ALU.add).then_inc(s.bound_sq, 1)
            me.do(v.tensor_reduce(bsm[:, 12:18], bnd[:], AX, ALU.max, apply_absolute_value=True))
            dve.wait_ge(s.bound_root, 1)
            pair = bsm[:, 12:18].rearrange("p (n two) -> p n two", two=2)
            root = bsm[:, 6:12].rearrange("p (n two) -> p n two", two=2)
            me.do(v.scalar_tensor_tensor(out=bsm[:, 18:21], in0=pair[:, :, 0], scalar=float(D0) ** 0.5, in1=root[:, :, 1],
                                         op0=ALU.mult, op1=ALU.add))
            me.do(v.tensor_scalar(bsm[:, 22:24], bsm[:, 19:21], bsm[:, 18:19], SCALE0, ALU.mult, ALU.mult))
            me.do(v.tensor_scalar(bsm[:, 22:24], bsm[:, 22:24], EXP_ROOM, 0.0, ALU.subtract, ALU.max))
            v.tensor_scalar(bsm[:, 24:26], bsm[:, 22:24], -1.0, None, ALU.mult).then_inc(s.bound0_ready, 1)
            norm(0)
            for t in range(KT0):
                read_projected(t, t, t % 2)
            for j in range(4):
                dve.wait_ge(s.q0_made, j + 1)
                v.tensor_tensor(qn[:, 2 * j:2 * j + 2, :, :].rearrange("p t h d -> p t (h d)"),
                                ps[:, 4 + j, :].rearrange("p (t n) -> p t n", t=2),
                                bq0[:].unsqueeze(1).to_broadcast([P, 2, D]), ALU.add).then_inc(s.q0_read, 1)
            dve.wait_ge(s.q0_read, 4)
            NQ = NT * H0
            qf = qn[:].rearrange("p t h d -> p (t h) d")
            qtmp = kc[:].rearrange("p g t h d -> p (g t h) d")[:, 0:NQ, :]
            me.do(v.tensor_reduce(s2[:, 0:NQ], qf, AX, ALU.add))
            me.do(v.tensor_scalar(s2[:, 0:NQ], s2[:, 0:NQ], 1.0 / D0, None, ALU.mult))
            me.do(v.tensor_tensor(qf, qf, bc(s2[:, 0:NQ], D0), ALU.subtract))
            me.do(v.tensor_tensor(qtmp, qf, qf, ALU.mult))
            me.do(v.tensor_reduce(s1[:, 0:NQ], qtmp, AX, ALU.add))
            v.tensor_scalar(s1[:, 0:NQ], s1[:, 0:NQ], 1.0 / D0, 1e-6, ALU.mult, ALU.add).then_inc(s.q0_var, 1)
            dve.wait_ge(s.q0_std, 1)
            me.do(v.reciprocal(s2[:, 0:NQ], s1[:, 0:NQ]))
            me.do(v.tensor_tensor(qf, qf, bc(s2[:, 0:NQ], D0), ALU.mult))
            q3 = qn[:].rearrange("p t h d -> p t (h d)")
            me.do(v.tensor_tensor(q3, q3, qnw[:, 0, :].unsqueeze(1).to_broadcast([P, NT, D]), ALU.mult))
            me.do(v.tensor_tensor(q3, q3, qnw[:, 1, :].unsqueeze(1).to_broadcast([P, NT, D]), ALU.add))

            kf = kx[:].rearrange("p g t h d -> p (g t h) d")

            def mean_keys(read):
                dve.wait_ge(s.misc_read, primed(read))
                me.do(v.tensor_reduce(s1[:], kf, AX, ALU.add))
                me.do(v.tensor_scalar(s1[:], s1[:], 1.0 / D0, None, ALU.mult))

            def center_keys():
                v.tensor_tensor(kf, kf, bc(s1[:], D0), ALU.subtract).then_inc(s.k_centered, 1)

            def key_variance(k):
                for g in range(NG):
                    dve.wait_ge(s.k_squared, k * 4 + (g + 1))
                    v.tensor_reduce(s2[:, g * KT0 * HG:(g + 1) * KT0 * HG], ksq[:].rearrange("p (m d) -> p m d", d=D0),
                                    AX, ALU.add).then_inc(s.k_sq_read, 1)
                dve.wait_ge(s.k_sq_read, k * 4 + 4)
                v.tensor_scalar(s2[:], s2[:], 1.0 / D0, 1e-6, ALU.mult, ALU.add).then_inc(s.k_var, 1)

            def key_scale(k):
                dve.wait_ge(s.k_std, k + 1)
                me.do(v.reciprocal(s1[:], s2[:]))

            def normed_keys(g, free):
                if free is not None:
                    dve.wait_ge(s.hi_ready, free)
                v.tensor_tensor(kgroup(kc, g), kgroup(kx, g), bc(s1[:, g * KT0 * HG:(g + 1) * KT0 * HG], D0),
                                ALU.mult).then_inc(s.k_normed, 1)

            def stack_queries(tile, g):
                for t in range(TB):
                    me.did(v.tensor_copy(qst[:, t, :, 0::2, :].bitcast(F32R), parts(qhead(tile, t, g))))
                me.wait()
                me.did(v.tensor_tensor(qst[:, 0, :, 1::2, :].bitcast(F32R), parts(qhead(tile, 0, g)), qst[:, 0, :, 0::2, :], ALU.subtract))
                v.tensor_tensor(qst[:, 1, :, 1::2, :].bitcast(F32R), parts(qhead(tile, 1, g)), qst[:, 1, :, 0::2, :],
                                ALU.subtract).then_inc(s.qst_ready, 1)

            def qhead(tile, t, g):
                return qn[:, bass.ds(tile + t, 1), g * HG:(g + 1) * HG, :].rearrange("p t h d -> p (t h) d")

            def read_queries(slot, m, par, free):
                if free is not None:
                    dve.wait_ge(s.scores0, primed(free))
                dve.wait_ge(s.misc_made, m + 1)
                src = ps[:, 6 + par, :].rearrange("p (a n) -> p a n", a=2)
                me.did(v.tensor_copy(qg[0:64, slot, :, 0, :], src[0:64]))
                v.tensor_copy(qg[64:P, slot, :, 1, :], src[64:P]).then_inc(s.misc_read, 1)

            def keys_lo(g, ready):
                dve.wait_ge(s.hi_ready, ready)
                v.tensor_tensor(kst[:, :, 2:4, :].bitcast(F32R), parts(kgroup(kc, g)),
                                kst[:, :, 0:2, :], ALU.subtract).then_inc(s.kst_ready, 1)

            def read_keys(j, slot, m, par):
                dve.wait_ge(s.misc_made, m + 1)
                v.tensor_copy(kT0[:, slot, j * 512:(j + 1) * 512], ps[:, 6 + par, :]).then_inc(s.misc_read, 1)

            def read_sums(b, st, m, par):
                dve.wait_ge(s.pv0, primed(b * (NG * KT0) + (st + 1) * KT0))
                v.tensor_copy(oT0[:], ps[:, 4:6, 0:SQ]).then_inc(s.o0_read, 1)
                dve.wait_ge(s.misc_made, m + 1)
                o = ps[:, 6 + par, :].rearrange("p (n d) -> p n d", d=2 * D0)
                me.do(v.tensor_copy(rd0[:], o[:, :, D0]))
                me.do(v.reciprocal(rd0[:], rd0[:]))
                v.tensor_tensor(on0[:], o[:, :, 0:D0], bc(rd0[:], D0), ALU.mult).then_inc(s.misc_read, 1)
                dve.wait_ge(s.misc_read, primed(m + 1))
                me.do(v.tensor_tensor(on0[:, 0:2 * HG, :], on0[:, 0:2 * HG, :], on0[:, 2 * HG:4 * HG, :], ALU.add))
                v.tensor_copy(xn[:, bass.ds(b * TB, TB), st * HG * D0:(st + 1) * HG * D0],
                              on0[:, 0:2 * HG, :].rearrange("p (t h) d -> p t (h d)", t=TB)).then_inc(s.ctx_made, 1)

            mean_keys(KT0)
            center_keys()
            key_variance(0)
            key_scale(0)
            for g in range(NG):
                normed_keys(g, None)
            stack_queries(0, 0)
            read_queries(0, KT0, KT0 % 2, None)
            keys_lo(0, 1)
            for j in range(7):
                read_keys(j, 0, KT0 + 1 + j, (KT0 + 1 + j) % 2)

            def dve_step(b, st, last):
                over = last and st == NG - 1
                nkv = KT0 if st == 0 and not last else 0
                par = MISC0 + MISC[st]
                slot = (st + 1) % 2
                if not over:
                    g1_ = (st + 1) % NG
                    stack_queries((b + 1) * TB if st == NG - 1 else b * TB, g1_)
                    read_queries(slot, misc(b, st, 0, last), par % 2, b * (NG * KT0) + st * KT0)
                    if nkv:
                        dve.wait_ge(s.vc_ready, b * 4 + 4)
                        for t in range(KT0):
                            read_projected(t, misc(b, st, 1 + t), (par + 1 + t) % 2)
                    if st == 1 and not last:
                        mean_keys(misc(b, 0, 1 + KT0))
                    if st == 2 and not last:
                        key_variance(b + 1)
                    keys_lo(g1_, b * 4 + (st + 2))
                    if st == 3 and not last:
                        for g in range(1, NG):
                            normed_keys(g, b * 4 + (g + 1))
                    for j in range(7):
                        k = 1 + nkv + j
                        read_keys(j, slot, misc(b, st, k, last), (par + k) % 2)
                        if j == 1 and st == 2 and not last:
                            key_scale(b + 1)
                            normed_keys(0, b * 4 + 1)
                k = 0 if over else 8 + nkv
                read_sums(b, st, misc(b, st, k, last), (par + k) % 2)
                if st == 1 and not last:
                    center_keys()

            with dve.Fori(0, B - 1) as b:
                me.enter(b, PER0)
                for st in range(NG):
                    dve_step(b, st, False)
                me.leave(B - 1)
            for st in range(NG):
                dve_step(B - 1, st, True)
            dve.wait_ge(s.y0_made, 1)
            ks = kc[:].rearrange("p g t h d -> p (g t h d)")[:, 0:NT * D]
            me.do(v.tensor_tensor(ks.rearrange("p (t n) -> p t n", t=NT), ps[:, 0:4, :].rearrange("p a (b n) -> p (a b) n", b=2),
                                  bo0[:].unsqueeze(1).to_broadcast([P, NT, D]), ALU.add))
            dve.wait_ge(s.tanh_made, 1)
            xflat = x[:].rearrange("p t n -> p (t n)")
            v.scalar_tensor_tensor(out=xflat, in0=ks, scalar=tg[:, 0:1], in1=xflat, op0=ALU.mult, op1=ALU.add).then_inc(s.x_updated, 1)
            dve.wait_ge(s.x_updated, 1)
            if stages < 2:
                return

            def shifted(E, k):
                dve.wait_ge(s.logits_made, k)
                lg = ps[:, 7, 0:NT * E].rearrange("p (t e) -> p t e", t=NT)
                me.do(v.tensor_copy(rr[:, :, 0:E], lg))
                me.do(v.tensor_reduce(rsm[:, 0, :], rr[:, :, 0:E], AX, ALU.max))
                v.tensor_tensor(rl[:, :, 0:E], rr[:, :, 0:E], bc(rsm[:, 0, :], E), ALU.subtract).then_inc(s.r_shifted, 1)
                dve.wait_ge(s.r_exp, k)

            def weights_parts(E, dsts, k):
                dve.wait_ge(s.w_turned, k)
                wt = ps[0:E, 4:6, :].rearrange("p a n -> p (a n)")
                me.do(v.tensor_copy(hi0[0:E, :], wt))
                me.do(v.tensor_tensor(rem1[0:E, :], wt, hi0[0:E, :], ALU.subtract))
                me.do(v.tensor_copy(mid0[0:E, :], rem1[0:E, :]))
                me.do(v.tensor_tensor(rem2[0:E, :], rem1[0:E, :], mid0[0:E, :], ALU.subtract))
                me.did(v.tensor_copy(dsts[0], hi0[0:E, :]))
                me.did(v.tensor_copy(dsts[1], mid0[0:E, :]))
                me.do(v.tensor_copy(dsts[2], rem2[0:E, :]))
                v.tensor_copy(rem1[0:1, 0:1], rem2[0:1, 0:1]).then_inc(s.wT_ready, 1)

            def ffn(u0, i, units, rows):
                for j in range(units):
                    dve.wait_ge(s.silu_made, at(u0, i, 4, j + 1))
                    dve.wait_ge(s.u_made, at(u0, i, 4, j + 1))
                    dve.wait_ge(s.h_made, primed(at(u0, i, 4, j)))
                    v.tensor_tensor(hh[0:rows, :], sg[0:rows, :], ps[0:rows, 5, :], ALU.mult).then_inc(s.h1_made, 1)
                    dve.wait_ge(s.h1_made, primed(at(u0, i, 4, j + 1)))
                    dve.wait_ge(s.w_made, at(u0, i, 4, j + 1))
                    dve.wait_ge(s.down_done, primed(at(u0 + (2 if u0 >= 2 * E0 else 1), i, 4, j - 1)))
                    v.tensor_tensor(hw[0:rows, j % 2, :], hh[0:rows, :], ps[0:rows, 6, :], ALU.mult).then_inc(s.h_made, 1)
                    dve.wait_ge(s.hs_hi, primed(at(u0, i, 4, j + 1)))
                    v.tensor_tensor(hs[0:rows, j % 2, 1, :], hw[0:rows, j % 2, :], hs[0:rows, j % 2, 0, :].bitcast(F32),
                                    ALU.subtract).then_inc(s.hs_lo, 1)

            norm(1)
            shifted(E0, 1)
            for t in range(NT):
                me.did(v.max(m8[:, t, :], re[:, t, 0:E0]))
            me.wait()
            for t in range(NT):
                me.did(v.match_replace(rr[:, t, 0:E0], m8[:, t, :], re[:, t, 0:E0], -1.0))
            me.wait()
            me.do(v.tensor_scalar(selb[:], rr[:, :, 0:E0], 0.0, None, ALU.is_lt))
            me.do(v.tensor_scalar(pre[:, 0, :], selb[:, 0, :], 0.0, None, ALU.mult))
            for t in range(1, NT):
                me.do(v.tensor_tensor(pre[:, t, :], pre[:, t - 1, :], selb[:, t - 1, :], ALU.add))
            v.tensor_tensor(rw[:, :, 0:E0], re[:, :, 0:E0], selb[:], ALU.mult).then_inc(s.sel_ready, 1)
            dve.wait_ge(s.sel_ready, 1)
            me.do(v.tensor_reduce(rsm[:, 1, :], rw[:, :, 0:E0], AX, ALU.add))
            me.do(v.reciprocal(rsm[:, 2, :], rsm[:, 1, :]))
            me.do(v.tensor_tensor(rw[:, :, 0:E0], rw[:, :, 0:E0], bc(rsm[:, 2, :], E0), ALU.mult))
            dve.wait_ge(s.pos_made, 1)
            wf = rw[:, :, 0:E0]
            v.scalar_tensor_tensor(out=wf, in0=ps[:, 7, 0:NT * E0].rearrange("p (t e) -> p t e", t=NT), scalar=float(CAP),
                                   in1=wf, op0=ALU.is_lt, op1=ALU.mult).then_inc(s.w_ready, 1)
            weights_parts(E0, [wT0[0:E0, :], wT0[E0:2 * E0, :], wT0[2 * E0:3 * E0, :]], 1)
            with dve.Fori(0, E0 // 2) as i:
                ffn(0, i, 4, I0)
            dve.wait_ge(s.down_done, primed(1 + 2 * E0))
            v.scalar_tensor_tensor(out=xflat, in0=ps[:, 0:4, :].rearrange("p a n -> p (a n)"), scalar=tg[:, 2:3], in1=xflat,
                                   op0=ALU.mult, op1=ALU.add).then_inc(s.x_updated, 1)
            dve.wait_ge(s.x_updated, 2)
            if stages < 3:
                return

            norm(2)
            dve.wait_ge(s.w1_loaded, 16 * 7)
            me.do(v.scalar_tensor_tensor(out=g1[:, 2:3], in0=g1[:, 0:1], scalar=float(D1) ** -0.5, in1=g1[:, 1:2],
                                         op0=ALU.mult, op1=ALU.mult))
            me.do(v.tensor_tensor(g1r[:, 2, :], g1r[:, 0, :], g1r[:, 1, :], ALU.mult))
            me.do(v.tensor_reduce(g1[:, 3:4], g1r[:, 2, :], AX, ALU.max, apply_absolute_value=True))
            me.do(v.tensor_scalar(g1[:, 3:4], g1[:, 3:4], float(D1) ** 0.5, -EXP_ROOM, ALU.mult, ALU.add))
            v.tensor_scalar(g1[:, 3:4], g1[:, 3:4], 0.0, -1.0, ALU.max, ALU.mult).then_inc(s.bound1_ready, 1)
            dve.wait_ge(s.wk_hi, 1)
            v.tensor_tensor(wk1[:, 1, :], stage[:, 0:H1 * D1], wk1[:, 0, :].bitcast(F32), ALU.subtract).then_inc(s.wk_lo, 1)
            for j in range(8):
                dve.wait_ge(s.m1_made, j + 1)
                v.tensor_copy(m1[:, 2 * j:2 * j + 2, :].rearrange("p h n -> p (h n)"), ps[:, 4 + j % 4, :]).then_inc(s.m1_read, 1)
            for b in range(B):
                if b == 0:
                    me.do(v.memset(rk1[:], 1.0))
                    me.do(v.memset(acc1[:], 0.0))
                else:
                    dve.wait_ge(s.probs1, primed(KT * 8 * b))
                dve.wait_ge(s.ctxT_hi, b + 1)
                v.tensor_tensor(ctxT1[:, 1, 0:KV], stage[:, 0:KV], ctxT1[:, 0, 0:KV].bitcast(F32), ALU.subtract).then_inc(s.ctxT_lo, 1)
                for t in range(TB):
                    tt = TB * b + t
                    dve.wait_ge(s.q1_read, 2 * (tt + 1))
                    me.do(v.tensor_reduce(rq1[:, 1, :], q1T[:], AX, ALU.add))
                    v.tensor_scalar(rq1[:, 0, :], rq1[:, 1, :], 1.0 / D1, 1e-5, ALU.mult, ALU.add).then_inc(s.q1_var, 1)
                    dve.wait_ge(s.q1_std, tt + 1)
                    me.do(v.reciprocal(rq1[:, 1, :], rq1[:, 0, :]))
                    v.tensor_tensor(q1, q1, bc(rq1[:, 1, :], D1), ALU.mult).then_inc(s.q1_normed, 1)
                    with dve.Fori(0, 2) as i:
                        for u in range(KT):
                            dve.wait_ge(s.k1_squared, primed(at(2 * KT * tt, i, KT, u + 1)))
                            r = ROWS1[u]
                            v.tensor_reduce(rk1[0:r, u, bass.ds(i * 4 + t * 8, 4)],
                                            ksq1[0:r, u % 2, :].rearrange("p (h d) -> p h d", h=4),
                                            AX, ALU.add).then_inc(s.k1_reduced, 1)
                    for j in range(4):
                        dve.wait_ge(s.q1_turned, 4 * tt + j + 1)
                        v.tensor_scalar(q1T[:, 4 * j:4 * j + 4, :].rearrange("p h n -> p (h n)"), ps[:, 4 + j, :],
                                        g1[:, 2:3], None, ALU.mult).then_inc(s.q1T_ready, 1)
                    for j in range(4):
                        dve.wait_ge(s.qq_hi, 4 * tt + j + 1)
                        v.tensor_tensor(qq_out(1, j, t), ps[:, 4 + j, :].rearrange("p (h n) -> p h n", h=4),
                                        qq_out(0, j, t).bitcast(F32), ALU.subtract).then_inc(s.qq_read, 1)
                dve.wait_ge(s.k1_reduced, primed(4 * KT * (b + 1)))
                v.tensor_scalar(rk1[:], rk1[:], 1.0 / D1, 1e-5, ALU.mult, ALU.add).then_inc(s.k1_var, 1)
                dve.wait_ge(s.k1_std, b + 1)
                v.reciprocal(rk1[:], rk1[:]).then_inc(s.rk1_ready, 1)
                with dve.Fori(0, H1 // 2) as hp:
                    me.enter(hp, 3)
                    k0 = KT * 8 * b
                    for t in range(KT):
                        r = ROWS1[t]
                        pt = p1[:, BANK1[t], :, :].rearrange("p a n -> p (a n)")
                        dve.wait_ge(s.probs1, primed(at(k0, hp, KT, t + 1)))
                        if t == 0:
                            dve.wait_ge(s.den_made, primed(at(8 * b, hp, 1, 0)))
                            v.tensor_copy(dsum[:], pt).then_inc(s.summed, 1)
                        else:
                            dve.wait_ge(s.summed, primed(at(k0, hp, KT, t)))
                            v.tensor_tensor(dsum[0:r, :], dsum[0:r, :], pt[0:r, :], ALU.add).then_inc(s.summed, 1)
                    dve.wait_ge(s.pv1, primed(at(k0, hp, KT, KT)))
                    v.tensor_copy(oT1[:], ps[:, 4, :]).then_inc(s.o1_read, 1)
                    dve.wait_ge(s.den_made, primed(at(8 * b, hp, 1, 1)))
                    v.reciprocal(rd1[:], ps[:, 7, 0:4]).then_inc(s.den_read, 1)
                    dve.wait_ge(s.den_read, primed(at(8 * b, hp, 1, 1)))
                    dve.wait_ge(s.y1_made, at(8 * b, hp, 1, 1))
                    for j in range(4):
                        o = acc1[:, TB * b + j % 2, :]
                        if j == 2:
                            me.wait()
                        ins = v.scalar_tensor_tensor(out=o, in0=ps[:, 5 + j // 2, (j % 2) * D:(j % 2 + 1) * D], scalar=rd1[:, j:j + 1],
                                                     in1=o, op0=ALU.mult, op1=ALU.add)
                        if j < 3:
                            me.did(ins)
                        else:
                            ins.then_inc(s.y1_added, 1)
                    me.wait()
                    dve.wait_ge(s.y1_added, primed(at(8 * b, hp, 1, 1)))
                    me.leave(H1 // 2)
            v.scalar_tensor_tensor(out=xflat, in0=acc1[:].rearrange("p t n -> p (t n)"), scalar=tg[:, 1:2], in1=xflat,
                                   op0=ALU.mult, op1=ALU.add).then_inc(s.x_updated, 1)
            dve.wait_ge(s.x_updated, 3)
            if stages < 4:
                return

            norm(3)
            dve.wait_ge(s.xnT_act, 8)
            dve.wait_ge(s.xnT_dve, 8)
            dve.wait_ge(s.router_loaded, 16 * 16)
            me.do(v.tensor_reduce(xm[:], xnT[:].rearrange("p k (b n) -> p (k b) n", b=B), AX, ALU.add))
            v.tensor_scalar(xm[:], xm[:], 1.0 / SQ, None, ALU.mult).then_inc(s.xm_ready, 1)
            dve.wait_ge(s.tl_made, 1)
            me.do(v.tensor_tensor(td[:, 1, :], ps[0:B, 6, 0:ND], teb2[:], ALU.add))
            me.do(v.tensor_reduce(td[:, 2, 0:1], td[:, 1, :], AX, ALU.max))
            v.tensor_scalar(td[:, 0, :], td[:, 1, :], td[:, 2, 0:1], None, ALU.subtract).then_inc(s.tl_shifted, 1)
            dve.wait_ge(s.tl_exp, 1)
            me.do(v.tensor_reduce(td[:, 2, 0:1], td[:, 1, :], AX, ALU.add))
            me.do(v.reciprocal(td[:, 2, 1:2], td[:, 2, 0:1]))
            v.tensor_scalar(td[:, 3, :], td[:, 1, :], td[:, 2, 1:2], 0.5, ALU.mult, ALU.mult).then_inc(s.td_ready, 1)
            dve.wait_ge(s.td_turned, 1)
            v.tensor_copy(tdT[:], bc(ps[0:ND, 6, 0:B], P)).then_inc(s.tdT_ready, 1)
            shifted(E1, 2)
            me.did(v.tensor_reduce(rsm[:, 3, :], re[:], AX, ALU.add))
            me.did(v.tensor_tensor(rl[:, :, 0:E1], rr[:, :, 0:E1], rb1[:].unsqueeze(1).to_broadcast([P, NT, E1]), ALU.add))
            me.do(v.memset(rl[:, :, E1:E1 + TOPS - TOP1], -FAR))
            for t in range(NT):
                me.did(v.max(m8[:, t, :], rl[:, t, 0:E1]))
            me.wait()
            me.do(v.memset(m8[:, :, TOP1:TOPS], -FAR))
            for t in range(NT):
                me.did(v.match_replace(rr[:, t, :], m8[:, t, :], rl[:, t, :], FAR))
            me.wait()
            me.do(v.tensor_scalar(rr[:, :, 0:E1], rr[:, :, 0:E1], 0.5 * FAR, None, ALU.is_gt))
            me.do(v.tensor_tensor(rw[:], re[:], rr[:, :, 0:E1], ALU.mult))
            me.do(v.tensor_reduce(rsm[:, 1, :], rw[:], AX, ALU.add))
            me.do(v.scalar_tensor_tensor(out=rsm[:, 2, :], in0=rsm[:, 3, :], scalar=1e-8, in1=rsm[:, 1, :],
                                         op0=ALU.mult, op1=ALU.add))
            me.do(v.reciprocal(rsm[:, 4, :], rsm[:, 2, :]))
            v.tensor_tensor(rw[:], rw[:], bc(rsm[:, 4, :], E1), ALU.mult).then_inc(s.w_ready, 1)
            weights_parts(E1, [wT1a[0:E1, :], wT1a[E1:2 * E1, :], wT1b[0:E1, :]], 2)
            u0 = 2 * E0
            ffn(u0, None, 8, P)
            with dve.Fori(0, E1 // 4) as i:
                ffn(u0 + 8, i, 4, P)
            dve.wait_ge(s.down_done, primed(2 + 2 * E0 + 8 + E1))
            v.scalar_tensor_tensor(out=xflat, in0=ps[:, 0:4, :].rearrange("p a n -> p (a n)"), scalar=tg[:, 3:4], in1=xflat,
                                   op0=ALU.mult, op1=ALU.add).then_inc(s.x_updated, 1)


def _layout(i):
    import numpy as np
    def rows(v, n=128):
        return np.ascontiguousarray(np.broadcast_to(v, (n,) + v.shape))
    g = lambda n: i["L0_xattn_" + n]
    h = lambda n: i["L1_xattn_" + n]
    f = lambda n: i["L1_ffn_" + n]
    dca = lambda w: w.reshape(-1, 2, 16, 16).transpose(0, 2, 1, 3).reshape(-1, 512)
    tile = lambda w, n: np.tile(w, n)
    main, extra = 13 * 4, 4
    knwb = np.stack([np.concatenate([tile(g("kn_w"), main), tile(g("kn_dca_w"), extra)]),
                     np.concatenate([tile(g("kn_b"), main), tile(g("kn_dca_b"), extra)])])
    new = {
        "gates": rows(np.concatenate([i["g_xattn"], i["g_ffn"]])),
        "Wkv0": np.concatenate([g("Wk"), g("Wv")], axis=1),
        "Wdca0": dca(g("Wkv_dca")),
        "bq0": rows(g("bq")),
        "bkv0": rows(np.stack([np.concatenate([g("bk"), g("bv")]), dca(g("bkv_dca")[None])[0]])),
        "bo0": rows(g("bo")),
        "qnw": rows(np.stack([tile(g("qn_w"), 16), tile(g("qn_b"), 16)])),
        "knwb": rows(knwb),
        "bnd": rows(np.stack([g(n) for n in ("qn_w", "qn_b", "kn_w", "kn_b", "kn_dca_w", "kn_dca_b")])),
        "ctxT": i["ctx_1024"].transpose(0, 2, 1),
        "WrT": f("Wr").T, "rb1": rows(f("router_bias")), "affT": f("affinity").T,
        "te_W1T": f("te_W1").T, "teb1": f("te_b1")[:, None], "te_W2T": f("te_W2").T, "teb2": rows(f("te_b2"), 4),
        "WkT1": h("Wk").reshape(128, 16, 128).transpose(2, 1, 0),
        "WvT1": h("Wv").reshape(128, 16, 128).transpose(2, 1, 0),
        "g1": np.stack([h("gq"), h("gk")], axis=1),
        "g1r": rows(np.stack([h("gq"), h("gk")])),
    }
    for n in ("x", "ctx_1024", "L0_xattn_Wq", "L0_xattn_Wo", "L0_ffn_gate_w", "L0_ffn_w_gate", "L0_ffn_w_up", "L0_ffn_w_down",
              "L1_xattn_Wq", "L1_xattn_Wk", "L1_xattn_Wo", "L1_ffn_Wg", "L1_ffn_Wu", "L1_ffn_Wd", "L1_ffn_Sg", "L1_ffn_Su", "L1_ffn_Sd"):
        new[n] = i[n]
    return {k: np.ascontiguousarray(v) for k, v in new.items()}


def kernel(**inputs):
    import numpy as _np
    import concourse.bacc as _bacc
    from concourse import mybir as _mybir
    from concourse.bass_utils import run_bass_kernel_spmd as _run

    nc = _bacc.Bacc("TRN2", target_bir_lowering=False, num_devices=1)
    laid = _layout({k: _np.asarray(v) for k, v in inputs.items()})
    arrays, args = {}, {}
    for name, v in laid.items():
        arrays[f"in_{name}_dram"] = v
        args[name] = nc.dram_tensor(f"in_{name}_dram", v.shape, _mybir.dt.from_np(v.dtype), kind="ExternalInput").ap()
    out = nc.dram_tensor("out_0_dram", (4, 256, 256), _mybir.dt.float32, kind="ExternalOutput").ap()
    program(nc, args, out)
    r = _run(nc, [arrays], core_ids=[0])
    return r.results[0]["out_0_dram"]
```

```python
from contextlib import ExitStack

import numpy as np

import concourse.bass as bass
from concourse import mybir

F32 = mybir.dt.float32
F32R = mybir.dt.float32r
BF16 = mybir.dt.bfloat16
ALU = mybir.AluOpType
ACT = mybir.ActivationFunctionType
AX = mybir.AxisListType.X

P = 128
B, SQ, D = 4, 256, 256
KV, C = 1601, 128
NT = B * SQ // P
KD = D // P
TB = SQ // P
KT = -(-KV // P)
HALF = 512

H0, D0 = 16, 16
DCA = 16
KMAIN = KV - DCA
KT0 = KT + 1
ROWS0 = [P] * (KT - 1) + [KMAIN - P * (KT - 1), DCA]
COL0 = [P * t for t in range(KT)] + [KMAIN]
HG = 4
NG = H0 // HG
SCALE0 = D0 ** -0.5
E0, I0, TOP0 = 32, 96, 8
CAP = 2 * (B * SQ * TOP0 // E0)
H1, D1 = 16, 128
ROWS1 = [P] * (KT - 1) + [KV - P * (KT - 1)]
BANK1 = [t % 3 for t in range(KT - 1)] + [3]
KSQ = 7
E1, F1, TOP1, ND = 64, 64, 4, 4
NSH = 2
TOPS = 8
EXP_ROOM = 70.0
FAR = 3.0e38


PRIMED = ("probs0 pv0 o0_read misc_read h1_made h_made hs_hi hs_lo down_done "
          "probs1 pv1 summed den_made den_read o1_read y1_added scores0 scores1").split()


PRIME = 4


def primed(count):
    return count + PRIME


class Steps:

    def __init__(self, eng, sem):
        self.eng, self.sem, self.n, self.i, self.per = eng, sem, 0, None, 0

    def did(self, ins):
        ins.then_inc(self.sem, 1)
        self.n += 1

    def wait(self):
        self.eng.wait_ge(self.sem, self.n if self.i is None else self.i * self.per + self.n)

    def do(self, ins):
        self.did(ins)
        self.wait()

    def enter(self, i, per):
        self.i, self.per, self.first = i, per, self.n

    def leave(self, rounds):
        assert self.n - self.first == self.per, (self.n - self.first, self.per)
        self.n = self.first + self.per * rounds
        self.i = None


def at(base, i, per, k):
    return base + k if i is None else i * per + (base + k)


PER0 = 43


def program(nc, a, out, stages=4):
    ctx = ExitStack()
    with ctx:
        def sem(name):
            return ctx.enter_context(nc.semaphore(name))

        def sb(name, shape, dt=F32, scope=ctx):
            return scope.enter_context(nc.sbuf_tensor("s_" + name, shape, dt))

        ps = ctx.enter_context(nc.psum_tensor("ps", [P, 8, 512], F32))
        x = sb("x", [P, NT, D])
        xn = sb("xn", [P, NT, D])
        xnT = sb("xnT", [P, KD, NT * P])
        ident = sb("ident", [P, P])
        ones = sb("ones", [P, 8])
        tg = sb("tg", [P, 4])
        bn = sb("bn", [P, NT, 6])
        mv = sb("mv", [P, NT, 2])
        lnv = sb("lnv", [P, NT])
        lnr = sb("lnr", [P, NT])
        sa = ExitStack()
        wq0 = sb("wq0", [P, KD, D], scope=sa)
        wkv0 = sb("wkv0", [P, 2 * D], scope=sa)
        wdca0 = sb("wdca0", [P, 2 * D], scope=sa)
        wo0 = sb("wo0", [P, KD, D], scope=sa)
        bq0 = sb("bq0", [P, D], scope=sa)
        bkv0 = sb("bkv0", [P, 2, 2 * D], scope=sa)
        bo0 = sb("bo0", [P, D], scope=sa)
        qnw = sb("qnw", [P, 2, H0 * D0], scope=sa)
        knwb = sb("knwb", [P, 2, KT0 * HG * D0], scope=sa)
        bnd = sb("bnd", [P, 6, D0], scope=sa)
        bsm = sb("bsm", [P, 32], scope=sa)
        ctxT0 = sb("ctxT0", [P, KV], scope=sa)
        qn = sb("qn", [P, NT, H0, D0], scope=sa)
        qst = sb("qst", [P, TB, HG, 4, D0], scope=sa)
        qg = sb("qg", [P, 2, 2, 2, SQ], F32R, scope=sa)
        kst = sb("kst", [P, KT0 * HG, 4, D0], scope=sa)
        kT0 = sb("kT0", [P, 2, KT0 * 2 * P], F32R, scope=sa)
        vg = sb("vg", [P, 2, KT0, HG, 2 * D0], scope=sa)
        kc = sb("kc", [P, NG, KT0, HG, D0], scope=sa)
        kx = sb("kx", [P, NG, KT0, HG, D0], scope=sa)
        vc = sb("vc", [P, NG, KT0, HG, D0], scope=sa)
        vx = sb("vx", [P, NG, KT0, HG, D0], scope=sa)
        ksq = sb("ksq", [P, KT0 * HG * D0], scope=sa)
        p0 = sb("p0", [P, 2, 4 * SQ], scope=sa)
        s1 = sb("s1", [P, KT0 * H0], scope=sa)
        s2 = sb("s2", [P, KT0 * H0], scope=sa)
        oT0 = qnw
        rd0 = sb("rd0", [P, 4 * HG], scope=sa)
        rq0 = sb("rq0", [P, 3, NT * H0], scope=sa)
        on0 = sb("on0", [P, 4 * HG, D0], scope=sa)
        sa.close()

        tri = sb("tri", [P, P], BF16)
        onesb = sb("onesb", [P, P], BF16)
        sel1 = sb("sel1", [P, E1, F1], BF16)
        wT1a = sb("wT1a", [P, NT * P], BF16)
        wT1b = sb("wT1b", [P, NT * P], BF16)
        g1 = sb("g1", [P, 4])
        g1r = sb("g1r", [P, 3, D1])
        zb = sb("zb", [P, HALF], BF16)
        ones512 = sb("ones512", [1, NT * P], BF16)

        sc = ExitStack()
        sel0 = sb("sel0", [3 * E0, E0, I0], BF16, scope=sc)
        wT0 = sb("wT0", [3 * E0, NT * P], BF16, scope=sc)
        gatew = sb("gatew", [P, KD, E0], scope=sc)
        wr1 = sb("wr1", [P, KD, E1], scope=sc)
        rb1 = sb("rb1", [P, E1], scope=sc)
        aff1 = sb("aff1", [ND, E1], scope=sc)
        te1 = sb("te1", [P, KD, P], scope=sc)
        teb1 = sb("teb1", [P, 1], scope=sc)
        te2 = sb("te2", [P, ND], scope=sc)
        teb2 = sb("teb2", [B, ND], scope=sc)
        xm = sb("xm", [P, KD * B], scope=sc)
        h1t = sb("h1t", [P, B], scope=sc)
        td = sb("td", [B, 4, ND], scope=sc)
        tdT = sb("tdT", [ND, B, P], scope=sc)
        rl = sb("rl", [P, NT, E1 + TOPS - TOP1], scope=sc)
        rr = sb("rr", [P, NT, E1 + TOPS - TOP1], scope=sc)
        re = sb("re", [P, NT, E1], scope=sc)
        rw = sb("rw", [P, NT, E1], scope=sc)
        m8 = sb("m8", [P, NT, TOPS], scope=sc)
        rsm = sb("rsm", [P, 6, NT], scope=sc)
        selb = sb("selb", [P, NT, E0], BF16, scope=sc)
        pre = sb("pre", [P, NT, E0], BF16, scope=sc)
        mid0 = sb("mid0", [E1, NT * P], BF16, scope=sc)
        rem1 = sb("rem1", [E1, NT * P], scope=sc)
        wgu = sb("wgu", [P, 2, 2, KD, P], scope=sc)
        wd = sb("wd", [P, 2, D], scope=sc)
        wgus = sb("wgus", [P, 2, 2, 2, KD, P], F32R, scope=sc)
        wds = sb("wds", [P, 2, 2, D], F32R, scope=sc)
        xT = sb("xT", [P, 2, KD, NT * P], F32R, scope=sc)
        sg = sb("sg", [P, HALF], scope=sc)
        hh = sb("hh", [P, HALF], scope=sc)
        hw = sb("hw", [P, 2, HALF], scope=sc)
        hs = sb("hs", [P, 2, 2, HALF], F32R, scope=sc)
        sc.close()

        se = ExitStack()
        m1 = sb("m1", [P, H1, D], scope=se)
        ctxT1 = sb("ctxT1", [P, 2, KV + 1], F32R, scope=se)
        ctx1 = sb("ctx1", [P, KT, C], scope=se)
        rk1 = sb("rk1", [P, KT, H1], scope=se)
        q1T = sb("q1T", [P, H1, P], scope=se)
        rq1 = sb("rq1", [P, 2, H1], scope=se)
        ksq1 = sb("ksq1", [P, KSQ, HALF], scope=se)
        p1 = sb("p1", [P, 4, 2, SQ], scope=se)
        dsum = sb("dsum", [P, 2 * SQ], scope=se)
        oT1 = sb("oT1", [P, 2 * SQ], scope=se)
        rd1 = sb("rd1", [P, 4], scope=se)
        wk1 = sb("wk1", [P, 2, H1 * D1], F32R, scope=se)
        wq1 = sb("wq1", [P, KD, H1 * D1], scope=se)
        wkT1 = sb("wkT1", [P, H1, C], scope=se)
        stage = sb("stage", [P, KV + KT * C], scope=se)
        q1 = stage[:, 0:H1 * D1].rearrange("p (h d) -> p h d", h=H1)
        sw = ExitStack()
        wkv1 = sb("wkv1", [P, H1 * (C + D)], scope=sw)
        sw.close()
        qq1 = sb("qq1", [P, 2, H1 * SQ], F32R, scope=se)
        se.close()
        acc1 = xn
        wvT1 = wkv1[:, 0:H1 * C].rearrange("p (h c) -> p h c", h=H1)
        wo1 = wkv1[:, H1 * C:].rearrange("p (h n) -> p h n", h=H1)

        S = {n: sem(n) for n in (
            "x_loaded gates_loaded w0_loaded small0_loaded ctxT0_loaded "
            "router_loaded w1_loaded ctx1_loaded0 ctx1_loaded1 stored "
            "consts_made ident_made dve_steps act_steps pool_steps tanh_made "
            "ln_var ln_std ln_done ln_turned xnT_act xnT_dve "
            "q0_made q0_read q0_var q0_std qst_ready bound_sq bound_root bound0_ready "
            "qn_ready w0_centered q0_squared q0_scale misc_made misc_read k_squared k_sq_read k_var k_std k_normed "
            "hi_ready kst_ready vc_ready vg_ready scores0 probs0 pv0 o0_read "
            "ctx_made cx_turned cxT_act y0_made x_updated "
            "logits_made r_shifted r_exp sel_ready pos_made w_ready w_turned wT_ready "
            "xm_ready te_made te_gelu tl_made tl_shifted tl_exp td_ready td_turned tdT_ready "
            "g_made u_made w_made silu_made h1_made h_made hs_hi hs_lo down_done wslot0 wslot1 w_split xT_hi xT_lo "
            "m1_made m1_read bound1_ready "
            "k1_made k1_squared k1_reduced k1_var k1_std rk1_ready sums_zeroed q1_scale wk_hi wk_lo ctxT_hi ctxT_lo ctx_kept "
            "q1_made q1_read q1_var q1_std q1_normed q1_turned q1T_ready qq_made qq_hi qq_read "
            "scores1 probs1 pv1 summed o1_read den_made den_read y1_made y1_added").split()}
        s = type("Sems", (), S)

        xf = a["x"].rearrange("b s d -> (b s) d").rearrange("(t p) d -> p t d", p=P)
        of = out.rearrange("b s d -> (b s) d").rearrange("(t p) d -> p t d", p=P)

        def act_turn(act, k):
            act.wait_ge(s.ln_var, k + 1)
            nc.scalar.activation(lnr[:], lnv[:], ACT.Sqrt).then_inc(s.ln_std, 1)
            for j in range(2):
                act.wait_ge(s.ln_turned, 16 * k + 8 * j + 4)
                nc.scalar.copy(xnT[:, 0, j * HALF:(j + 1) * HALF], ps[:, 2 * j, :]).then_inc(s.xnT_act, 1)

        def act_split(act, k):
            for j in range(KD):
                act.wait_ge(s.xnT_dve if j else s.xnT_act, 2 * (k + 1))
                nc.scalar.copy(xT[:, 0, j, :], xnT[:, j, :]).then_inc(s.xT_hi, 1)

        def act_ffn(act, u0, i, units, rows):
            for j in range(units):
                u = at(u0, i, 4, j)
                act.wait_ge(s.g_made, at(u0, i, 4, j + 1))
                act.wait_ge(s.h1_made, primed(u))
                nc.scalar.activation(sg[0:rows, :], ps[0:rows, 4, :], ACT.Silu).then_inc(s.silu_made, 1)
                act.wait_ge(s.h_made, primed(at(u0, i, 4, j + 1)))
                act.wait_ge(s.down_done, primed(at(u0 + (2 if u0 >= 2 * E0 else 1), i, 4, j - 1)))
                nc.scalar.copy(hs[0:rows, j % 2, 0, :], hw[0:rows, j % 2, :]).then_inc(s.hs_hi, 1)

        def key_tiles(b):
            return [(q, u, (4 * b + q) * KT + u) for q in range(4) for u in range(KT)]

        def qq_out(part, j, t):
            return qq1[:, part, :].rearrange("p (h t n) -> p h t n", t=TB, n=P)[:, 4 * j:4 * j + 4, t, :]

        def rk_col(t, hp, j, r):
            return rk1[0:r, t, bass.ds(hp * 2 + j, 1)]

        def pe_turn(pe, k):
            for j in range(4):
                pe.wait_ge(s.ln_done, NT * k + NT // 2 * (j // 2 + 1))
                for t in range(4):
                    tt = 4 * (j // 2) + t
                    nc.tensor.transpose(ps[:, j, t * P:(t + 1) * P], xn[:, tt, (j % 2) * P:(j % 2 + 1) * P],
                                        ident[:]).then_inc(s.ln_turned, 1)
            pe.wait_ge(s.xnT_act, 2 * (k + 1))
            pe.wait_ge(s.xnT_dve, 2 * (k + 1))

        def pe_zero(pe):
            for j in range(4):
                ins = nc.tensor.matmul(ps[:, j, :], zb[:, 0:P], zb[:], start=True, stop=False, skip_group_check=True)
            ins.then_inc(s.down_done, 1)

        PRODUCT = ((0, 0), (0, 1), (1, 0))

        def pe_up(pe, u0, i, j, rows, weight, loaded):
            slot, half = j // 2 % 2, j % 2
            n = slice(half * HALF, (half + 1) * HALF)
            if half == 0:
                pe.wait_ge(s.w_split, loaded)
            for g in range(2):
                if g == 0:
                    pe.wait_ge(s.silu_made, at(u0, i, 4, j))
                else:
                    pe.wait_ge(s.h1_made, primed(at(u0, i, 4, j)))
                ops = [(k, w, x_) for k in range(KD) for w, x_ in PRODUCT]
                for c, (k, w, x_) in enumerate(ops):
                    ins = nc.tensor.matmul(ps[0:rows, 4 + g, :], wgus[:, slot, w, g, k, 0:rows], xT[:, x_, k, n],
                                           start=c == 0, stop=c == len(ops) - 1)
                ins.then_inc(s.u_made if g else s.g_made, 1)
            pe.wait_ge(s.h_made, primed(at(u0, i, 4, j)))
            parts = weight(i, j)
            for k, (sel, wt) in enumerate(parts):
                ins = nc.tensor.matmul(ps[0:rows, 6, :], sel, wt[:, n], start=k == 0, stop=k == len(parts) - 1)
            ins.then_inc(s.w_made, 1)

        def pe_down(pe, u0, i, j, rows):
            slot, half = j // 2 % 2, j % 2
            pe.wait_ge(s.hs_lo, primed(at(u0, i, 4, j + 1)))
            for t in range(4):
                tt = half * 4 + t
                for h, w in PRODUCT:
                    ins = nc.tensor.matmul(ps[:, tt // 2, (tt % 2) * D:(tt % 2 + 1) * D],
                                           hs[0:rows, j % 2, h, t * P:(t + 1) * P], wds[0:rows, slot, w, :],
                                           start=False, stop=False, skip_group_check=True)
            ins.then_inc(s.down_done, 1)

        MISC0 = KT0 + 1 + 7
        MISC = [0, KT0 + 9, KT0 + 18, KT0 + 27]
        MISCB = KT0 + 36

        def misc(b, st, k, last=False):
            return b * MISCB + (MISC0 + MISC[st] + k - (KT0 if last and st else 0))

        def parts(ap):
            return ap.unsqueeze(2).to_broadcast([P, ap.shape[1], 2, D0])

        def kgroup(t, g):
            return t[:, g].rearrange("p t h d -> p (t h) d")

        block = ctx.enter_context(nc.Block())
        def store(sp):
            halves = 2 if stages == 4 else 1
            n = NT // halves
            for half in range(halves):
                sp.wait_ge(s.x_updated, stages + half)
                sp.dma_start(of[:, half * n:(half + 1) * n, :], x[:, half * n:(half + 1) * n, :]).then_inc(s.stored, 16)
            sp.wait_ge(s.stored, 16 * halves)

        @block.sync
        def _(sp):
            for name in PRIMED:
                sp.sem_inc(S[name], PRIME)
            sp.dma_start(x[:], xf).then_inc(s.x_loaded, 16)
            for dst, src in ((wkv0[:], a["Wkv0"]), (wdca0[:], a["Wdca0"]), (bkv0[:], a["bkv0"]),
                             (wq0[:], a["L0_xattn_Wq"].rearrange("(k p) n -> p k n", p=P)), (bq0[:], a["bq0"])):
                sp.dma_start(dst, src).then_inc(s.w0_loaded, 16)
            sp.dma_start(ctxT0[:], a["ctxT"][0]).then_inc(s.ctxT0_loaded, 16)
            for dst, src in ((knwb[:], a["knwb"]), (qnw[:], a["qnw"]), (bnd[:], a["bnd"]), (bo0[:], a["bo0"]),
                             (wo0[:], a["L0_xattn_Wo"].rearrange("(k p) n -> p k n", p=P))):
                sp.dma_start(dst, src).then_inc(s.small0_loaded, 16)
            sp.dma_start(tg[:], a["gates"]).then_inc(s.gates_loaded, 16)
            for b in range(1, B):
                sp.wait_ge(s.misc_made, KT0 if b == 1 else misc(b - 2, 0, 1 + KT0))
                sp.dma_start(ctxT0[:], a["ctxT"][b]).then_inc(s.ctxT0_loaded, 16)

            def weights(slot, split, g_src, u_src, d_src, rows):
                if split is not None:
                    sp.wait_ge(s.w_split, split)
                w = s.wslot1 if slot else s.wslot0
                cols = slice(0, rows)
                for j, src in enumerate((g_src, u_src)):
                    sp.dma_start(wgu[:, slot, j, :, cols], src.rearrange("(k p) n -> p k n", p=P)).then_inc(w, 16)
                sp.dma_start(wd[cols, slot, :], d_src).then_inc(w, 16)

            def expert0(e, slot, split):
                weights(slot, split, a["L0_ffn_w_gate"][e], a["L0_ffn_w_up"][e], a["L0_ffn_w_down"][e], I0)

            def load_router():
                for dst, src in ((gatew[:], a["L0_ffn_gate_w"].rearrange("(k p) n -> p k n", p=P)),
                                 (wr1[:], a["WrT"].rearrange("(k p) n -> p k n", p=P)),
                                 (rb1[:], a["rb1"]), (aff1[:], a["affT"]),
                                 (te1[:], a["te_W1T"].rearrange("(k p) n -> p k n", p=P)),
                                 (teb1[:], a["teb1"]), (te2[:], a["te_W2T"]), (teb2[:], a["teb2"])):
                    sp.dma_start(dst, src).then_inc(s.router_loaded, 16)

            if stages < 2:
                return store(sp)
            sp.wait_ge(s.x_updated, 1)
            load_router()
            expert0(0, 0, None)
            expert0(1, 1, None)
            for dst, src in ((stage[:, 0:H1 * D1], a["L1_xattn_Wk"]), (wvT1, a["WvT1"]),
                             (wo1, a["L1_xattn_Wo"].rearrange("(h d) n -> d h n", d=D1)),
                             (wkT1[:], a["WkT1"]),
                             (wq1[:], a["L1_xattn_Wq"].rearrange("(k p) n -> p k n", p=P)),
                             (g1[:, 0:2], a["g1"]), (g1r[:, 0:2, :], a["g1r"])):
                sp.dma_start(dst, src).then_inc(s.w1_loaded, 16)
            with sp.Fori(1, E0 // 2) as i:
                for slot in range(2):
                    expert0(i * 2 + slot, slot, i * 2 + (slot - 1))

            if stages < 3:
                return store(sp)
            for b in range(B):
                if b == 0:
                    sp.wait_ge(s.wk_lo, 1)
                else:
                    sp.wait_ge(s.q1_turned, 4 * TB * b)
                sp.dma_start(stage[:, 0:KV], a["ctxT"][b]).then_inc(s.ctx1_loaded0, 16)
                st = stage[:, KV:].rearrange("p (t c) -> p t c", c=C)
                sp.dma_start(st[:, 0:KT - 1, :],
                             a["ctx_1024"][b, 0:P * (KT - 1), :].rearrange("(t p) c -> p t c", p=P)).then_inc(s.ctx1_loaded1, 16)
                sp.dma_start(st[0:ROWS1[-1], KT - 1, :], a["ctx_1024"][b, P * (KT - 1):KV, :]).then_inc(s.ctx1_loaded1, 16)

            if stages < 4:
                return store(sp)
            sp.wait_ge(s.x_updated, 3)
            load_router()

            def shared(j, slot, split):
                i, cols = j // 2, slice(j % 2 * P, (j % 2 + 1) * P)
                weights(slot, split, a["L1_ffn_Sg"][i, :, cols], a["L1_ffn_Su"][i, :, cols], a["L1_ffn_Sd"][i, cols, :], P)

            def pair1(e, slot, split):
                sp.wait_ge(s.w_split, split)
                w = s.wslot1 if slot else s.wslot0
                for j in range(2):
                    n = slice(j * F1, (j + 1) * F1)
                    for k, name in enumerate(("L1_ffn_Wg", "L1_ffn_Wu")):
                        sp.dma_start(wgu[:, slot, k, :, n], a[name][e * 2 + j].rearrange("(k p) n -> p k n", p=P)).then_inc(w, 16)
                    sp.dma_start(wd[n, slot, :], a["L1_ffn_Wd"][e * 2 + j]).then_inc(w, 16)

            for j in range(2 * NSH):
                shared(j, j % 2, None if j < 2 else E0 + j - 1)
            with sp.Fori(0, E1 // 4) as i:
                for slot in range(2):
                    pair1(i * 2 + slot, slot, i * 2 + (E0 + 2 * NSH + slot - 1))

            store(sp)

        @block.gpsimd
        def _(pool):
            me = Steps(pool, s.pool_steps)
            g_ = nc.gpsimd
            me.do(g_.memset(ident[:], 0.0))
            g_.affine_select(out=ident[:], in_=ident[:], compare_op=ALU.not_equal, fill=1.0, base=0,
                             pattern=[[-1, P]], channel_multiplier=1).then_inc(s.ident_made, 1)
            me.did(g_.memset(ones[:], 1.0))
            me.do(g_.memset(vg[:], 1.0))
            for j in range(2):
                for t in (KT0 - 2, KT0 - 1):
                    me.did(g_.affine_select(out=vg[:, j, t], in_=vg[:, j, t], compare_op=ALU.is_gt, fill=0.0, base=ROWS0[t],
                                            pattern=[[0, HG], [0, 2 * D0]], channel_multiplier=-1))
            me.wait()
            pool.wait_ge(s.small0_loaded, 16 * 5)

            def unit(ap):
                return ones[:, 0:1].unsqueeze(2).unsqueeze(3).to_broadcast(list(ap.shape))

            def keys_hi(g, normed, kst_free):
                pool.wait_ge(s.k_normed, normed)
                flat = kc[:, g].rearrange("p t h d -> p (t h d)")
                me.do(g_.tensor_tensor(flat, flat, knwb[:, 0, :], ALU.mult))
                if kst_free is not None:
                    pool.wait_ge(s.misc_made, kst_free)
                bias = knwb[:, 1, :].rearrange("p (r d) -> p r d", d=D0)
                me.do(g_.tensor_tensor(kst[:, :, 0:2, :].bitcast(F32R), parts(kgroup(kc, g)), parts(bias), ALU.add))
                g_.tensor_tensor(flat, flat, knwb[:, 1, :], ALU.add).then_inc(s.hi_ready, 1)

            def values_group(g, slot, pv, copied):
                pool.wait_ge(s.vc_ready, copied)
                if pv is not None:
                    pool.wait_ge(s.pv0, primed(pv))
                g_.tensor_tensor(vg[:, slot, :, :, 0:D0], vc[:, g], unit(vc[:, g]), ALU.mult).then_inc(s.vg_ready, 1)

            def take_values(g, read):
                pool.wait_ge(s.misc_read, primed(read))
                g_.tensor_tensor(vc[:, g], vx[:, g], unit(vx[:, g]), ALU.mult).then_inc(s.vc_ready, 1)

            for g in range(NG):
                take_values(g, KT0)
            keys_hi(0, 1, None)
            values_group(0, 0, None, 4)
            pool.wait_ge(s.q0_scale, 2)
            qf = qn[:, TB:].rearrange("p t h d -> p (t h) d")
            me.do(g_.tensor_tensor(qf, qf, rq0[:, 2, TB * H0:].unsqueeze(2).to_broadcast([P, (NT - TB) * H0, D0]), ALU.mult))
            q3 = qn[:, TB:].rearrange("p t h d -> p t (h d)")
            me.do(g_.tensor_tensor(q3, q3, qnw[:, 0, :].unsqueeze(1).to_broadcast([P, NT - TB, D]), ALU.mult))
            g_.tensor_tensor(q3, q3, qnw[:, 1, :].unsqueeze(1).to_broadcast([P, NT - TB, D]), ALU.add).then_inc(s.qn_ready, 1)

            def step(b, st, last):
                if st < 3:
                    keys_hi(st + 1, b * 4 + (st + 2), misc(b, 0, 0) if st == 0 else misc(b, st - 1, (KT0 if st == 1 and not last else 0) + 8, last))
                    values_group(st + 1, (st + 1) % 2, b * (4 * KT0) + st * KT0, b * 4 + 4)
                    if st == 2 and not last:
                        pool.wait_ge(s.vg_ready, b * 4 + 4)
                        for g in range(NG):
                            take_values(g, misc(b, 0, 1 + KT0))
                elif not last:
                    keys_hi(0, b * 4 + 5, misc(b, 2, 8))
                    values_group(0, 0, b * (4 * KT0) + 3 * KT0, b * 4 + 8)

            with pool.Fori(0, B - 1) as b:
                me.enter(b, 8)
                for st in range(NG):
                    step(b, st, False)
                me.leave(B - 1)
            for st in range(NG):
                step(B - 1, st, True)

            pool.wait_ge(s.x_updated, 1)
            me.did(g_.memset(tri[:], 1.0))
            me.do(g_.memset(sel0[:], 0.0))
            g_.affine_select(out=tri[:], in_=tri[:], compare_op=ALU.is_gt, fill=0.0, base=0,
                             pattern=[[1, P]], channel_multiplier=-1).then_inc(s.consts_made, 1)
            g_.memset(onesb[:], 1.0).then_inc(s.consts_made, 1)
            g_.memset(zb[:], 0.0).then_inc(s.consts_made, 1)
            for j in range(3):
                me.do(g_.affine_select(out=sel0[:], in_=sel0[:], compare_op=ALU.not_equal, fill=1.0, base=-j * E0,
                                       pattern=[[-1, E0], [0, I0]], channel_multiplier=1))
            g_.memset(ones512[:], 1.0).then_inc(s.consts_made, 1)

            def tables1():
                g_.memset(wT1b[:], 0.0).then_inc(s.consts_made, 1)
                me.do(g_.memset(sel1[:], 0.0))
                for j in range(2):
                    me.do(g_.affine_select(out=sel1[:], in_=sel1[:], compare_op=ALU.not_equal, fill=1.0, base=-j * E1,
                                           pattern=[[-1, E1], [0, F1]], channel_multiplier=1))
                g_.memset(ones512[0:1, 0:1], 1.0).then_inc(s.consts_made, 1)

            def stream_rest(k):
                pool.wait_ge(s.xT_hi, KD * k)
                g_.tensor_tensor(xT[:, 1], xnT[:], xT[:, 0].bitcast(F32), ALU.subtract).then_inc(s.xT_lo, 1)

            def split_weights(slot, loaded, free, rows):
                pool.wait_ge(s.wslot1 if slot else s.wslot0, loaded)
                if free is not None:
                    pool.wait_ge(s.down_done, primed(free))
                cols = slice(0, rows)
                gu = wgu[:, slot].rearrange("p g k n -> p (g k) n")[:, :, cols]
                gus = [wgus[:, slot, part].rearrange("p g k n -> p (g k) n")[:, :, cols] for part in range(2)]
                d, ds = wd[cols, slot, :], [wds[cols, slot, part, :] for part in range(2)]
                me.did(g_.tensor_tensor(gus[0], gu, ones[:, 0:1].unsqueeze(2).to_broadcast(list(gu.shape)), ALU.mult))
                me.do(g_.tensor_tensor(ds[0], d, ones[cols, 0:1].to_broadcast(list(d.shape)), ALU.mult))
                me.did(g_.tensor_tensor(gus[1], gu, gus[0].bitcast(F32), ALU.subtract))
                g_.tensor_tensor(ds[1], d, ds[0].bitcast(F32), ALU.subtract).then_inc(s.w_split, 1)

            if stages < 2:
                return
            for e in range(2):
                split_weights(e, 48, None, I0)
                if e == 0:
                    stream_rest(1)
            with pool.Fori(1, E0 // 2) as i:
                me.enter(i - 1, 6)
                for slot in range(2):
                    split_weights(slot, i * 48 + 48, i * 4 + (2 * slot - 1), I0)
                me.leave(E0 // 2 - 1)
            tables1()
            if stages < 3:
                return
            pool.wait_ge(s.ln_turned, 48)
            pool.wait_ge(s.wk_hi, 1)
            g_.tensor_tensor(wk1[:, 1, :], stage[:, 0:H1 * D1], wk1[:, 0, :].bitcast(F32), ALU.subtract).then_inc(s.wk_lo, 1)
            me.do(g_.memset(rk1[:], 1.0))
            g_.memset(acc1[:], 0.0).then_inc(s.sums_zeroed, 1)
            for tt in range(NT):
                pool.wait_ge(s.q1_scale, tt + 1)
                g_.tensor_tensor(q1, q1, rq1[:, 1, :].unsqueeze(2).to_broadcast([P, H1, D1]), ALU.mult).then_inc(s.q1_normed, 1)
            if stages < 4:
                return
            base, m0 = 48 * E0 // 2, 2 + 2 * E0
            for j in range(2 * NSH):
                split_weights(j % 2, base + 48 * (j // 2 + 1), None if j < 2 else m0 + 2 * (j - 1), P)
                if j == 0:
                    stream_rest(2)
            with pool.Fori(0, E1 // 4) as i:
                me.enter(i, 6)
                for slot in range(2):
                    split_weights(slot, i * 96 + (base + 96 + 96), i * 4 + (m0 + 2 * (2 * NSH + slot - 1)), P)
                me.leave(E1 // 4)

        @block.scalar
        def _(act):
            act.wait_ge(s.gates_loaded, 16)
            nc.scalar.activation(tg[:], tg[:], ACT.Tanh).then_inc(s.tanh_made, 1)
            act_turn(act, 0)

            def square_keys(g, k, read):
                act.wait_ge(s.misc_read, primed(read))
                act.wait_ge(s.k_sq_read, k * 4 + g)
                nc.scalar.activation(ksq[:], kx[:, g].rearrange("p t h d -> p (t h d)"), ACT.Square).then_inc(s.k_squared, 1)

            def key_std(k):
                act.wait_ge(s.k_var, k + 1)
                nc.scalar.activation(s2[:], s2[:], ACT.Sqrt).then_inc(s.k_std, 1)

            for g in range(NG):
                square_keys(g, 0, KT0)
            key_std(0)
            for j, ts in enumerate((slice(0, TB), slice(TB, NT))):
                act.wait_ge(s.q0_read, 4 if j else 1)
                nc.scalar.activation(p0[:].rearrange("p a n -> p (a n)")[:, ts.start * D:ts.stop * D],
                                     qn[:, ts].rearrange("p t h d -> p (t h d)"), ACT.Square).then_inc(s.q0_squared, 1)
                act.wait_ge(s.q0_var, j + 1)
                m = slice(ts.start * H0, ts.stop * H0)
                nc.scalar.activation(rq0[:, 1, m], rq0[:, 0, m], ACT.Sqrt).then_inc(s.q0_std, 1)
            act.wait_ge(s.bound_sq, 1)
            nc.scalar.activation(bsm[:, 6:12], bsm[:, 0:6], ACT.Sqrt).then_inc(s.bound_root, 1)
            act.wait_ge(s.bound0_ready, 1)

            def act_step(b, st, last):
                for t in range(KT0):
                    n = st * KT0 + t
                    act.wait_ge(s.scores0, primed(b * (NG * KT0) + (n + 1)))
                    act.wait_ge(s.pv0, primed(b * (NG * KT0) + (n - 1)))
                    r, dca = ROWS0[t], t == KT0 - 1
                    nc.scalar.activation(p0[0:r, t % 2, :],
                                         ps[0:r, 2 * (t % 2):2 * (t % 2) + 2, :].rearrange("p a n -> p (a n)"),
                                         ACT.Exp, bias=bsm[0:r, 24 + dca:25 + dca], scale=SCALE0).then_inc(s.probs0, 1)
                    if st == 2 and not last:
                        if 3 <= t < 3 + NG:
                            square_keys(t - 3, b + 1, misc(b, 0, 1 + KT0))
                        if t == 9:
                            key_std(b + 1)

            with act.Fori(0, B - 1) as b:
                for st in range(NG):
                    act_step(b, st, False)
            for st in range(NG):
                act_step(B - 1, st, True)
            act.wait_ge(s.cx_turned, 16)
            for j in range(4):
                nc.scalar.copy(xnT[:, j // 2, (j % 2) * HALF:(j % 2 + 1) * HALF], ps[:, j, :]).then_inc(s.cxT_act, 1)
            if stages < 2:
                return
            act_turn(act, 1)
            act_split(act, 1)
            act.wait_ge(s.r_shifted, 1)
            nc.scalar.activation(re[:, :, 0:E0], rl[:, :, 0:E0], ACT.Exp).then_inc(s.r_exp, 1)
            with act.Fori(0, E0 // 2) as i:
                act_ffn(act, 0, i, 4, I0)
            if stages < 3:
                return
            act_turn(act, 2)
            act.wait_ge(s.w1_loaded, 16 * 7)
            nc.scalar.copy(wk1[:, 0, :], stage[:, 0:H1 * D1]).then_inc(s.wk_hi, 1)
            for b in range(B):
                act.wait_ge(s.ctx1_loaded0, 16 * (b + 1))
                act.wait_ge(s.scores1, primed(KT * 8 * b))
                nc.scalar.copy(ctxT1[:, 0, 0:KV], stage[:, 0:KV]).then_inc(s.ctxT_hi, 1)
                act.wait_ge(s.ctx1_loaded1, 32 * (b + 1))
                act.wait_ge(s.pv1, primed(KT * 8 * b))
                st = stage[:, KV:].rearrange("p (t c) -> p t c", c=C)
                nc.scalar.copy(ctx1[:, 0:KT - 1, :], st[:, 0:KT - 1, :]).then_inc(s.ctx_kept, 1)
                nc.scalar.copy(ctx1[0:ROWS1[-1], KT - 1, :], st[0:ROWS1[-1], KT - 1, :]).then_inc(s.ctx_kept, 1)

                def take_queries(tt, j):
                    act.wait_ge(s.q1_made, 4 * tt + j + 1)
                    if tt % TB == 0:
                        act.wait_ge(s.ctxT_lo, b + 1)
                        act.wait_ge(s.ctx_kept, 2 * (b + 1))
                    act.wait_ge(s.qq_made, 4 * tt)
                    nc.scalar.copy(q1[:, 4 * j:4 * j + 4, :].rearrange("p h d -> p (h d)"), ps[:, 4 + j, :]).then_inc(s.q1_read, 1)
                    nc.scalar.activation(q1T[:, 4 * j:4 * j + 4, :].rearrange("p h n -> p (h n)"), ps[:, 4 + j, :],
                                         ACT.Square).then_inc(s.q1_read, 1)

                for j in range(4):
                    take_queries(TB * b, j)
                for q, u, n in key_tiles(b):
                    tt = TB * b + q // 2
                    act.wait_ge(s.k1_made, n + 1)
                    if n >= KSQ:
                        act.wait_ge(s.k1_reduced, n + 1 - KSQ)
                    r = ROWS1[u]
                    nc.scalar.activation(ksq1[0:r, n % KSQ, :], ps[0:r, n % 4, :], ACT.Square).then_inc(s.k1_squared, 1)
                    if q % 2 == 0 and u == 2:
                        act.wait_ge(s.q1_var, tt + 1)
                        nc.scalar.activation(rq1[:, 0, :], rq1[:, 0, :], ACT.Sqrt).then_inc(s.q1_std, 1)
                    if q % 2 == 1 and 4 <= u < 8:
                        j = u - 4
                        act.wait_ge(s.qq_made, 4 * tt + j + 1)
                        nc.scalar.copy(qq_out(0, j, q // 2), ps[:, 4 + j, :].rearrange("p (h n) -> p h n", h=4)).then_inc(s.qq_hi, 1)
                    if q == 1 and u >= 9:
                        take_queries(tt + 1, u - 9)
                act.wait_ge(s.k1_var, b + 1)
                nc.scalar.activation(rk1[:], rk1[:], ACT.Sqrt).then_inc(s.k1_std, 1)
                act.wait_ge(s.rk1_ready, b + 1)
                act.wait_ge(s.bound1_ready, 1)
                nc.scalar.activation(rq1[0:1, 1, 0:1], ones[0:1, 0:1], ACT.Exp).then_inc(s.act_steps, 1)
                with act.Fori(0, H1 // 2) as hp:
                    k = KT * 8 * b

                    for t in range(KT):
                        act.wait_ge(s.scores1, primed(at(k, hp, KT, t + 1)))
                        act.wait_ge(s.pv1, primed(at(k, hp, KT, t - 2 if t >= 3 else t - 3)))
                        act.wait_ge(s.summed, primed(at(k, hp, KT, t - 2 if t >= 3 else t - 3)))
                        r = ROWS1[t]
                        for j in range(2):
                            ins = nc.scalar.activation(p1[0:r, BANK1[t], j, :], ps[0:r, BANK1[t], j * SQ:(j + 1) * SQ], ACT.Exp,
                                                       bias=g1[0:r, 3:4], scale=rk_col(t, hp, j, r))
                        ins.then_inc(s.probs1, 1)
            if stages < 4:
                return
            act_turn(act, 3)
            act_split(act, 3)
            act.wait_ge(s.te_made, 1)
            nc.scalar.activation(h1t[:], ps[:, 6, 0:B], ACT.Gelu, bias=teb1[:, 0:1]).then_inc(s.te_gelu, 1)
            act.wait_ge(s.tl_shifted, 1)
            nc.scalar.activation(td[:, 1, :], td[:, 0, :], ACT.Exp).then_inc(s.tl_exp, 1)
            act.wait_ge(s.r_shifted, 2)
            nc.scalar.activation(re[:], rl[:, :, 0:E1], ACT.Exp).then_inc(s.r_exp, 1)
            u0 = 2 * E0
            act_ffn(act, u0, None, 8, P)
            with act.Fori(0, E1 // 4) as i:
                act_ffn(act, u0 + 8, i, 4, P)

        @block.tensor
        def _(pe):
            pe.wait_ge(s.ident_made, 1)
            pe.wait_ge(s.w0_centered, 1)

            def bank_free(m):
                pe.wait_ge(s.misc_read, primed(m - 1))

            def project(t, m, par, loaded):
                if t == 0:
                    pe.wait_ge(s.ctxT0_loaded, loaded)
                bank_free(m)
                nc.tensor.matmul(ps[0:ROWS0[t], 6 + par, :], ctxT0[:, COL0[t]:COL0[t] + ROWS0[t]],
                                 (wdca0 if t == KT0 - 1 else wkv0)[:], start=True, stop=True).then_inc(s.misc_made, 1)

            for t in range(KT0):
                project(t, t, t % 2, 16)
            pe_turn(pe, 0)
            pe.wait_ge(s.misc_read, primed(KT0))
            for t in range(NT):
                for k in range(KD):
                    ins = nc.tensor.matmul(ps[:, 4 + t // 2, (t % 2) * D:(t % 2 + 1) * D], xnT[:, k, t * P:(t + 1) * P],
                                           wq0[:, k, :], start=k == 0, stop=k == KD - 1)
                if t % 2:
                    ins.then_inc(s.q0_made, 1)
            def turn_queries(m, par, ready):
                pe.wait_ge(s.qst_ready, ready)
                bank_free(m)
                for k in range(4):
                    ins = nc.tensor.transpose(ps[:, 6 + par, k * P:(k + 1) * P],
                                              qst[:, k % 2, k // 2 * 2:k // 2 * 2 + 2, :, :].rearrange("p h r d -> p (h r d)"), ident[:])
                ins.then_inc(s.misc_made, 1)

            def turn_keys(j, m, par, ready):
                if j == 0:
                    pe.wait_ge(s.kst_ready, ready)
                bank_free(m)
                for k in range(4):
                    row = (2 * j + k // 2) * HG + 2 * (k % 2)
                    ins = nc.tensor.transpose(ps[:, 6 + par, k * P:(k + 1) * P],
                                              kst[:, row:row + 2, :, :].rearrange("p h r d -> p (h r d)"), ident[:])
                ins.then_inc(s.misc_made, 1)

            def turn_sums(m, par, read):
                pe.wait_ge(s.o0_read, primed(read))
                bank_free(m)
                for k in range(4):
                    ins = nc.tensor.transpose(ps[:, 6 + par, k * P:(k + 1) * P], oT0[:, k // 2, (k % 2) * P:(k % 2 + 1) * P], ident[:])
                ins.then_inc(s.misc_made, 1)

            def scores(b, st, t, ready=None):
                slot = st % 2
                if t or st or not isinstance(b, int) or b:
                    pe.wait_ge(s.probs0, primed(b * (NG * KT0) + (st * KT0 + t - 1)))
                if t == 0:
                    pe.wait_ge(s.misc_read, primed(ready))
                for hp in range(2):
                    c = (2 * t + hp) * P
                    ins = nc.tensor.matmul(ps[0:ROWS0[t], 2 * (t % 2) + hp, :], kT0[:, slot, c:c + ROWS0[t]],
                                           qg[:, slot, hp, :, :].rearrange("p a n -> p (a n)"), start=True, stop=True)
                ins.then_inc(s.scores0, 1)

            def values(b, st, t):
                slot = st % 2
                pe.wait_ge(s.probs0, primed(b * (NG * KT0) + (st * KT0 + t + 1)))
                if t == 0:
                    pe.wait_ge(s.o0_read, primed(b * NG + st))
                    pe.wait_ge(s.vg_ready, b * NG + (st + 1))
                dca = t == KT0 - 1
                for h in range(HG):
                    ins = nc.tensor.matmul(ps[32 * h:32 * h + 32, 5 if dca else 4, 0:SQ], vg[:, slot, t, h, :],
                                           p0[:, t % 2, h * SQ:(h + 1) * SQ], start=t == 0 or dca,
                                           stop=t >= KT0 - 2, skip_group_check=True)
                ins.then_inc(s.pv0, 1)

            def pe_step(b, st, last):
                over = last and st == NG - 1
                nkv = KT0 if st == 0 and not last else 0
                for t in range(KT0):
                    if t + 1 < KT0:
                        scores(b, st, t + 1)
                    if t == (1 if st == 0 else 2) and not over:
                        turn_queries(misc(b, st, 0, last), (MISC0 + MISC[st]) % 2, b * NG + (st + 2))
                    if st == 0 and 1 <= t <= 7 and not last:
                        for tt in (2 * t - 2, 2 * t - 1):
                            project(tt, misc(b, 0, 1 + tt), (MISC0 + 1 + tt) % 2, b * 16 + 32)
                    for j in range(max(2 * (t - 10), 0), min(2 * (t - 9), 7) if not over else 0):
                        turn_keys(j, misc(b, st, 1 + nkv + j, last), (MISC0 + MISC[st] + 1 + nkv + j) % 2, b * NG + (st + 2))
                    values(b, st, t)
                if not over:
                    ready = misc(b, st, 8 + nkv, last)
                    if st < NG - 1:
                        scores(b, st + 1, 0, ready)
                    else:
                        scores(b + 1, 0, 0, ready)
                k = 0 if over else 8 + nkv
                turn_sums(misc(b, st, k, last), (MISC0 + MISC[st] + k) % 2, b * NG + (st + 1))

            pe.wait_ge(s.q0_read, 4)
            turn_queries(KT0, KT0 % 2, 1)
            for j in range(7):
                turn_keys(j, KT0 + 1 + j, (KT0 + 1 + j) % 2, 1)
            scores(0, 0, 0, MISC0)
            with pe.Fori(0, B - 1) as b:
                for st in range(NG):
                    pe_step(b, st, False)
            for st in range(NG):
                pe_step(B - 1, st, True)
            pe.wait_ge(s.ctx_made, NG * B)
            pe.wait_ge(s.small0_loaded, 16 * 5)
            for j in range(4):
                for t in range(4):
                    tt = 4 * (j % 2) + t
                    nc.tensor.transpose(ps[:, j, t * P:(t + 1) * P], xn[:, tt, (j // 2) * P:(j // 2 + 1) * P],
                                        ident[:]).then_inc(s.cx_turned, 1)
            pe.wait_ge(s.cxT_act, 4)
            for t in range(NT):
                for k in range(KD):
                    ins = nc.tensor.matmul(ps[:, t // 2, (t % 2) * D:(t % 2 + 1) * D], xnT[:, k, t * P:(t + 1) * P],
                                           wo0[:, k, :], start=k == 0, stop=k == KD - 1)
            ins.then_inc(s.y0_made, 1)
            if stages < 2:
                return

            pe_turn(pe, 1)
            pe.wait_ge(s.router_loaded, 16 * 8)
            for t in range(NT):
                for k in range(KD):
                    ins = nc.tensor.matmul(ps[:, 7, t * E0:(t + 1) * E0], xnT[:, k, t * P:(t + 1) * P], gatew[:, k, :],
                                           start=k == 0, stop=k == KD - 1)
            ins.then_inc(s.logits_made, 1)
            pe.wait_ge(s.sel_ready, 1)
            pe.wait_ge(s.consts_made, 3)
            for t in range(NT):
                nc.tensor.matmul(ps[:, 7, t * E0:(t + 1) * E0], tri[:], selb[:, t, :], start=True, stop=False)
                ins = nc.tensor.matmul(ps[:, 7, t * E0:(t + 1) * E0], onesb[:], pre[:, t, :], start=False, stop=True)
            ins.then_inc(s.pos_made, 1)
            pe.wait_ge(s.w_ready, 1)
            for t in range(NT):
                ins = nc.tensor.transpose(ps[0:E0, 4 + t // 4, (t % 4) * P:(t % 4 + 1) * P], rw[:, t, 0:E0], ident[:])
            ins.then_inc(s.w_turned, 1)
            pe.wait_ge(s.wT_ready, 1)
            pe.wait_ge(s.consts_made, 4)
            pe_zero(pe)

            def weight0(i, j):
                e = i * 2 + j // 2
                return [(sel0[:, bass.ds(e, 1), :].rearrange("p e n -> p (e n)"), wT0)]

            pe.wait_ge(s.xT_lo, 1)
            pe_up(pe, 0, 0, 0, I0, weight0, 1)
            last = E0 // 2 - 1
            with pe.Fori(0, last) as i:
                for j in range(4):
                    if j < 3:
                        pe_up(pe, 0, i, j + 1, I0, weight0, i * 2 + ((j + 1) // 2 + 1))
                    else:
                        i1 = i + 1
                        pe_up(pe, 0, i1, 0, I0, weight0, i1 * 2 + 1)
                    pe_down(pe, 0, i, j, I0)
            for j in range(4):
                if j < 3:
                    pe_up(pe, 4 * last, None, j + 1, I0, lambda _, jj: weight0(last, jj), 2 * last + (j + 1) // 2 + 1)
                pe_down(pe, 4 * last, None, j, I0)
            if stages < 3:
                return

            pe_turn(pe, 2)
            pe.wait_ge(s.w1_loaded, 16 * 7)
            for h in range(H1):
                if h >= 8 and h % 2 == 0:
                    pe.wait_ge(s.m1_read, h // 2 - 3)
                ins = nc.tensor.matmul(ps[:, 4 + h // 2 % 4, (h % 2) * D:(h % 2 + 1) * D], wvT1[:, h, :], wo1[:, h, :],
                                       start=True, stop=True)
                if h % 2:
                    ins.then_inc(s.m1_made, 1)
            pe.wait_ge(s.m1_read, 8)
            pe.wait_ge(s.wk_lo, 1)

            def product(out, lhs, rhs, first=True, last=True):
                for n, (x_, y_) in enumerate(((0, 0), (0, 1), (1, 0))):
                    ins = nc.tensor.matmul(out, lhs(x_), rhs(y_), start=first and n == 0, stop=last and n == 2)
                return ins

            for b in range(B):
                def ctx_cols(t):
                    return lambda part: ctxT1[:, part, t * P:t * P + ROWS1[t]]

                def queries(tt, j):
                    if tt % TB:
                        pe.wait_ge(s.qq_read, 4 * (tt - 1) + j + 1)
                    for k in range(KD):
                        ins = nc.tensor.matmul(ps[:, 4 + j, :], xnT[:, k, tt * P:(tt + 1) * P], wq1[:, k, j * 512:(j + 1) * 512],
                                               start=k == 0, stop=k == KD - 1)
                    ins.then_inc(s.q1_made, 1)

                if b:
                    pe.wait_ge(s.y1_added, primed(8 * b))
                    pe.wait_ge(s.o1_read, primed(8 * b))
                for j in range(4):
                    queries(TB * b, j)
                pe.wait_ge(s.ctxT_lo, b + 1)
                pe.wait_ge(s.probs1, primed(KT * 8 * b))
                for q, u, n in key_tiles(b):
                    tt = TB * b + q // 2
                    if q % 2 == 1 and u == 0:
                        pe.wait_ge(s.q1_normed, tt + 1)
                        for j in range(4):
                            for h in range(4):
                                ins = nc.tensor.transpose(ps[:, 4 + j, h * P:(h + 1) * P], q1[:, 4 * j + h, :], ident[:])
                            ins.then_inc(s.q1_turned, 1)
                    if q % 2 == 1 and 3 <= u < 7:
                        j = u - 3
                        pe.wait_ge(s.q1T_ready, 4 * tt + j + 1)
                        for h in range(4):
                            ins = nc.tensor.matmul(ps[:, 4 + j, h * P:(h + 1) * P], wkT1[:, 4 * j + h, :], q1T[:, 4 * j + h, :],
                                                   start=True, stop=True)
                        ins.then_inc(s.qq_made, 1)
                    if q == 1 and u >= 9:
                        queries(tt + 1, u - 9)
                    if n >= 4:
                        pe.wait_ge(s.k1_squared, n - 3)
                    product(ps[0:ROWS1[u], n % 4, :], ctx_cols(u),
                            lambda part: wk1[:, part, q * 512:(q + 1) * 512]).then_inc(s.k1_made, 1)
                pe.wait_ge(s.k1_squared, 4 * KT * (b + 1))
                pe.wait_ge(s.qq_read, 4 * TB * (b + 1))
                pe.wait_ge(s.ctx_kept, 2 * (b + 1))
                k0 = KT * 8 * b

                def scores1(hp, t):
                    if t < KT - 1:
                        pe.wait_ge(s.probs1, primed(hp * KT + (k0 + (t - 2 if t >= 3 else t - 3))))
                    product(ps[0:ROWS1[t], BANK1[t], :], ctx_cols(t),
                            lambda part: qq1[:, part, bass.ds(hp * (2 * SQ), 2 * SQ)]).then_inc(s.scores1, 1)

                def pair(hp, following):
                    for t in range(KT):
                        if t + 2 < KT:
                            scores1(hp, t + 2)
                        if t == 0:
                            pe.wait_ge(s.o1_read, primed(hp + 8 * b))
                        pe.wait_ge(s.probs1, primed(hp * KT + (k0 + t + 1)))
                        nc.tensor.matmul(ps[:, 4, :], ctx1[0:ROWS1[t], t, :],
                                         p1[0:ROWS1[t], BANK1[t], :, :].rearrange("p a n -> p (a n)"),
                                         start=t == 0, stop=t == KT - 1).then_inc(s.pv1, 1)
                    if following:
                        scores1(hp + 1, 0)
                        scores1(hp + 1, 1)
                    pe.wait_ge(s.summed, primed(hp * KT + (k0 + KT)))
                    pe.wait_ge(s.den_read, primed(hp + 8 * b))
                    for j in range(4):
                        ins = nc.tensor.matmul(ps[:, 7, j:j + 1], dsum[:, j * P:(j + 1) * P], ones[:, 0:1], start=True, stop=True)
                    ins.then_inc(s.den_made, 1)
                    pe.wait_ge(s.o1_read, primed(hp + (8 * b + 1)))
                    pe.wait_ge(s.y1_added, primed(hp + 8 * b))
                    for j in range(4):
                        ins = nc.tensor.matmul(ps[:, 5 + j // 2, (j % 2) * D:(j % 2 + 1) * D], oT1[:, j * P:(j + 1) * P],
                                               m1[:].rearrange("p h n -> p (h n)")[:, bass.ds(hp * (2 * D) + (j // 2) * D, D)],
                                               start=True, stop=True)
                    ins.then_inc(s.y1_made, 1)

                scores1(0, 0)
                scores1(0, 1)
                with pe.Fori(0, H1 // 2 - 1) as hp:
                    pair(hp, True)
                pair(H1 // 2 - 1, False)
            if stages < 4:
                return

            pe_turn(pe, 3)
            pe.wait_ge(s.router_loaded, 16 * 16)
            pe.wait_ge(s.xm_ready, 1)
            for k in range(KD):
                ins = nc.tensor.matmul(ps[:, 6, 0:B], te1[:, k, :], xm[:, k * B:(k + 1) * B], start=k == 0, stop=k == KD - 1)
            ins.then_inc(s.te_made, 1)
            pe.wait_ge(s.te_gelu, 1)
            nc.tensor.matmul(ps[0:B, 6, 0:ND], h1t[:], te2[:], start=True, stop=True).then_inc(s.tl_made, 1)
            pe.wait_ge(s.td_ready, 1)
            nc.tensor.transpose(ps[0:ND, 6, 0:B], td[:, 3, :], ident[0:B, 0:B]).then_inc(s.td_turned, 1)
            pe.wait_ge(s.tdT_ready, 1)
            for t in range(NT):
                for k in range(KD):
                    nc.tensor.matmul(ps[:, 7, t * E1:(t + 1) * E1], xnT[:, k, t * P:(t + 1) * P], wr1[:, k, :],
                                     start=k == 0, stop=False)
                ins = nc.tensor.matmul(ps[:, 7, t * E1:(t + 1) * E1], tdT[:, t // TB, :], aff1[:], start=False, stop=True)
            ins.then_inc(s.logits_made, 1)
            pe.wait_ge(s.w_ready, 2)
            for t in range(NT):
                ins = nc.tensor.transpose(ps[0:E1, 4 + t // 4, (t % 4) * P:(t % 4 + 1) * P], rw[:, t, :], ident[:])
            ins.then_inc(s.w_turned, 1)
            pe.wait_ge(s.wT_ready, 2)
            pe.wait_ge(s.consts_made, 6)
            pe_zero(pe)
            u0 = 2 * E0

            def weight_one(i, j):
                return [(onesb[0:1, :], ones512)]

            def weight1(i, j):
                e = i * 4 + j // 2 * 2
                sel = sel1[:].rearrange("p e n -> p (e n)")[:, bass.ds(e * F1, 2 * F1)]
                return [(sel, wT1a), (sel, wT1b)]

            pe.wait_ge(s.xT_lo, 2)
            pe_up(pe, u0, None, 0, P, weight_one, E0 + 1)
            for j in range(8):
                if j < 7:
                    pe_up(pe, u0, None, j + 1, P, weight_one, E0 + (j + 1) // 2 + 1)
                else:
                    pe_up(pe, u0 + 8, None, 0, P, lambda i, jj: weight1(0, jj), E0 + 2 * NSH + 1)
                pe_down(pe, u0, None, j, P)
            last = E1 // 4 - 1
            with pe.Fori(0, last) as i:
                for j in range(4):
                    if j < 3:
                        pe_up(pe, u0 + 8, i, j + 1, P, weight1, i * 2 + (E0 + 2 * NSH + (j + 1) // 2 + 1))
                    else:
                        i1 = i + 1
                        pe_up(pe, u0 + 8, i1, 0, P, weight1, i1 * 2 + (E0 + 2 * NSH + 1))
                    pe_down(pe, u0 + 8, i, j, P)
            for j in range(4):
                if j < 3:
                    pe_up(pe, u0 + 8 + 4 * last, None, j + 1, P, lambda _, jj: weight1(last, jj), 2 * last + (E0 + 2 * NSH + (j + 1) // 2 + 1))
                pe_down(pe, u0 + 8 + 4 * last, None, j, P)


        @block.vector
        def _(dve):
            v = nc.vector
            me = Steps(dve, s.dve_steps)

            def statistics(tiles):
                for t in tiles:
                    me.did(v.bn_stats(bn[:, t, :], x[:, t, :]))
                me.wait()
                for t in tiles:
                    me.did(v.bn_aggr(mv[:, t, :], bn[:, t, :]))

            def norm(k):
                me.wait()
                v.tensor_scalar(lnv[:], mv[:, :, 1], 1e-5, None, ALU.add).then_inc(s.ln_var, 1)
                dve.wait_ge(s.ln_std, k + 1)
                me.do(v.reciprocal(lnv[:], lnr[:]))
                for t in range(NT):
                    v.tensor_scalar(xn[:, t, :], x[:, t, :], mv[:, t, 0:1], lnv[:, t:t + 1],
                                    ALU.subtract, ALU.mult).then_inc(s.ln_done, 1)
                for j in range(2):
                    dve.wait_ge(s.ln_turned, 16 * k + 8 * (j + 1))
                    v.tensor_copy(xnT[:, 1, j * HALF:(j + 1) * HALF], ps[:, 2 * j + 1, :]).then_inc(s.xnT_dve, 1)

            def bc(ap, n):
                return ap.unsqueeze(2).to_broadcast([ap.shape[0], ap.shape[1], n])

            def read_projected(t, m, par):
                dve.wait_ge(s.misc_made, m + 1)
                r, dca = ROWS0[t], t == KT0 - 1
                pv = ps[0:r, 6 + par, :].rearrange("p (g h two d) -> p g h two d", g=NG, h=HG, two=2)
                bv = bkv0[0:r, int(dca), :].rearrange("p (g h two d) -> p g h two d", g=NG, h=HG, two=2)
                me.did(v.tensor_tensor(kx[0:r, :, t], pv[:, :, :, 0, :], bv[:, :, :, 0, :], ALU.add))
                v.tensor_tensor(vx[0:r, :, t], pv[:, :, :, 1, :], bv[:, :, :, 1, :], ALU.add).then_inc(s.misc_read, 1)

            me.did(v.memset(kx[:, :, KT0 - 2:KT0], 0.0))
            me.did(v.memset(vx[:, :, KT0 - 2:KT0], 0.0))
            me.did(v.memset(qg[:].bitcast(F32), 0.0))
            dve.wait_ge(s.w0_loaded, 16 * 5)
            centered = [(wkv0[:].rearrange("p (h two d) -> p h two d", two=2, d=D0)[:, :, 0, :], H0),
                        (wdca0[:].rearrange("p (h two d) -> p h two d", two=2, d=D0)[:, :, 0, :], H0),
                        (bkv0[:].rearrange("p n (h two d) -> p (n h) two d", two=2, d=D0)[:, :, 0, :], 2 * H0),
                        (wq0[:].rearrange("p k (h d) -> p (k h) d", d=D0), KD * H0),
                        (bq0[:].rearrange("p (h d) -> p h d", d=D0), H0)]
            starts = np.cumsum([0] + [n for _, n in centered])
            for (w, n), c in zip(centered, starts):
                me.did(v.tensor_reduce(s1[:, c:c + n], w, AX, ALU.add))
            me.wait()
            me.do(v.tensor_scalar(s1[:, 0:starts[-1]], s1[:, 0:starts[-1]], 1.0 / D0, None, ALU.mult))
            for j, ((w, n), c) in enumerate(zip(centered, starts)):
                ins = v.tensor_tensor(w, w, bc(s1[:, c:c + n], D0), ALU.subtract)
                if j < len(centered) - 1:
                    me.did(ins)
                else:
                    ins.then_inc(s.w0_centered, 1)
            dve.wait_ge(s.x_loaded, 16)
            for t in range(KT0):
                read_projected(t, t, t % 2)
                if t < NT:
                    me.did(v.bn_stats(bn[:, t, :], x[:, t, :]))
            me.wait()
            for t in range(NT):
                me.did(v.bn_aggr(mv[:, t, :], bn[:, t, :]))
            norm(0)

            def bounds():
                dve.wait_ge(s.bound_root, 1)
                pair = bsm[:, 12:18].rearrange("p (n two) -> p n two", two=2)
                root = bsm[:, 6:12].rearrange("p (n two) -> p n two", two=2)
                me.do(v.scalar_tensor_tensor(out=bsm[:, 18:21], in0=pair[:, :, 0], scalar=float(D0) ** 0.5, in1=root[:, :, 1],
                                             op0=ALU.mult, op1=ALU.add))
                me.do(v.tensor_scalar(bsm[:, 22:24], bsm[:, 19:21], bsm[:, 18:19], SCALE0, ALU.mult, ALU.mult))
                me.do(v.tensor_scalar(bsm[:, 22:24], bsm[:, 22:24], EXP_ROOM, 0.0, ALU.subtract, ALU.max))
                v.tensor_scalar(bsm[:, 24:26], bsm[:, 22:24], -1.0, None, ALU.mult).then_inc(s.bound0_ready, 1)
            def key_variance(k):
                for g in range(NG):
                    dve.wait_ge(s.k_squared, k * 4 + (g + 1))
                    v.tensor_reduce(s2[:, g * KT0 * HG:(g + 1) * KT0 * HG], ksq[:].rearrange("p (m d) -> p m d", d=D0),
                                    AX, ALU.add).then_inc(s.k_sq_read, 1)
                dve.wait_ge(s.k_sq_read, k * 4 + 4)
                v.tensor_scalar(s2[:], s2[:], 1.0 / D0, 1e-6, ALU.mult, ALU.add).then_inc(s.k_var, 1)

            def key_scale(k):
                dve.wait_ge(s.k_std, k + 1)
                me.do(v.reciprocal(s1[:], s2[:]))

            def normed_keys(g, free):
                if free is not None:
                    dve.wait_ge(s.hi_ready, free)
                v.tensor_tensor(kgroup(kc, g), kgroup(kx, g), bc(s1[:, g * KT0 * HG:(g + 1) * KT0 * HG], D0),
                                ALU.mult).then_inc(s.k_normed, 1)

            def stack_queries(tile, g):
                for t in range(TB):
                    me.did(v.tensor_copy(qst[:, t, :, 0::2, :].bitcast(F32R), parts(qhead(tile, t, g))))
                me.wait()
                me.did(v.tensor_tensor(qst[:, 0, :, 1::2, :].bitcast(F32R), parts(qhead(tile, 0, g)), qst[:, 0, :, 0::2, :], ALU.subtract))
                v.tensor_tensor(qst[:, 1, :, 1::2, :].bitcast(F32R), parts(qhead(tile, 1, g)), qst[:, 1, :, 0::2, :],
                                ALU.subtract).then_inc(s.qst_ready, 1)

            def qhead(tile, t, g):
                return qn[:, bass.ds(tile + t, 1), g * HG:(g + 1) * HG, :].rearrange("p t h d -> p (t h) d")

            def read_queries(slot, m, par, free):
                if free is not None:
                    dve.wait_ge(s.scores0, primed(free))
                dve.wait_ge(s.misc_made, m + 1)
                src = ps[:, 6 + par, :].rearrange("p (a n) -> p a n", a=2)
                me.did(v.tensor_copy(qg[0:64, slot, :, 0, :], src[0:64]))
                v.tensor_copy(qg[64:P, slot, :, 1, :], src[64:P]).then_inc(s.misc_read, 1)

            def keys_lo(g, ready):
                dve.wait_ge(s.hi_ready, ready)
                v.tensor_tensor(kst[:, :, 2:4, :].bitcast(F32R), parts(kgroup(kc, g)),
                                kst[:, :, 0:2, :], ALU.subtract).then_inc(s.kst_ready, 1)

            def read_keys(j, slot, m, par):
                dve.wait_ge(s.misc_made, m + 1)
                v.tensor_copy(kT0[:, slot, j * 512:(j + 1) * 512], ps[:, 6 + par, :]).then_inc(s.misc_read, 1)

            def read_sums(b, st, m, par):
                dve.wait_ge(s.pv0, primed(b * (NG * KT0) + (st + 1) * KT0))
                v.tensor_copy(oT0[:], ps[:, 4:6, 0:SQ]).then_inc(s.o0_read, 1)
                dve.wait_ge(s.misc_made, m + 1)
                o = ps[:, 6 + par, :].rearrange("p (n d) -> p n d", d=2 * D0)
                me.do(v.tensor_copy(rd0[:], o[:, :, D0]))
                me.do(v.reciprocal(rd0[:], rd0[:]))
                v.tensor_tensor(on0[:], o[:, :, 0:D0], bc(rd0[:], D0), ALU.mult).then_inc(s.misc_read, 1)
                dve.wait_ge(s.misc_read, primed(m + 1))
                me.do(v.tensor_tensor(on0[:, 0:2 * HG, :], on0[:, 0:2 * HG, :], on0[:, 2 * HG:4 * HG, :], ALU.add))
                v.tensor_copy(xn[:, bass.ds(b * TB, TB), st * HG * D0:(st + 1) * HG * D0],
                              on0[:, 0:2 * HG, :].rearrange("p (t h) d -> p t (h d)", t=TB)).then_inc(s.ctx_made, 1)

            def take_queries(j):
                dve.wait_ge(s.q0_made, j + 1)
                v.tensor_tensor(qn[:, 2 * j:2 * j + 2, :, :].rearrange("p t h d -> p t (h d)"),
                                ps[:, 4 + j, :].rearrange("p (t n) -> p t n", t=2),
                                bq0[:].unsqueeze(1).to_broadcast([P, 2, D]), ALU.add).then_inc(s.q0_read, 1)

            key_variance(0)
            key_scale(0)
            normed_keys(0, None)
            def query_scale(j, ts):
                m = slice(ts.start * H0, ts.stop * H0)
                dve.wait_ge(s.q0_squared, j + 1)
                me.do(v.tensor_reduce(rq0[:, 0, m], p0[:].rearrange("p a (m d) -> p (a m) d", d=D0)[:, m, :], AX, ALU.add))
                v.tensor_scalar(rq0[:, 0, m], rq0[:, 0, m], 1.0 / D0, 1e-6, ALU.mult, ALU.add).then_inc(s.q0_var, 1)
                if j == 0:
                    dve.wait_ge(s.small0_loaded, 16 * 5)
                    me.do(v.tensor_tensor(on0[:, 0:6, :], bnd[:], bnd[:], ALU.mult))
                    v.tensor_reduce(bsm[:, 0:6], on0[:, 0:6, :], AX, ALU.add).then_inc(s.bound_sq, 1)
                dve.wait_ge(s.q0_std, j + 1)
                v.reciprocal(rq0[:, 2, m], rq0[:, 1, m]).then_inc(s.q0_scale, 1)

            for j in range(4):
                take_queries(j)
            query_scale(0, slice(0, TB))
            me.do(v.tensor_reduce(bsm[:, 12:18], bnd[:], AX, ALU.max, apply_absolute_value=True))
            dve.wait_ge(s.q0_scale, 1)
            qf = qn[:, 0:TB].rearrange("p t h d -> p (t h) d")
            me.do(v.tensor_tensor(qf, qf, bc(rq0[:, 2, 0:TB * H0], D0), ALU.mult))
            q3 = qn[:, 0:TB].rearrange("p t h d -> p t (h d)")
            me.do(v.tensor_tensor(q3, q3, qnw[:, 0, :].unsqueeze(1).to_broadcast([P, TB, D]), ALU.mult))
            me.do(v.tensor_tensor(q3, q3, qnw[:, 1, :].unsqueeze(1).to_broadcast([P, TB, D]), ALU.add))
            stack_queries(0, 0)
            query_scale(1, slice(TB, NT))
            read_queries(0, KT0, KT0 % 2, None)
            keys_lo(0, 1)
            for j in range(7):
                read_keys(j, 0, KT0 + 1 + j, (KT0 + 1 + j) % 2)
            bounds()
            for g in range(1, NG):
                normed_keys(g, None)
            dve.wait_ge(s.qn_ready, 1)

            def dve_step(b, st, last):
                over = last and st == NG - 1
                nkv = KT0 if st == 0 and not last else 0
                par = MISC0 + MISC[st]
                slot = (st + 1) % 2
                if not over:
                    g1_ = (st + 1) % NG
                    stack_queries((b + 1) * TB if st == NG - 1 else b * TB, g1_)
                    read_queries(slot, misc(b, st, 0, last), par % 2, b * (NG * KT0) + st * KT0)
                    if nkv:
                        dve.wait_ge(s.vc_ready, b * 4 + 4)
                        for t in range(KT0):
                            read_projected(t, misc(b, st, 1 + t), (par + 1 + t) % 2)
                    if st == 2 and not last:
                        key_variance(b + 1)
                    keys_lo(g1_, b * 4 + (st + 2))
                    if st == 3 and not last:
                        for g in range(1, NG):
                            normed_keys(g, b * 4 + (g + 1))
                    for j in range(7):
                        k = 1 + nkv + j
                        read_keys(j, slot, misc(b, st, k, last), (par + k) % 2)
                        if j == 1 and st == 2 and not last:
                            key_scale(b + 1)
                            normed_keys(0, b * 4 + 1)
                k = 0 if over else 8 + nkv
                read_sums(b, st, misc(b, st, k, last), (par + k) % 2)

            with dve.Fori(0, B - 1) as b:
                me.enter(b, PER0)
                for st in range(NG):
                    dve_step(b, st, False)
                me.leave(B - 1)
            for st in range(NG):
                dve_step(B - 1, st, True)
            dve.wait_ge(s.y0_made, 1)
            ks = kc[:].rearrange("p g t h d -> p (g t h d)")[:, 0:NT * D]
            me.do(v.tensor_tensor(ks.rearrange("p (t n) -> p t n", t=NT), ps[:, 0:4, :].rearrange("p a (b n) -> p (a b) n", b=2),
                                  bo0[:].unsqueeze(1).to_broadcast([P, NT, D]), ALU.add))
            dve.wait_ge(s.tanh_made, 1)

            def update(src, gate, half, last):
                xs = x[:, half * 4:half * 4 + 4, :].rearrange("p t n -> p (t n)")
                ins = v.scalar_tensor_tensor(out=xs, in0=src, scalar=tg[:, gate:gate + 1], in1=xs, op0=ALU.mult, op1=ALU.add)
                if last:
                    ins.then_inc(s.x_updated, 1)
                    dve.wait_ge(s.x_updated, last)
                else:
                    me.do(ins)
                statistics(range(half * 4, half * 4 + 4))

            for half in range(2):
                update(ks[:, half * 4 * D:(half + 1) * 4 * D], 0, half, half)
            if stages < 2:
                return

            def shifted(E, k):
                dve.wait_ge(s.logits_made, k)
                lg = ps[:, 7, 0:NT * E].rearrange("p (t e) -> p t e", t=NT)
                me.do(v.tensor_copy(rr[:, :, 0:E], lg))
                me.do(v.tensor_reduce(rsm[:, 0, :], rr[:, :, 0:E], AX, ALU.max))
                v.tensor_tensor(rl[:, :, 0:E], rr[:, :, 0:E], bc(rsm[:, 0, :], E), ALU.subtract).then_inc(s.r_shifted, 1)
                dve.wait_ge(s.r_exp, k)

            def weights_parts(E, dsts, k):
                dve.wait_ge(s.w_turned, k)
                wt = ps[0:E, 4:6, :].rearrange("p a n -> p (a n)")
                me.do(v.tensor_copy(dsts[0], wt))
                me.do(v.tensor_tensor(rem1[0:E, :], wt, dsts[0], ALU.subtract))
                me.did(v.tensor_copy(dsts[1], rem1[0:E, :]))
                me.do(v.tensor_copy(mid0[0:E, :], rem1[0:E, :]))
                v.tensor_tensor(dsts[2], rem1[0:E, :], mid0[0:E, :], ALU.subtract).then_inc(s.wT_ready, 1)

            def ffn(u0, i, units, rows):
                for j in range(units):
                    dve.wait_ge(s.silu_made, at(u0, i, 4, j + 1))
                    dve.wait_ge(s.u_made, at(u0, i, 4, j + 1))
                    dve.wait_ge(s.h_made, primed(at(u0, i, 4, j)))
                    v.tensor_tensor(hh[0:rows, :], sg[0:rows, :], ps[0:rows, 5, :], ALU.mult).then_inc(s.h1_made, 1)
                    dve.wait_ge(s.h1_made, primed(at(u0, i, 4, j + 1)))
                    dve.wait_ge(s.w_made, at(u0, i, 4, j + 1))
                    dve.wait_ge(s.down_done, primed(at(u0 + (2 if u0 >= 2 * E0 else 1), i, 4, j - 1)))
                    v.tensor_tensor(hw[0:rows, j % 2, :], hh[0:rows, :], ps[0:rows, 6, :], ALU.mult).then_inc(s.h_made, 1)
                    dve.wait_ge(s.hs_hi, primed(at(u0, i, 4, j + 1)))
                    v.tensor_tensor(hs[0:rows, j % 2, 1, :], hw[0:rows, j % 2, :], hs[0:rows, j % 2, 0, :].bitcast(F32),
                                    ALU.subtract).then_inc(s.hs_lo, 1)

            norm(1)
            shifted(E0, 1)
            for t in range(NT):
                me.did(v.max(m8[:, t, :], re[:, t, 0:E0]))
            me.wait()
            for t in range(NT):
                me.did(v.match_replace(rr[:, t, 0:E0], m8[:, t, :], re[:, t, 0:E0], -1.0))
            me.wait()
            me.do(v.tensor_scalar(selb[:], rr[:, :, 0:E0], 0.0, None, ALU.is_lt))
            me.do(v.tensor_scalar(pre[:, 0, :], selb[:, 0, :], 0.0, None, ALU.mult))
            for t in range(1, NT):
                me.do(v.tensor_tensor(pre[:, t, :], pre[:, t - 1, :], selb[:, t - 1, :], ALU.add))
            v.tensor_tensor(rw[:, :, 0:E0], re[:, :, 0:E0], selb[:], ALU.mult).then_inc(s.sel_ready, 1)
            dve.wait_ge(s.sel_ready, 1)
            me.do(v.tensor_reduce(rsm[:, 1, :], rw[:, :, 0:E0], AX, ALU.add))
            me.do(v.reciprocal(rsm[:, 2, :], rsm[:, 1, :]))
            me.do(v.tensor_tensor(rw[:, :, 0:E0], rw[:, :, 0:E0], bc(rsm[:, 2, :], E0), ALU.mult))
            dve.wait_ge(s.pos_made, 1)
            wf = rw[:, :, 0:E0]
            v.scalar_tensor_tensor(out=wf, in0=ps[:, 7, 0:NT * E0].rearrange("p (t e) -> p t e", t=NT), scalar=float(CAP),
                                   in1=wf, op0=ALU.is_lt, op1=ALU.mult).then_inc(s.w_ready, 1)
            weights_parts(E0, [wT0[0:E0, :], wT0[E0:2 * E0, :], wT0[2 * E0:3 * E0, :]], 1)
            with dve.Fori(0, E0 // 2) as i:
                ffn(0, i, 4, I0)
            for half in range(2):
                dve.wait_ge(s.down_done, primed(2 * E0 + half))
                update(ps[:, 2 * half:2 * half + 2, :].rearrange("p a n -> p (a n)"), 2, half, 2 * half)
            if stages < 3:
                return

            norm(2)
            dve.wait_ge(s.w1_loaded, 16 * 7)
            me.do(v.scalar_tensor_tensor(out=g1[:, 2:3], in0=g1[:, 0:1], scalar=float(D1) ** -0.5, in1=g1[:, 1:2],
                                         op0=ALU.mult, op1=ALU.mult))
            me.do(v.tensor_tensor(g1r[:, 2, :], g1r[:, 0, :], g1r[:, 1, :], ALU.mult))
            me.do(v.tensor_reduce(g1[:, 3:4], g1r[:, 2, :], AX, ALU.max, apply_absolute_value=True))
            me.do(v.tensor_scalar(g1[:, 3:4], g1[:, 3:4], float(D1) ** 0.5, -EXP_ROOM, ALU.mult, ALU.add))
            v.tensor_scalar(g1[:, 3:4], g1[:, 3:4], 0.0, -1.0, ALU.max, ALU.mult).then_inc(s.bound1_ready, 1)
            for j in range(8):
                dve.wait_ge(s.m1_made, j + 1)
                v.tensor_copy(m1[:, 2 * j:2 * j + 2, :].rearrange("p h n -> p (h n)"), ps[:, 4 + j % 4, :]).then_inc(s.m1_read, 1)
            for b in range(B):
                if b == B // 2:
                    update(acc1[:, 0:4, :].rearrange("p t n -> p (t n)"), 1, 0, 0)
                if b == 0:
                    dve.wait_ge(s.sums_zeroed, 1)
                else:
                    dve.wait_ge(s.probs1, primed(KT * 8 * b))
                dve.wait_ge(s.ctxT_hi, b + 1)
                v.tensor_tensor(ctxT1[:, 1, 0:KV], stage[:, 0:KV], ctxT1[:, 0, 0:KV].bitcast(F32), ALU.subtract).then_inc(s.ctxT_lo, 1)
                for q, u, n in key_tiles(b):
                    tt = TB * b + q // 2
                    if q % 2 == 0 and u == 0:
                        dve.wait_ge(s.q1_read, 8 * (tt + 1))
                        me.do(v.tensor_reduce(rq1[:, 1, :], q1T[:], AX, ALU.add))
                        v.tensor_scalar(rq1[:, 0, :], rq1[:, 1, :], 1.0 / D1, 1e-5, ALU.mult, ALU.add).then_inc(s.q1_var, 1)
                    dve.wait_ge(s.k1_squared, n + 1)
                    r = ROWS1[u]
                    v.tensor_reduce(rk1[0:r, u, 4 * q:4 * q + 4], ksq1[0:r, n % KSQ, :].rearrange("p (h d) -> p h d", h=4),
                                    AX, ALU.add).then_inc(s.k1_reduced, 1)
                    if q % 2 == 0 and u == 3:
                        dve.wait_ge(s.q1_std, tt + 1)
                        v.reciprocal(rq1[:, 1, :], rq1[:, 0, :]).then_inc(s.q1_scale, 1)
                    if q % 2 == 0 and 9 <= u < 11:
                        for j in (2 * (u - 9), 2 * (u - 9) + 1):
                            dve.wait_ge(s.q1_turned, 4 * tt + j + 1)
                            v.tensor_scalar(q1T[:, 4 * j:4 * j + 4, :].rearrange("p h n -> p (h n)"), ps[:, 4 + j, :],
                                            g1[:, 2:3], None, ALU.mult).then_inc(s.q1T_ready, 1)
                    if q % 2 == 1 and 5 <= u < 9:
                        j = u - 5
                        dve.wait_ge(s.qq_hi, 4 * tt + j + 1)
                        v.tensor_tensor(qq_out(1, j, q // 2), ps[:, 4 + j, :].rearrange("p (h n) -> p h n", h=4),
                                        qq_out(0, j, q // 2).bitcast(F32), ALU.subtract).then_inc(s.qq_read, 1)
                dve.wait_ge(s.k1_reduced, 4 * KT * (b + 1))
                v.tensor_scalar(rk1[:], rk1[:], 1.0 / D1, 1e-5, ALU.mult, ALU.add).then_inc(s.k1_var, 1)
                dve.wait_ge(s.k1_std, b + 1)
                v.reciprocal(rk1[:], rk1[:]).then_inc(s.rk1_ready, 1)
                with dve.Fori(0, H1 // 2) as hp:
                    me.enter(hp, 3)
                    k0 = KT * 8 * b
                    for t in range(KT):
                        r = ROWS1[t]
                        pt = p1[:, BANK1[t], :, :].rearrange("p a n -> p (a n)")
                        dve.wait_ge(s.probs1, primed(at(k0, hp, KT, t + 1)))
                        if t == 0:
                            dve.wait_ge(s.den_made, primed(at(8 * b, hp, 1, 0)))
                            v.tensor_copy(dsum[:], pt).then_inc(s.summed, 1)
                        else:
                            dve.wait_ge(s.summed, primed(at(k0, hp, KT, t)))
                            v.tensor_tensor(dsum[0:r, :], dsum[0:r, :], pt[0:r, :], ALU.add).then_inc(s.summed, 1)
                    dve.wait_ge(s.pv1, primed(at(k0, hp, KT, KT)))
                    v.tensor_copy(oT1[:], ps[:, 4, :]).then_inc(s.o1_read, 1)
                    dve.wait_ge(s.den_made, primed(at(8 * b, hp, 1, 1)))
                    v.reciprocal(rd1[:], ps[:, 7, 0:4]).then_inc(s.den_read, 1)
                    dve.wait_ge(s.den_read, primed(at(8 * b, hp, 1, 1)))
                    dve.wait_ge(s.y1_made, at(8 * b, hp, 1, 1))
                    for j in range(4):
                        o = acc1[:, TB * b + j % 2, :]
                        if j == 2:
                            me.wait()
                        ins = v.scalar_tensor_tensor(out=o, in0=ps[:, 5 + j // 2, (j % 2) * D:(j % 2 + 1) * D], scalar=rd1[:, j:j + 1],
                                                     in1=o, op0=ALU.mult, op1=ALU.add)
                        if j < 3:
                            me.did(ins)
                        else:
                            ins.then_inc(s.y1_added, 1)
                    me.wait()
                    dve.wait_ge(s.y1_added, primed(at(8 * b, hp, 1, 1)))
                    me.leave(H1 // 2)
            update(acc1[:, 4:8, :].rearrange("p t n -> p (t n)"), 1, 1, 3)
            if stages < 4:
                return

            norm(3)
            dve.wait_ge(s.xnT_act, 8)
            dve.wait_ge(s.xnT_dve, 8)
            dve.wait_ge(s.router_loaded, 16 * 16)
            me.do(v.tensor_reduce(xm[:], xnT[:].rearrange("p k (b n) -> p (k b) n", b=B), AX, ALU.add))
            v.tensor_scalar(xm[:], xm[:], 1.0 / SQ, None, ALU.mult).then_inc(s.xm_ready, 1)
            dve.wait_ge(s.tl_made, 1)
            me.do(v.tensor_tensor(td[:, 1, :], ps[0:B, 6, 0:ND], teb2[:], ALU.add))
            me.do(v.tensor_reduce(td[:, 2, 0:1], td[:, 1, :], AX, ALU.max))
            v.tensor_scalar(td[:, 0, :], td[:, 1, :], td[:, 2, 0:1], None, ALU.subtract).then_inc(s.tl_shifted, 1)
            dve.wait_ge(s.tl_exp, 1)
            me.do(v.tensor_reduce(td[:, 2, 0:1], td[:, 1, :], AX, ALU.add))
            me.do(v.reciprocal(td[:, 2, 1:2], td[:, 2, 0:1]))
            v.tensor_scalar(td[:, 3, :], td[:, 1, :], td[:, 2, 1:2], 0.5, ALU.mult, ALU.mult).then_inc(s.td_ready, 1)
            dve.wait_ge(s.td_turned, 1)
            v.tensor_copy(tdT[:], bc(ps[0:ND, 6, 0:B], P)).then_inc(s.tdT_ready, 1)
            shifted(E1, 2)
            me.did(v.tensor_reduce(rsm[:, 3, :], re[:], AX, ALU.add))
            me.did(v.tensor_tensor(rl[:, :, 0:E1], rr[:, :, 0:E1], rb1[:].unsqueeze(1).to_broadcast([P, NT, E1]), ALU.add))
            me.do(v.memset(rl[:, :, E1:E1 + TOPS - TOP1], -FAR))
            for t in range(NT):
                me.did(v.max(m8[:, t, :], rl[:, t, 0:E1]))
            me.wait()
            me.do(v.memset(m8[:, :, TOP1:TOPS], -FAR))
            for t in range(NT):
                me.did(v.match_replace(rr[:, t, :], m8[:, t, :], rl[:, t, :], FAR))
            me.wait()
            me.do(v.tensor_scalar(rr[:, :, 0:E1], rr[:, :, 0:E1], 0.5 * FAR, None, ALU.is_gt))
            me.do(v.tensor_tensor(rw[:], re[:], rr[:, :, 0:E1], ALU.mult))
            me.do(v.tensor_reduce(rsm[:, 1, :], rw[:], AX, ALU.add))
            me.do(v.scalar_tensor_tensor(out=rsm[:, 2, :], in0=rsm[:, 3, :], scalar=1e-8, in1=rsm[:, 1, :],
                                         op0=ALU.mult, op1=ALU.add))
            me.do(v.reciprocal(rsm[:, 4, :], rsm[:, 2, :]))
            v.tensor_tensor(rw[:], rw[:], bc(rsm[:, 4, :], E1), ALU.mult).then_inc(s.w_ready, 1)
            dve.wait_ge(s.consts_made, 6)
            weights_parts(E1, [wT1a[0:E1, :], wT1a[E1:2 * E1, :], wT1b[0:E1, :]], 2)
            u0 = 2 * E0
            ffn(u0, None, 8, P)
            with dve.Fori(0, E1 // 4) as i:
                ffn(u0 + 8, i, 4, P)
            for half in range(2):
                dve.wait_ge(s.down_done, primed(2 + 2 * E0 + 8 + E1 - 1 + half))
                xs = x[:, half * 4:half * 4 + 4, :].rearrange("p t n -> p (t n)")
                v.scalar_tensor_tensor(out=xs, in0=ps[:, 2 * half:2 * half + 2, :].rearrange("p a n -> p (a n)"), scalar=tg[:, 3:4],
                                       in1=xs, op0=ALU.mult, op1=ALU.add).then_inc(s.x_updated, 1)


def _layout(i):
    import numpy as np
    def rows(v, n=128):
        return np.ascontiguousarray(np.broadcast_to(v, (n,) + v.shape))
    g = lambda n: i["L0_xattn_" + n]
    h = lambda n: i["L1_xattn_" + n]
    f = lambda n: i["L1_ffn_" + n]
    dca = lambda w: w.reshape(-1, 2, 16, 16).transpose(0, 2, 1, 3).reshape(-1, 512)
    tile = lambda w, n: np.tile(w, n)
    main, extra = 13 * 4, 4
    knwb = np.stack([np.concatenate([tile(g("kn_w"), main), tile(g("kn_dca_w"), extra)]),
                     np.concatenate([tile(g("kn_b"), main), tile(g("kn_dca_b"), extra)])])
    new = {
        "gates": rows(np.concatenate([i["g_xattn"], i["g_ffn"]])),
        "Wkv0": np.concatenate([g("Wk"), g("Wv")], axis=1),
        "Wdca0": dca(g("Wkv_dca")),
        "bq0": rows(g("bq")),
        "bkv0": rows(np.stack([np.concatenate([g("bk"), g("bv")]), dca(g("bkv_dca")[None])[0]])),
        "bo0": rows(g("bo")),
        "qnw": rows(np.stack([tile(g("qn_w"), 16), tile(g("qn_b"), 16)])),
        "knwb": rows(knwb),
        "bnd": rows(np.stack([g(n) for n in ("qn_w", "qn_b", "kn_w", "kn_b", "kn_dca_w", "kn_dca_b")])),
        "ctxT": i["ctx_1024"].transpose(0, 2, 1),
        "WrT": f("Wr").T, "rb1": rows(f("router_bias")), "affT": f("affinity").T,
        "te_W1T": f("te_W1").T, "teb1": f("te_b1")[:, None], "te_W2T": f("te_W2").T, "teb2": rows(f("te_b2"), 4),
        "WkT1": h("Wk").reshape(128, 16, 128).transpose(2, 1, 0),
        "WvT1": h("Wv").reshape(128, 16, 128).transpose(2, 1, 0),
        "g1": np.stack([h("gq"), h("gk")], axis=1),
        "g1r": rows(np.stack([h("gq"), h("gk")])),
    }
    for n in ("x", "ctx_1024", "L0_xattn_Wq", "L0_xattn_Wo", "L0_ffn_gate_w", "L0_ffn_w_gate", "L0_ffn_w_up", "L0_ffn_w_down",
              "L1_xattn_Wq", "L1_xattn_Wk", "L1_xattn_Wo", "L1_ffn_Wg", "L1_ffn_Wu", "L1_ffn_Wd", "L1_ffn_Sg", "L1_ffn_Su", "L1_ffn_Sd"):
        new[n] = i[n]
    return {k: np.ascontiguousarray(v) for k, v in new.items()}


def kernel(**inputs):
    import numpy as _np
    import concourse.bacc as _bacc
    from concourse import mybir as _mybir
    from concourse.bass_utils import run_bass_kernel_spmd as _run

    nc = _bacc.Bacc("TRN2", target_bir_lowering=False, num_devices=1)
    laid = _layout({k: _np.asarray(v) for k, v in inputs.items()})
    arrays, args = {}, {}
    for name, v in laid.items():
        arrays[f"in_{name}_dram"] = v
        args[name] = nc.dram_tensor(f"in_{name}_dram", v.shape, _mybir.dt.from_np(v.dtype), kind="ExternalInput").ap()
    out = nc.dram_tensor("out_0_dram", (4, 256, 256), _mybir.dt.float32, kind="ExternalOutput").ap()
    program(nc, args, out)
    r = _run(nc, [arrays], core_ids=[0])
    return r.results[0]["out_0_dram"]
```
